# Optimizing a Trainium2 kernel written in Bass

```python
import numpy as np
import jax
import jax.numpy as jnp

def _softmax(x, axis=-1):
    return jax.nn.softmax(x, axis=axis)

def _gelu(x):
    return jax.nn.gelu(x, approximate=True)

def _silu(x):
    return jax.nn.silu(x)

def _sigmoid(x):
    return jax.nn.sigmoid(x)

def _layernorm(x, axis=-1, eps=1e-05):
    m = jnp.mean(x, axis=axis, keepdims=True)
    v = jnp.var(x, axis=axis, keepdims=True)
    return (x - m) / jnp.sqrt(v + eps)

def _scatter_add(tgt, idx, src, axis=0):
    return tgt.at[idx].add(src)

def _segment_sum(src, seg, n):
    return jax.ops.segment_sum(src, seg, n)
kernel_name = 'mk_macaron_d1_jaxref_r4_b64c45'

def setup_inputs(seed: int=0):
    np.random.seed(seed)
    _w = jnp.asarray

    def _L0_attn_setup():
        import jax, jax.numpy as jnp
        import numpy as np
        EMBED_DIM = 256
        NUM_HEADS = 16
        CHUNK_SIZE = 128
        BATCH = 4
        SEQ_LEN = 2048

        def _chunked_attention(x, wq, bq, wk, bk, wv, bv, wo, bo):
            B, S, E = x.shape
            H, T = (NUM_HEADS, CHUNK_SIZE)
            D = E // H
            C = S // T
            scale = 1.0 / float(np.sqrt(D))

            def proj(w, b):
                y = jnp.einsum('bse,fe->bsf', x, w) + b
                return y.reshape(B, C, T, H, D).transpose(0, 3, 1, 2, 4)
            q = proj(wq, bq)
            k = proj(wk, bk)
            v = proj(wv, bv)
            s_intra = jnp.einsum('bhctd,bhcsd->bhcts', q, k) * scale
            a_intra = jax.nn.softmax(s_intra, axis=-1)
            intra = jnp.einsum('bhcts,bhcsd->bhctd', a_intra, v)
            k_means = k.mean(axis=3)
            v_means = v.mean(axis=3)
            s_inter = jnp.einsum('bhctd,bhjd->bhctj', q, k_means) * scale
            chunk_pos = jnp.arange(C)
            causal = chunk_pos[:, None] >= chunk_pos[None, :]
            s_inter = jnp.where(causal[None, None, :, None, :], s_inter, -jnp.inf)
            a_inter = jax.nn.softmax(s_inter, axis=-1)
            inter = jnp.einsum('bhctj,bhjd->bhctd', a_inter, v_means)
            out = intra + inter
            out = out.transpose(0, 2, 3, 1, 4).reshape(B, S, E)
            return jnp.einsum('bse,fe->bsf', out, wo) + bo
        key = jax.random.key(seed)
        ks = jax.random.split(key, 9)
        E = EMBED_DIM
        s = 1.0 / np.sqrt(E)
        inp = {'hidden_states': jax.random.normal(ks[0], (BATCH, SEQ_LEN, E), dtype=jnp.float32), 'wq': jax.random.normal(ks[1], (E, E), dtype=jnp.float32) * s, 'bq': jax.random.normal(ks[2], (E,), dtype=jnp.float32) * s, 'wk': jax.random.normal(ks[3], (E, E), dtype=jnp.float32) * s, 'bk': jax.random.normal(ks[4], (E,), dtype=jnp.float32) * s, 'wv': jax.random.normal(ks[5], (E, E), dtype=jnp.float32) * s, 'bv': jax.random.normal(ks[6], (E,), dtype=jnp.float32) * s, 'wo': jax.random.normal(ks[7], (E, E), dtype=jnp.float32) * s, 'bo': jax.random.normal(ks[8], (E,), dtype=jnp.float32) * s}
        return inp
    _L0_attn_in = _L0_attn_setup()

    def _L0_ffn_setup():
        import jax, jax.numpy as jnp
        import numpy as np
        E = 16
        F_C = 2.0
        D = 256
        I = 4 * D
        IS = 2 * D
        B, S = (4, 256)
        key = jax.random.key(seed)
        ks = jax.random.split(key, 8)
        w = 0.02
        return {'hidden_states': jax.random.normal(ks[0], (B, S, D), dtype=jnp.float32), 'gate_w': jax.random.normal(ks[1], (E, D), dtype=jnp.float32) * w, 'Wg': jax.random.normal(ks[2], (E, I, D), dtype=jnp.float32) * w, 'Wu': jax.random.normal(ks[3], (E, I, D), dtype=jnp.float32) * w, 'Wd': jax.random.normal(ks[4], (E, D, I), dtype=jnp.float32) * w, 'Sg': jax.random.normal(ks[5], (IS, D), dtype=jnp.float32) * w, 'Su': jax.random.normal(ks[6], (IS, D), dtype=jnp.float32) * w, 'Sd': jax.random.normal(ks[7], (D, IS), dtype=jnp.float32) * w}
    _L0_ffn_in = _L0_ffn_setup()
    _d = {'L0_attn_hidden_states': _L0_attn_in['hidden_states'], 'L0_attn_wq': _L0_attn_in['wq'], 'L0_attn_bq': _L0_attn_in['bq'], 'L0_attn_wk': _L0_attn_in['wk'], 'L0_attn_bk': _L0_attn_in['bk'], 'L0_attn_wv': _L0_attn_in['wv'], 'L0_attn_bv': _L0_attn_in['bv'], 'L0_attn_wo': _L0_attn_in['wo'], 'L0_attn_bo': _L0_attn_in['bo'], 'L0_ffn_gate_w': _L0_ffn_in['gate_w'], 'L0_ffn_Wg': _L0_ffn_in['Wg'], 'L0_ffn_Wu': _L0_ffn_in['Wu'], 'L0_ffn_Wd': _L0_ffn_in['Wd'], 'L0_ffn_Sg': _L0_ffn_in['Sg'], 'L0_ffn_Su': _L0_ffn_in['Su'], 'L0_ffn_Sd': _L0_ffn_in['Sd']}
    _x0 = _d['L0_attn_hidden_states']
    _d['L0_attn_hidden_states'] = jax.random.normal(jax.random.fold_in(jax.random.key(seed), 1), (1, 4096, 256), dtype=_x0.dtype)
    del _x0
    return _d

def reference(L0_attn_hidden_states, L0_attn_wq, L0_attn_bq, L0_attn_wk, L0_attn_bk, L0_attn_wv, L0_attn_bv, L0_attn_wo, L0_attn_bo, L0_ffn_gate_w, L0_ffn_Wg, L0_ffn_Wu, L0_ffn_Wd, L0_ffn_Sg, L0_ffn_Su, L0_ffn_Sd):

    def _L0_attn_ref(hidden_states, wq, bq, wk, bk, wv, bv, wo, bo):
        import jax, jax.numpy as jnp
        import numpy as np
        EMBED_DIM = 256
        NUM_HEADS = 16
        CHUNK_SIZE = 128
        BATCH = 4
        SEQ_LEN = 2048

        def _chunked_attention(x, wq, bq, wk, bk, wv, bv, wo, bo):
            B, S, E = x.shape
            H, T = (NUM_HEADS, CHUNK_SIZE)
            D = E // H
            C = S // T
            scale = 1.0 / float(np.sqrt(D))

            def proj(w, b):
                y = jnp.einsum('bse,fe->bsf', x, w) + b
                return y.reshape(B, C, T, H, D).transpose(0, 3, 1, 2, 4)
            q = proj(wq, bq)
            k = proj(wk, bk)
            v = proj(wv, bv)
            s_intra = jnp.einsum('bhctd,bhcsd->bhcts', q, k) * scale
            a_intra = jax.nn.softmax(s_intra, axis=-1)
            intra = jnp.einsum('bhcts,bhcsd->bhctd', a_intra, v)
            k_means = k.mean(axis=3)
            v_means = v.mean(axis=3)
            s_inter = jnp.einsum('bhctd,bhjd->bhctj', q, k_means) * scale
            chunk_pos = jnp.arange(C)
            causal = chunk_pos[:, None] >= chunk_pos[None, :]
            s_inter = jnp.where(causal[None, None, :, None, :], s_inter, -jnp.inf)
            a_inter = jax.nn.softmax(s_inter, axis=-1)
            inter = jnp.einsum('bhctj,bhjd->bhctd', a_inter, v_means)
            out = intra + inter
            out = out.transpose(0, 2, 3, 1, 4).reshape(B, S, E)
            return jnp.einsum('bse,fe->bsf', out, wo) + bo
        return _chunked_attention(hidden_states, wq, bq, wk, bk, wv, bv, wo, bo)

    def _L0_ffn_ref(hidden_states, gate_w, Wg, Wu, Wd, Sg, Su, Sd):
        import jax, jax.numpy as jnp
        import numpy as np
        E = 16
        F_C = 2.0
        D = 256
        I = 4 * D
        IS = 2 * D
        B, S = (4, 256)
        b, s, d = hidden_states.shape
        T = b * s
        C = int(T * F_C / E)
        flat_x = hidden_states.reshape(T, d)
        logits = flat_x @ gate_w.T
        scores = jax.nn.softmax(logits, axis=-1).T
        topk_weight, topk_idx = jax.lax.top_k(scores, C)
        xg = flat_x[topk_idx]
        g = jnp.einsum('ecd,eid->eci', xg, Wg)
        u = jnp.einsum('ecd,eid->eci', xg, Wu)
        h = jax.nn.gelu(g, approximate=False) * u
        eo = jnp.einsum('eci,edi->ecd', h, Wd)
        eo = eo * topk_weight[..., None]
        flat_out = jnp.zeros_like(flat_x).at[topk_idx.reshape(-1)].add(eo.reshape(-1, d))
        out = flat_out.reshape(b, s, d)
        sg = hidden_states @ Sg.T
        su = hidden_states @ Su.T
        shared = jax.nn.gelu(sg, approximate=False) * su @ Sd.T
        return out + shared
    x = L0_attn_hidden_states
    x = x + 0.5 * _L0_ffn_ref(_layernorm(x, axis=-1), L0_ffn_gate_w, L0_ffn_Wg, L0_ffn_Wu, L0_ffn_Wd, L0_ffn_Sg, L0_ffn_Su, L0_ffn_Sd)
    x = x + _L0_attn_ref(_layernorm(x, axis=-1), L0_attn_wq, L0_attn_bq, L0_attn_wk, L0_attn_bk, L0_attn_wv, L0_attn_bv, L0_attn_wo, L0_attn_bo)
    x = x + 0.5 * _L0_ffn_ref(_layernorm(x, axis=-1), L0_ffn_gate_w, L0_ffn_Wg, L0_ffn_Wu, L0_ffn_Wd, L0_ffn_Sg, L0_ffn_Su, L0_ffn_Sd)
    return x

_drawn_inputs = setup_inputs


def setup_inputs(seed=0):
    import zlib

    import numpy as np

    out = dict(_drawn_inputs(seed))
    spreads = {}
    factors = {'L0_attn_bq': 16.098,
     'L0_attn_bk': 200.0,
     'L0_ffn_gate_w': 8.0,
     'L0_ffn_Wg': 8.0,
     'L0_ffn_Wu': 8.0,
     'L0_ffn_Wd': 8.0,
     'L0_attn_bo': 3.259,
     'L0_ffn_Sg': 5.374,
     'L0_ffn_Su': 5.128,
     'L0_ffn_Sd': 5.136}
    for name, (base, spread) in spreads.items():
        noise = np.random.default_rng([zlib.crc32(name.encode()), seed]).standard_normal(out[name].shape)
        drawn = base * np.exp(spread * noise) if base else spread * noise
        out[name] = jnp.asarray(drawn.astype(out[name].dtype))
    for name, factor in factors.items():
        out[name] = (out[name] * factor).astype(out[name].dtype)
    return out
```

```python
from contextlib import ExitStack, contextmanager

import concourse.bass as bass
from concourse import mybir

F32 = mybir.dt.float32
F32R = mybir.dt.float32r
BF16 = mybir.dt.bfloat16
U32 = mybir.dt.uint32
ALU = mybir.AluOpType
ACT = mybir.ActivationFunctionType
AX_X = mybir.AxisListType.X

P = 128
TOK = 4096
D = 256
DC = D // P
NT = TOK // P
BLK = 512
TPB = BLK // P
NB = TOK // BLK
E = 16
CAP = TOK * 2 // E
IE = 1024
UE = IE // P
US = 512 // P
UW = 3 * D
ROW = D + E
EPS = 1e-5
BITS = 30
ROUNDS = NB * US
AHEAD = 6
RAW = 4

H = 16
HD = D // H
GH = P // HD
NC = NT
SCALE = 1.0 / HD ** 0.5
NEG = -1e30


def at_least(engine, sem, value):
    if isinstance(value, int) and value <= 0:
        return
    engine.wait_ge(sem, value)


def first(i):
    return isinstance(i, int) and i == 0


def loop(engine, n, body):
    body(0)
    if n > 1:
        with engine.Fori(1, n) as i:
            body(i)


def loop_last(engine, n, body):
    body(0, False)
    with engine.Fori(1, n - 1) as i:
        body(i, False)
    body(n - 1, True)


class Chain:

    def __init__(self, engine, sem, base=0):
        self.engine, self.sem, self.base, self.n = engine, sem, base, 0

    def step(self, instruction):
        self.n += 1
        instruction.then_inc(self.sem, 1)
        self.engine.wait_ge(self.sem, self.base + self.n)


def split3(pe, out, lhs, rhs, first, last):
    pairs = [(0, 0), (0, 1), (1, 0)]
    for n, (a, b) in enumerate(pairs):
        ins = pe.matmul(out, lhs[a], rhs[b], start=first and n == 0, stop=last and n == 2,
                        skip_group_check=True)
    return ins


class Memory:

    def __init__(self, nc, ctx, prefix):
        self.nc, self.ctx, self.prefix, self.sems = nc, ctx, prefix, []

    def sb(self, name, shape, dt=F32):
        return self.ctx.enter_context(self.nc.sbuf_tensor(self.prefix + name, shape, dt))

    def ps(self, name, shape=(P, BLK), dt=F32):
        return self.ctx.enter_context(self.nc.psum_tensor(self.prefix + name, list(shape), dt))

    def sem(self, name):
        self.sems.append(self.ctx.enter_context(self.nc.semaphore(self.prefix + name)))
        return self.sems[-1]

    @contextmanager
    def run(self):
        with self.nc.Block() as block:
            yield block
        with self.nc.Block() as block:
            @block.sync
            def _(sp):
                for s in self.sems:
                    sp.sem_clear(s)


class Norm:

    STEPS = 7

    def __init__(self, m):
        self.stats = [m.sb(f"stats{s}", [P, TPB, 6]) for s in range(2)]
        self.mv = [m.sb(f"meanvar{s}", [P, TPB, 2]) for s in range(2)]
        self.ve = [m.sb(f"vareps{s}", [P, TPB]) for s in range(2)]
        self.sd = [m.sb(f"std{s}", [P, TPB]) for s in range(2)]
        self.ri = [m.sb(f"rstd{s}", [P, 3, TPB]) for s in range(2)]
        self.chain, self.note = m.sem("norm_chain"), m.sem("norm_note")
        self.var_ready, self.std_ready, self.xn_ready = m.sem("var_ready"), m.sem("std_ready"), m.sem("xn_ready")

    def statistics(self, dve, b, s, tiles):
        for t in range(TPB):
            last = dve.bn_stats(self.stats[s][:, t, :], tiles(t))
        Chain(dve, self.chain, b * self.STEPS).step(last)
        dve.sem_inc(self.note, 1)
        for t in range(TPB):
            last = dve.bn_aggr(self.mv[s][:, t, :], self.stats[s][:, t, :])
        Chain(dve, self.chain, b * self.STEPS + 1).step(last)
        dve.tensor_scalar(self.ve[s][:], self.mv[s][:, :, 1], EPS, None, ALU.add).then_inc(self.var_ready, 1)

    def root(self, act, b, s):
        act.wait_ge(self.var_ready, b + 1)
        act.activation(self.sd[s][:], self.ve[s][:], ACT.Sqrt).then_inc(self.std_ready, 1)

    def scale(self, dve, b, s):
        dve.wait_ge(self.std_ready, b + 1)
        ch = Chain(dve, self.chain, b * self.STEPS + 2)
        r0, r1, r2 = (self.ri[s][:, k, :] for k in range(3))
        ch.step(dve.reciprocal(r0, self.sd[s][:]))
        ch.step(dve.tensor_tensor(r1, r0, r0, ALU.mult))
        ch.step(dve.tensor_tensor(r2, r1, self.ve[s][:], ALU.mult))
        ch.step(dve.tensor_scalar(r1, r2, -0.5, 1.5, ALU.mult, ALU.add))
        ch.step(dve.tensor_tensor(r2, r0, r1, ALU.mult))

    def apply(self, dve, b, s, out, tiles):
        for t in range(TPB):
            dve.tensor_scalar(out[:, t, :], tiles(t), self.mv[s][:, t, 0:1], self.ri[s][:, 2, t:t + 1],
                              ALU.subtract, ALU.mult).then_inc(self.xn_ready, 1)


def ffn_prepare(nc, name, con, X, x_in, gate, table, XTH, XTL, LG):
    with ExitStack() as ctx:
        m = Memory(nc, ctx, name)
        nm = Norm(m)
        XN = [m.sb(f"xn{s}", [P, TPB, D]) for s in range(2)]
        GR = m.sb("gate_raw", [P, DC, E])
        G = [m.sb(f"gate_part{s}", [P, DC, P], F32R) for s in range(2)]
        LS = [m.sb(f"logits_t{s}", [P, BLK]) for s in range(2)]
        TP = [[m.ps(f"tp{s}{c}") for c in range(DC)] for s in range(2)]
        LP = [m.ps(f"lp{s}") for s in range(2)]
        TL = [m.ps(f"tl{s}") for s in range(2)]
        x_loaded = [m.sem(f"x_loaded{s}") for s in range(2)]
        gate_loaded, gate_split = m.sem("gate_loaded"), m.sem("gate_split")
        xn_ready = nm.xn_ready
        xn_stored = [m.sem(f"xn_stored{s}") for s in range(2)]
        xt_ready, hi_ready, lo_ready = m.sem("xt_ready"), m.sem("hi_ready"), m.sem("lo_ready")
        lt_ready, ls_ready, tl_ready, lg_ready = (m.sem("lt_ready"), m.sem("ls_ready"),
                                                  m.sem("tl_ready"), m.sem("lg_ready"))
        block = ctx.enter_context(m.run())
        tab = table.rearrange("(t p) c -> p t c", p=P)
        half = NB // 2

        @block.sync
        def _(sp):
            sp.dma_start(GR[:], gate).then_inc(gate_loaded, 16)

            def body(i):
                for s in range(2):
                    b = 2 * i + s
                    at_least(sp, x_loaded[s], 16 * i)
                    sp.dma_start(X[:, bass.ds(b * TPB, TPB), :],
                                 x_in.rearrange("(t p) c -> p t c", p=P)[:, bass.ds(b * TPB, TPB), :]
                                 ).then_inc(x_loaded[s], 16)

            def store(i):
                for s in range(2):
                    b = 2 * i + s
                    sp.wait_ge(xn_ready, TPB * (b + 1))
                    sp.dma_start(tab[:, bass.ds(b * TPB, TPB), 0:D], XN[s][:]).then_inc(xn_stored[s], 16)

            loop(sp, half, body)
            loop(sp, half, store)
            for s in range(2):
                sp.wait_ge(xn_stored[s], 16 * half)

        @block.vector
        def _(dve):
            gc = Chain(dve, gate_split)
            gc.step(dve.memset(G[0][:].bitcast(F32), 0.0))
            gc.step(dve.memset(G[1][:].bitcast(F32), 0.0))
            dve.wait_ge(gate_loaded, 16)
            gc.step(dve.tensor_copy(G[0][:, :, 0:E], GR[:]))
            gc.step(dve.tensor_tensor(G[1][:, :, 0:E], GR[:], G[0][:, :, 0:E].bitcast(F32), ALU.subtract))
            def stats(i, s):
                b = 2 * i + s
                dve.wait_ge(x_loaded[s], 16 * (i + 1))
                nm.statistics(dve, b, s, lambda t: X[:, b * TPB + t, :])

            def norm(i, s):
                b = 2 * i + s
                nm.scale(dve, b, s)
                at_least(dve, xn_stored[s], 16 * i)
                at_least(dve, xt_ready, b - 1)
                nm.apply(dve, b, s, XN[s], lambda t: X[:, b * TPB + t, :])

            def low(i, s):
                b = 2 * i + s
                dve.wait_ge(hi_ready, DC * (b + 1))
                for c in range(DC):
                    dve.tensor_tensor(XTL[:, c, bass.ds(b * BLK, BLK)], TP[s][c][:],
                                      XTH[:, c, bass.ds(b * BLK, BLK)].bitcast(F32),
                                      ALU.subtract).then_inc(lo_ready, 1)

            def logits(i, s):
                b = 2 * i + s
                dve.wait_ge(tl_ready, b + 1)
                dve.tensor_copy(LG[:, bass.ds(b * TPB, TPB), :],
                                TL[s][:].rearrange("p (t e) -> p t e", e=P)[:, :, 0:E]).then_inc(lg_ready, 1)

            def body(i, last):
                for s in range(2):
                    if not (last and s):
                        stats(*((i, 1) if s == 0 else (i + 1, 0)))
                    low(i, s)
                    if not (last and s):
                        norm(*((i, 1) if s == 0 else (i + 1, 0)))
                    logits(i, s)

            stats(0, 0)
            norm(0, 0)
            loop_last(dve, half, body)

        @block.scalar
        def _(act):
            def body(i, last):
                for s in range(2):
                    b = 2 * i + s
                    if not (last and s):
                        nm.root(act, b + 1, 1 - s)
                    act.wait_ge(xt_ready, b + 1)
                    for c in range(DC):
                        nc.scalar.activation(XTH[:, c, bass.ds(b * BLK, BLK)], TP[s][c][:],
                                             ACT.Copy).then_inc(hi_ready, 1)
                    act.wait_ge(lt_ready, b + 1)
                    at_least(act, tl_ready, b - 1)
                    nc.scalar.activation(LS[s][:], LP[s][:], ACT.Copy).then_inc(ls_ready, 1)

            nm.root(act, 0, 0)
            loop_last(act, half, body)

        @block.tensor
        def _(pe):
            pe.wait_ge(gate_split, 4)

            def body(i):
                for s in range(2):
                    b = 2 * i + s
                    pe.wait_ge(xn_ready, TPB * (b + 1))
                    at_least(pe, lo_ready, DC * (b - 1))
                    for c in range(DC):
                        for t in range(TPB):
                            last = pe.transpose(TP[s][c][:, t * P:(t + 1) * P], XN[s][:, t, c * P:(c + 1) * P],
                                                con["ident"])
                    last.then_inc(xt_ready, 1)
                    pe.wait_ge(lo_ready, DC * (b + 1))
                    at_least(pe, ls_ready, b - 1)
                    for c in range(DC):
                        last = split3(pe, LP[s][:], [G[k][:, c, :] for k in range(2)],
                                      [x[:, c, bass.ds(b * BLK, BLK)] for x in (XTH, XTL)],
                                      c == 0, c == DC - 1)
                    last.then_inc(lt_ready, 1)
                    pe.wait_ge(ls_ready, b + 1)
                    at_least(pe, lg_ready, b - 1)
                    for t in range(TPB):
                        last = pe.transpose(TL[s][:, t * P:(t + 1) * P], LS[s][:, t * P:(t + 1) * P],
                                            con["ident"])
                    last.then_inc(tl_ready, 1)

            loop(pe, half, body)


def ffn_shared_and_route(nc, name, con, X, acc, shared_w, table, XTH, XTL, LG, SLOT, CODE):
    with ExitStack() as ctx:
        m = Memory(nc, ctx, name)
        WR = m.sb("w_raw", [P, US, UW])
        W = [m.sb(f"w_part{k}", [P, US, UW], F32R) for k in range(2)]
        GEL = [m.sb(f"gelu{s}", [P, BLK]) for s in range(2)]
        HF = [m.sb(f"h{s}", [P, BLK]) for s in range(2)]
        HP = [[m.sb(f"h_part{k}{s}", [P, BLK], F32R) for k in range(2)] for s in range(2)]
        SC = m.sb("scores", [P, E, NT])
        EX = m.sb("exp", [P, NT, E])
        MX = m.sb("max", [P, NT])
        PR = m.sb("probs", [P, NT, E])
        THR, CAND, HIT, BIT, NGT = (m.sb(n, [P, E]) for n in ("thr", "cand", "hit", "bit", "need"))
        CNT = m.sb("count", [P, E])
        MASK = m.sb("mask", [P, E, NT], BF16)
        EQ = m.sb("equal", [P, E, NT], BF16)
        ABOVE = m.sb("above", [P, E, NT], BF16)
        INC, RANK, COL, FIT = (m.sb(n, [P, E, NT]) for n in ("incl", "rank", "column", "fit"))
        GP = [m.ps(f"g{s}") for s in range(2)]
        UP = [m.ps(f"u{s}") for s in range(2)]
        OP = [m.ps(f"o{s}") for s in range(2)]
        CP = m.ps("count_ps")
        WP = m.ps("within_ps")
        w_loaded, w_hi, w_lo = m.sem("w_loaded"), m.sem("w_hi"), m.sem("w_lo")
        g_ready, u_ready, gelu_done, h_chain, h_ready = (m.sem("g_ready"), m.sem("u_ready"),
                                                         m.sem("gelu_done"), m.sem("h_chain"), m.sem("h_ready"))
        h_used, x_ready, stored = m.sem("h_used"), m.sem("x_ready"), m.sem("stored")
        soft, ex_ready, mask_ready, count_ready, route = (m.sem("soft"), m.sem("ex_ready"), m.sem("mask_ready"),
                                                          m.sem("count_ready"), m.sem("route"))
        sc_stored, ranks, bis, hf_ready, pick = (m.sem("sc_stored"), m.sem("ranks"), m.sem("bis"),
                                              m.sem("hf_ready"), m.sem("pick"))
        block = ctx.enter_context(m.run())
        acc_v = acc.rearrange("(t p) c -> p t c", p=P)

        @block.sync
        def _(sp):
            sp.dma_start(WR[:], shared_w.rearrange("u p w -> p u w")).then_inc(w_loaded, 16)
            sp.wait_ge(soft, 5)
            with nc.allow_non_contiguous_dma(reason="64 bytes of scores a row"):
                sp.dma_start(table.rearrange("(t p) c -> p t c", p=P)[:, :, D:ROW], PR[:]).then_inc(sc_stored, 16)

            for b in range(NB):
                sp.wait_ge(x_ready, 2 * (b + 1))
                sp.dma_start(acc_v[:, b * TPB:(b + 1) * TPB, :], X[:, b * TPB:(b + 1) * TPB, :]).then_inc(stored, 16)
            sp.wait_ge(stored, 16 * NB)
            sp.wait_ge(sc_stored, 16)

        @block.gpsimd
        def _(pool):
            for u in range(US):
                pool.wait_ge(w_hi, u + 1)
                pool.tensor_tensor(W[1][:, u, :], WR[:, u, :], W[0][:, u, :].bitcast(F32),
                                   ALU.subtract).then_inc(w_lo, 1)

        @block.scalar
        def _(act):
            act.wait_ge(w_loaded, 16)
            for u in range(US):
                nc.scalar.activation(W[0][:, u, :], WR[:, u, :], ACT.Copy).then_inc(w_hi, 1)
            act.wait_ge(soft, 2)
            nc.scalar.activation(EX[:].rearrange("p t e -> p (t e)"), PR[:].rearrange("p t e -> p (t e)"),
                                 ACT.Exp).then_inc(ex_ready, 1)

            def body(b):
                for u in range(US):
                    n = b * US + u
                    act.wait_ge(g_ready, n + 1)
                    at_least(act, hf_ready, n - 1)
                    nc.scalar.activation(GEL[u % 2][:], GP[u % 2][:], ACT.Gelu).then_inc(gelu_done, 1)

            loop(act, NB, body)

        @block.tensor
        def _(pe):
            def down(n, u, last):
                pe.wait_ge(h_ready, n + 1)
                for t in range(TPB):
                    o = OP[t // 2][:, (t % 2) * D:(t % 2 + 1) * D]
                    ins = split3(pe, o, [HP[u % 2][k][:, t * P:(t + 1) * P] for k in range(2)],
                                 [W[k][:, u, 2 * D:UW] for k in range(2)], u == 0 and t % 2 == 0,
                                 u == US - 1 and t % 2 == 1)
                ins.then_inc(h_used, 1)

            def up(b, u, n):
                pe.wait_ge(w_lo, u + 1)
                at_least(pe, gelu_done, n - 1)
                for g, bank, ready in ((0, GP, g_ready), (1, UP, u_ready)):
                    if g:
                        at_least(pe, hf_ready, n - 1)
                    for c in range(DC):
                        ins = split3(pe, bank[u % 2][:],
                                     [W[k][:, u, g * D + c * P:g * D + (c + 1) * P] for k in range(2)],
                                     [x[:, c, bass.ds(b * BLK, BLK)] for x in (XTH, XTL)], c == 0, c == DC - 1)
                    ins.then_inc(ready, 1)

            def count(n):
                pe.wait_ge(mask_ready, n + 1)
                pe.matmul(CP[:], con["ones"], MASK[:].rearrange("p e t -> p (e t)"), start=True,
                          stop=True).then_inc(count_ready, 1)

            def body(b):
                for u in range(US):
                    n = b * US + u
                    up(b, u, n)
                    if u:
                        if u == 1:
                            at_least(pe, x_ready, 2 * b)
                        down(n - 1, u - 1, False)
                    elif not first(b):
                        down(n - 1, US - 1, False)
                    count(n)

            loop(pe, NB, body)
            down(NB * US - 1, US - 1, True)
            for r in range(3):
                pe.wait_ge(ranks, r + 1)
                flat = (MASK, EQ, MASK)[r][:].rearrange("p e t -> p (e t)")
                pe.matmul(WP[:], con["before"], flat, start=True, stop=True)
                pe.matmul(CP[:], con["ones"], flat, start=True, stop=True).then_inc(route, 1)

        @block.vector
        def _(dve):
            sc = Chain(dve, soft)
            lg = LG[:]
            sc.step(dve.tensor_reduce(MX[:], lg, AX_X, ALU.max))
            sc.step(dve.tensor_tensor(PR[:], lg, MX[:].unsqueeze(2).broadcast_to([P, NT, E]), ALU.subtract))
            dve.wait_ge(ex_ready, 1)
            sc.step(dve.tensor_reduce(MX[:], EX[:], AX_X, ALU.add))
            sc.step(dve.reciprocal(MX[:], MX[:]))
            sc.step(dve.tensor_tensor(PR[:], EX[:], MX[:].unsqueeze(2).broadcast_to([P, NT, E]), ALU.mult))
            sc.step(dve.tensor_copy(SC[:].rearrange("p e t -> p t e"), PR[:]))
            sc.step(dve.memset(THR[:], 0.0))
            sc.step(dve.tensor_copy(BIT[:].bitcast(U32), con["top_bit"].broadcast_to([P, E])))
            sc.step(dve.tensor_copy(CAND[:].bitcast(U32), con["top_bit"].broadcast_to([P, E])))

            def compare(n):
                dve.tensor_tensor(MASK[:], SC[:], CAND[:].unsqueeze(2).broadcast_to([P, E, NT]),
                                  ALU.is_ge).then_inc(mask_ready, 1)

            def update(n):
                ch = Chain(dve, bis, 5 * n)
                dve.wait_ge(count_ready, n + 1)
                ch.step(dve.tensor_reduce(CNT[:], CP[:].rearrange("p (e t) -> p e t", t=NT), AX_X, ALU.add))
                ch.step(dve.scalar_tensor_tensor(HIT[:], CNT[:], CAP - 0.5, CAND[:], ALU.is_ge, ALU.mult))
                ch.step(dve.tensor_tensor(THR[:], THR[:], HIT[:], ALU.max))
                ch.step(dve.tensor_single_scalar(BIT[:].bitcast(U32), BIT[:].bitcast(U32), 1,
                                                 ALU.logical_shift_right))
                ch.step(dve.tensor_tensor(CAND[:].bitcast(U32), THR[:].bitcast(U32), BIT[:].bitcast(U32),
                                          ALU.bitwise_or))

            def hidden(n, u):
                s = u % 2
                ch = Chain(dve, h_chain, n)
                dve.wait_ge(gelu_done, n + 1)
                dve.wait_ge(u_ready, n + 1)
                dve.tensor_tensor(HF[s][:], GEL[s][:], UP[s][:], ALU.mult).then_inc(hf_ready, 1)
                dve.wait_ge(hf_ready, n + 1)
                at_least(dve, h_used, n - 1)
                ch.step(dve.tensor_copy(HP[s][0][:], HF[s][:]))
                dve.tensor_tensor(HP[s][1][:], HF[s][:], HP[s][0][:].bitcast(F32), ALU.subtract).then_inc(h_ready, 1)

            def residual(b):
                dve.wait_ge(h_used, US * (b + 1))
                for k in range(2):
                    xs = X[:, bass.ds(b * TPB + 2 * k, 2), :].rearrange("p t c -> p (t c)")
                    dve.scalar_tensor_tensor(xs, OP[k][:], 0.5, xs, ALU.mult, ALU.add).then_inc(x_ready, 1)

            def body(b):
                for u in range(US):
                    n = b * US + u
                    if u or not first(b):
                        update(n - 1)
                    compare(n)
                    if u == 1 and not first(b):
                        residual(b - 1)
                    hidden(n, u)

            loop(dve, NB, body)
            update(ROUNDS - 1)
            residual(NB - 1)
            rc = Chain(dve, pick)
            thr = THR[:].unsqueeze(2).broadcast_to([P, E, NT])
            flat = lambda x: x[:].rearrange("p e t -> p (e t)")
            totals = CP[:].rearrange("p (e t) -> p e t", t=NT)

            def rank_of():
                rc.step(dve.tensor_tensor_scan(flat(INC), con["restart"], CP[:], 0.0, ALU.mult, ALU.add))
                rc.step(dve.tensor_tensor(RANK[:], INC[:], totals, ALU.subtract))
                rc.step(dve.tensor_tensor(flat(RANK), flat(RANK), WP[:], ALU.add))

            rc.step(dve.tensor_tensor(MASK[:], SC[:], thr, ALU.is_gt))
            dve.tensor_copy(ABOVE[:], MASK[:]).then_inc(ranks, 1)
            rc.step(dve.tensor_tensor(EQ[:], SC[:], thr, ALU.is_equal))
            dve.wait_ge(route, 1)
            rc.step(dve.tensor_reduce(CNT[:], totals, AX_X, ALU.add))
            dve.tensor_scalar(NGT[:], CNT[:], -1.0, float(CAP), ALU.mult, ALU.add).then_inc(ranks, 1)
            dve.wait_ge(ranks, 2)
            dve.wait_ge(route, 2)
            rank_of()
            rc.step(dve.tensor_tensor(FIT[:], RANK[:], NGT[:].unsqueeze(2).broadcast_to([P, E, NT]), ALU.is_lt))
            rc.step(dve.tensor_tensor(FIT[:], FIT[:], EQ[:], ALU.mult))
            dve.tensor_tensor(MASK[:], FIT[:], ABOVE[:], ALU.add).then_inc(ranks, 1)
            dve.wait_ge(ranks, 3)
            dve.wait_ge(route, 3)
            rank_of()
            rc.step(dve.tensor_scalar(COL[:], RANK[:], float(P), None, ALU.is_ge))
            for k in range(2, TPB):
                rc.step(dve.scalar_tensor_tensor(COL[:], RANK[:], float(k * P), COL[:], ALU.is_ge, ALU.add))
            rc.step(dve.scalar_tensor_tensor(RANK[:], COL[:], -float(P), RANK[:], ALU.mult, ALU.add))
            rc.step(dve.scalar_tensor_tensor(RANK[:], RANK[:], 1.0, MASK[:], ALU.add, ALU.mult))
            rc.step(dve.tensor_scalar(SLOT[:], RANK[:], 1.0, None, ALU.subtract))
            for k in range(TPB):
                dve.tensor_scalar(CODE[:, :, :, k, 0], COL[:], float(k), con["row"], ALU.is_equal, ALU.mult)
                dve.scalar_tensor_tensor(CODE[:, :, :, k, 1], COL[:], float(k),
                                         con["tile"].rearrange("p (e t) -> p e t", t=NT), ALU.is_equal, ALU.mult)


def ffn_experts(nc, name, con, acc, expert_w, table, SLOT, CODE):
    with ExitStack() as ctx:
        m = Memory(nc, ctx, name)
        WR = m.sb("w_raw", [P, RAW, UW])
        W = [m.sb(f"w_part{k}", [P, UE, UW], F32R) for k in range(2)]
        GEL = [m.sb(f"gelu{s}", [P, BLK]) for s in range(2)]
        HF = [m.sb(f"h{s}", [P, BLK]) for s in range(2)]
        HP = [[m.sb(f"h_part{k}{s}", [P, BLK], F32R) for k in range(2)] for s in range(2)]
        ONEHOT = m.sb("onehot", [P, NT, P], BF16)
        FOUND = m.sb("found", [P, TPB, 2])
        IDX = [m.sb(f"index{s}", [P, TPB], U32) for s in range(2)]
        XG = [m.sb(f"gathered{s}", [P, TPB, ROW]) for s in range(2)]
        XT = [[m.sb(f"xt_part{k}{s}", [P, DC, BLK], F32R) for k in range(2)] for s in range(2)]
        WT = [m.sb(f"weight{s}", [P, TPB]) for s in range(2)]
        EO = [m.sb(f"out{s}", [P, TPB, D]) for s in range(2)]
        GP = [m.ps(f"g{s}") for s in range(2)]
        UP = [m.ps(f"u{s}") for s in range(2)]
        OP = [m.ps(f"o{s}") for s in range(2)]
        TP = [m.ps(f"t{c}") for c in range(DC)]
        raw_loaded = [m.sem(f"raw_loaded{r}") for r in range(RAW)]
        w_hi, w_lo = m.sem("w_hi"), m.sem("w_lo")
        g_ready, u_ready, gelu_done, hf_ready, h_chain, h_ready, h_used = (
            m.sem(n) for n in ("g_ready", "u_ready", "gelu_done", "hf_ready", "h_chain", "h_ready", "h_used"))
        oh_ready, found_ready, found_read, idx_ready = (
            m.sem(n) for n in ("oh_ready", "found_ready", "found_read", "idx_ready"))
        gathered = [m.sem(f"gathered{s}") for s in range(2)]
        xt_ready, xhi_ready, xlo_ready, wt_ready = (
            m.sem(n) for n in ("xt_ready", "xhi_ready", "xlo_ready", "wt_ready"))
        eo_ready, scattered, note = m.sem("eo_ready"), m.sem("scattered"), m.sem("note")
        block = ctx.enter_context(m.run())
        half = E // 2
        PIECE = 8
        PIECES = NT // PIECE

        @block.sync
        def _(sp):
            def body(e):
                for u in range(UE):
                    n = e * UE + u
                    at_least(sp, w_lo, n - RAW + 1)
                    sp.dma_start(WR[:, u % RAW, :], expert_w[bass.ds(n, 1), :, :].rearrange("a p w -> p (a w)")
                                 ).then_inc(raw_loaded[u % RAW], 16)

            loop(sp, E, body)

        @block.gpsimd
        def _(pool):
            def low(n, u):
                pool.wait_ge(w_hi, n + 1)
                pool.tensor_tensor(W[1][:, u, :], WR[:, u % RAW, :], W[0][:, u, :].bitcast(F32),
                                   ALU.subtract).then_inc(w_lo, 1)

            def gather(x, q):
                pool.wait_ge(idx_ready, x + 1)
                at_least(pool, wt_ready, x - 1)
                at_least(pool, xt_ready, x - 1)
                pool.sem_inc(note, 1)
                for t in range(TPB):
                    pool.indirect_dma_start(XG[q][:, t, :], None, table,
                                            bass.IndirectOffsetOnAxis(IDX[q][:, t:t + 1], 0)
                                            ).then_inc(gathered[q], 16)

            def scatter(x, q):
                pool.wait_ge(eo_ready, TPB * (x + 1))
                at_least(pool, scattered, 16 * TPB * x)
                pool.sem_inc(note, 1)
                for t in range(TPB):
                    pool.indirect_dma_start(acc, bass.IndirectOffsetOnAxis(IDX[q][:, t:t + 1], 0),
                                            EO[q][:, t, :], None, compute_op=ALU.add).then_inc(scattered, 16)

            def body(i, last):
                for q in range(2):
                    e = 2 * i + q
                    final = last and q == 1
                    for u in range(UE):
                        if not (final and u + AHEAD >= UE):
                            low(e * UE + u + AHEAD, (u + AHEAD) % UE)
                        if u == 1 and (q or not first(i)):
                            scatter(e - 1, 1 - q)
                        if u == 4 and not final:
                            gather(e + 1, 1 - q)

            low(0, 0)
            gather(0, 0)
            for u in range(1, AHEAD):
                low(u, u)
            loop_last(pool, half, body)
            scatter(E - 1, 1)
            pool.wait_ge(scattered, 16 * TPB * E)

        @block.scalar
        def _(act):
            def gelu(n, u):
                act.wait_ge(g_ready, n + 1)
                at_least(act, hf_ready, n - 1)
                nc.scalar.activation(GEL[u % 2][:], GP[u % 2][:], ACT.Gelu).then_inc(gelu_done, 1)

            def high(n, e, u):
                act.wait_ge(raw_loaded[u % RAW], 16 * (e * (UE // RAW) + u // RAW + 1))
                at_least(act, h_used, n - UE + 1)
                nc.scalar.activation(W[0][:, u, :], WR[:, u % RAW, :], ACT.Copy).then_inc(w_hi, 1)

            def x_high(x, q):
                act.wait_ge(xt_ready, x + 1)
                for c in range(DC):
                    nc.scalar.activation(XT[q][0][:, c, :], TP[c][:], ACT.Copy).then_inc(xhi_ready, 1)

            def weigh(x, q):
                act.wait_ge(h_used, UE * (x + 1))
                act.wait_ge(wt_ready, x + 1)
                at_least(act, scattered, 16 * TPB * (x - 1))
                for t in range(TPB):
                    nc.scalar.activation(EO[q][:, t, :], OP[t // 2][:, (t % 2) * D:(t % 2 + 1) * D], ACT.Copy,
                                         scale=WT[q][:, t:t + 1]).then_inc(eo_ready, 1)

            def body(i, last):
                for q in range(2):
                    e = 2 * i + q
                    final = last and q == 1
                    for u in range(UE):
                        n = e * UE + u
                        if u == UE - 1 and not final:
                            x_high(e + 1, 1 - q)
                        gelu(n, u)
                        if u == 0 and (q or not first(i)):
                            weigh(e - 1, 1 - q)
                        if not (final and u + AHEAD >= UE):
                            a = u + AHEAD
                            high(n + AHEAD, e + a // UE, a % UE)

            for u in range(AHEAD):
                high(u, 0, u)
            x_high(0, 0)
            loop_last(act, half, body)
            weigh(E - 1, 1)

        @block.vector
        def _(dve):
            def onehot(x, k):
                at_least(dve, found_ready, x)
                sl = slice(k * PIECE, (k + 1) * PIECE)
                dve.tensor_tensor(ONEHOT[:, sl, :], con["slots"].unsqueeze(1).broadcast_to([P, PIECE, P]),
                                  SLOT[:, bass.ds(x, 1), sl].rearrange("p a t -> p (a t)").unsqueeze(2)
                                  .broadcast_to([P, PIECE, P]), ALU.is_equal).then_inc(oh_ready, 1)

            def index(x, q):
                dve.wait_ge(found_ready, x + 1)
                dve.tensor_copy(FOUND[:].rearrange("p t v -> p (t v)"), TP[0][:, 0:2 * TPB]).then_inc(found_read, 1)
                dve.wait_ge(found_read, x + 1)
                at_least(dve, scattered, 16 * TPB * (x - 1))
                dve.scalar_tensor_tensor(IDX[q][:], FOUND[:, :, 1], float(P), FOUND[:, :, 0], ALU.mult,
                                         ALU.add).then_inc(idx_ready, 1)

            def x_low(x, q, k):
                dve.wait_ge(gathered[q], 16 * TPB * (k + 1))
                dve.tensor_scalar(WT[q][:], XG[q][:, :, bass.ds(x + D, 1)].rearrange("p t a -> p (t a)"), 0.5, None,
                                  ALU.mult).then_inc(wt_ready, 1)
                dve.wait_ge(xhi_ready, DC * (x + 1))
                for c in range(DC):
                    dve.tensor_tensor(XT[q][1][:, c, :], TP[c][:], XT[q][0][:, c, :].bitcast(F32),
                                      ALU.subtract).then_inc(xlo_ready, 1)

            def hidden(n, u):
                s = u % 2
                dve.wait_ge(gelu_done, n + 1)
                dve.wait_ge(u_ready, n + 1)
                dve.tensor_tensor(HF[s][:], GEL[s][:], UP[s][:], ALU.mult).then_inc(hf_ready, 1)
                dve.wait_ge(hf_ready, n + 1)
                at_least(dve, h_used, n - 1)
                dve.tensor_copy(HP[s][0][:], HF[s][:]).then_inc(h_chain, 1)
                dve.wait_ge(h_chain, n + 1)
                dve.tensor_tensor(HP[s][1][:], HF[s][:], HP[s][0][:].bitcast(F32), ALU.subtract).then_inc(h_ready, 1)

            def body(i, last):
                for q in range(2):
                    e = 2 * i + q
                    final = last and q == 1
                    for u in range(UE):
                        if u == UE - 1 and not final:
                            x_low(e + 1, 1 - q, i + q)
                        if u < PIECES // 2 and not final:
                            onehot(e + 1, 2 * u)
                            onehot(e + 1, 2 * u + 1)
                        if u == 4 and not final:
                            index(e + 1, 1 - q)
                        hidden(e * UE + u, u)

            for k in range(PIECES):
                onehot(0, k)
            index(0, 0)
            x_low(0, 0, 0)
            loop_last(dve, half, body)

        @block.tensor
        def _(pe):
            def find(x):
                at_least(pe, xlo_ready, DC * x)
                pe.wait_ge(oh_ready, PIECES * (x + 1))
                for t in range(NT):
                    ins = pe.matmul(TP[0][:, 0:2 * TPB], ONEHOT[:, t, :],
                                    CODE[:, bass.ds(x, 1), t, :, :].rearrange("p a k v -> p (a k v)"),
                                    start=t == 0, stop=t == NT - 1)
                ins.then_inc(found_ready, 1)

            def transposes(x, q, k):
                pe.wait_ge(gathered[q], 16 * TPB * (k + 1))
                pe.wait_ge(found_read, x + 1)
                for c in range(DC):
                    for t in range(TPB):
                        ins = pe.transpose(TP[c][:, t * P:(t + 1) * P], XG[q][:, t, c * P:(c + 1) * P], con["ident"])
                ins.then_inc(xt_ready, 1)

            def up(n, u, q):
                pe.wait_ge(w_lo, n + 1)
                at_least(pe, gelu_done, n - 1)
                for g, bank, ready in ((0, GP, g_ready), (1, UP, u_ready)):
                    if g:
                        at_least(pe, hf_ready, n - 1)
                    for c in range(DC):
                        ins = split3(pe, bank[u % 2][:],
                                     [W[k][:, u, g * D + c * P:g * D + (c + 1) * P] for k in range(2)],
                                     [XT[q][k][:, c, :] for k in range(2)], c == 0, c == DC - 1)
                    ins.then_inc(ready, 1)

            def down(n, u):
                pe.wait_ge(h_ready, n + 1)
                for t in range(TPB):
                    ins = split3(pe, OP[t // 2][:, (t % 2) * D:(t % 2 + 1) * D],
                                 [HP[u % 2][k][:, t * P:(t + 1) * P] for k in range(2)],
                                 [W[k][:, u, 2 * D:UW] for k in range(2)], u == 0 and t % 2 == 0,
                                 u == UE - 1 and t % 2 == 1)
                ins.then_inc(h_used, 1)

            def body(i, last):
                for q in range(2):
                    e = 2 * i + q
                    final = last and q == 1
                    for u in range(UE):
                        n = e * UE + u
                        if u == 0:
                            pe.wait_ge(xlo_ready, DC * (e + 1))
                        up(n, u, q)
                        if u == 1:
                            at_least(pe, eo_ready, TPB * e)
                        if u or q or not first(i):
                            down(n - 1, (u - 1) % UE)
                        if u == 3 and not final:
                            find(e + 1)
                        if u == 6 and not final:
                            transposes(e + 1, 1 - q, i + q)

            find(0)
            transposes(0, 0, 0)
            loop_last(pe, half, body)
            down(E * UE - 1, UE - 1)


def ffn(nc, name, con, x_in, acc, gate, shared_w, expert_w, table):
    with ExitStack() as outer:
        m = Memory(nc, outer, name)
        SLOT = m.sb("slot", [P, E, NT], BF16)
        CODE = m.sb("code", [P, E, NT, TPB, 2], BF16)
        with ExitStack() as ctx:
            m = Memory(nc, ctx, name)
            X = m.sb("x", [P, NT, D])
            XTH = m.sb("xth", [P, DC, TOK], F32R)
            XTL = m.sb("xtl", [P, DC, TOK], F32R)
            LG = m.sb("logits", [P, NT, E])
            ffn_prepare(nc, name + "p_", con, X, x_in, gate, table, XTH, XTL, LG)
            ffn_shared_and_route(nc, name + "s_", con, X, acc, shared_w, table, XTH, XTL, LG, SLOT, CODE)
        ffn_experts(nc, name + "e_", con, acc, expert_w, table, SLOT, CODE)


def attention(nc, name, con, x_in, out, w_in, bias_in, row_bias_in):
    with ExitStack() as ctx:
        m = Memory(nc, ctx, name)
        nm = Norm(m)
        WR = m.sb("w_raw", [P, 4, DC, D])
        W = [m.sb(f"w_part{k}", [P, 4, DC, D], F32R) for k in range(2)]
        BC = m.sb("bias_col", [P, 2, DC])
        BR = m.sb("bias_row", [P, 2, D])
        X = [m.sb(f"x{s}", [P, TPB, D]) for s in range(2)]
        XN = m.sb("xn", [P, TPB, D])
        XT = [m.sb(f"xt_part{k}", [P, DC, BLK], F32R) for k in range(2)]
        XM = m.sb("x_sum", [P, DC, TPB])
        XA = m.sb("x_means", [P, DC, 4, NC])
        KT = m.sb("k_means", [P, DC, NC])
        KM = m.sb("k_means_by_head", [P, DC, GH, NC])
        VB = m.sb("v_means_all", [P, D])
        VM = m.sb("v_means_by_head", [P, D])
        Q = m.sb("q", [P, DC, BLK])
        KE = [m.sb(f"k_parity{k}", [P, DC, BLK]) for k in range(2)]
        V = m.sb("v", [P, TPB, H, HD + 1])
        MX = m.sb("max", [P, 4, 4])
        PB = m.sb("probs", [P, 4, 4, P])
        PT = [m.sb(f"probs_t{s}", [P, BLK]) for s in range(2)]
        SI = m.sb("inter", [P, H, NC])
        AI = m.sb("inter_probs", [P, H, NC])
        IM, IS, IR, RS = (m.sb(n, [P, H]) for n in ("inter_max", "inter_sum", "inter_recip", "recip"))
        AT = m.sb("inter_t", [P, BLK])
        O = m.sb("heads", [P, H, HD])
        OT = [m.sb(f"heads_t{k}", [P, DC, P], F32R) for k in range(2)]
        Y = [m.sb(f"y{s}", [P, TPB, D]) for s in range(2)]
        B = [m.ps(f"b{i}") for i in range(8)]
        S, TO, IB, OB = B[0:4], B[4], B[6], B[7]
        names = ("w_loaded", "w_hi", "w_lo", "clear", "xt_ready", "x_hi", "x_lo", "x_sums", "x_means", "q_mm", "k_mm",
                 "v_mm", "km_mm", "vm_mm", "q_ready", "k_ready", "v_ready", "kt_ready", "km_ready", "vb_ready",
                 "vm_ready", "s_mm", "max_ready", "sub_ready", "exp_ready", "pt_mm", "pt_ready", "pv_mm", "i_mm",
                 "i_chain", "isub_ready", "iexp_ready", "anorm_ready", "at_mm", "at_ready", "oi_mm", "o_chain",
                 "heads_ready", "ot_mm", "ot_hi", "ot_lo", "y_mm", "y_chain", "y_ready")
        sem = {n: m.sem(n) for n in names}
        x_loaded = [m.sem(f"x_loaded{s}") for s in range(2)]
        stored = [m.sem(f"stored{s}") for s in range(2)]
        block = ctx.enter_context(m.run())
        half = NB // 2
        x_v = x_in.rearrange("(t p) c -> p t c", p=P)
        out_v = out.rearrange("(t p) c -> p t c", p=P)

        @block.sync
        def _(sp):
            sp.dma_start(WR[:], w_in).then_inc(sem["w_loaded"], 16)
            sp.dma_start(BC[:], bias_in).then_inc(sem["w_loaded"], 16)
            sp.dma_start(BR[:], row_bias_in).then_inc(sem["w_loaded"], 16)
            for b in range(NB + 1):
                if b < NB:
                    at_least(sp, sem["y_ready"], TPB * (b - 1))
                    sp.dma_start(X[b % 2][:], x_v[:, b * TPB:(b + 1) * TPB, :]).then_inc(x_loaded[b % 2], 16)
                if b:
                    sp.wait_ge(sem["y_ready"], TPB * b)
                    sp.dma_start(out_v[:, (b - 1) * TPB:b * TPB, :], Y[(b - 1) % 2][:]).then_inc(stored[(b - 1) % 2], 16)
            for s in range(2):
                sp.wait_ge(stored[s], 16 * half)

        @block.gpsimd
        def _(pool):
            pool.memset(XA[:], 0.0).then_inc(sem["clear"], 1)
            pool.memset(V[:], 1.0).then_inc(sem["clear"], 1)
            pool.wait_ge(sem["w_hi"], 4)
            for k in range(4):
                pool.tensor_tensor(W[1][:, k], WR[:, k], W[0][:, k].bitcast(F32), ALU.subtract).then_inc(sem["w_lo"], 1)

        @block.scalar
        def _(act):
            act.wait_ge(sem["w_loaded"], 48)
            for k in range(4):
                nc.scalar.activation(W[0][:, k], WR[:, k], ACT.Copy).then_inc(sem["w_hi"], 1)

            def chunk(n, j):
                for i in range(4):
                    act.wait_ge(sem["sub_ready"], 4 * n + i + 1)
                    nc.scalar.activation(PB[:, i], PB[:, i], ACT.Exp, scale=SCALE).then_inc(sem["exp_ready"], 1)
                    if i == 1:
                        act.wait_ge(sem["isub_ready"], n + 1)
                        nc.scalar.activation(AI[:], SI[:], ACT.Exp, scale=SCALE).then_inc(sem["iexp_ready"], 1)
                    if i:
                        evacuate(n, i - 1)
                evacuate(n, 3)
                act.wait_ge(sem["at_mm"], n + 1)
                nc.scalar.activation(AT[:], IB[:], ACT.Copy).then_inc(sem["at_ready"], 1)
                act.wait_ge(sem["ot_mm"], n + 1)
                nc.scalar.activation(OT[0][:].rearrange("p c t -> p (c t)"), TO[:, 0:D], ACT.Copy).then_inc(sem["ot_hi"], 1)

            def evacuate(n, i):
                act.wait_ge(sem["pt_mm"], 4 * n + i + 1)
                at_least(act, sem["pv_mm"], 4 * n + i - 1)
                nc.scalar.activation(PT[i % 2][:], S[i][:], ACT.Copy).then_inc(sem["pt_ready"], 1)

            def body(i):
                for s in range(2):
                    b = 2 * i + s
                    nm.root(act, b, s)
                    act.wait_ge(sem["xt_ready"], b + 1)
                    for c in range(DC):
                        nc.scalar.activation(XT[0][:, c, :], B[c][:], ACT.Copy).then_inc(sem["x_hi"], 1)
                    act.wait_ge(sem["q_mm"], b + 1)
                    for g in range(DC):
                        nc.scalar.activation(Q[:, g, :], B[2 + g][:], ACT.Identity,
                                             bias=BC[:, 0, g:g + 1]).then_inc(sem["q_ready"], 1)
                    for j in range(TPB):
                        chunk(b * TPB + j, j)

            loop(act, half, body)

        @block.vector
        def _(dve):
            def chain(name, base):
                return Chain(dve, sem[name], base)

            def block_stage(i, s):
                b = 2 * i + s
                tiles = lambda t: X[s][:, t, :]
                dve.wait_ge(x_loaded[s], 16 * (i + 1))
                nm.statistics(dve, b, s, tiles)
                nm.scale(dve, b, s)
                nm.apply(dve, b, s, XN, tiles)
                dve.wait_ge(sem["x_hi"], DC * (b + 1))
                for c in range(DC):
                    dve.tensor_reduce(XM[:, c, :], B[c][:].rearrange("p (t k) -> p t k", k=P), AX_X,
                                      ALU.add).then_inc(sem["x_sums"], 1)
                    dve.tensor_tensor(XT[1][:, c, :], B[c][:], XT[0][:, c, :].bitcast(F32),
                                      ALU.subtract).then_inc(sem["x_lo"], 1)
                dve.wait_ge(sem["x_sums"], DC * (b + 1))
                for c in range(DC):
                    dve.tensor_scalar(XA[:, c, :, bass.ds(b * TPB, TPB)],
                                      XM[:, c, :].unsqueeze(1).broadcast_to([P, 4, TPB]), 1.0 / P, None,
                                      ALU.mult).then_inc(sem["x_means"], 1)
                dve.wait_ge(sem["k_mm"], b + 1)
                for g in range(DC):
                    for k in range(2):
                        dve.tensor_scalar(KE[k][:, g, :], B[4 + g][:], BC[:, 1, g:g + 1], con["parity"][:, k:k + 1],
                                          ALU.add, ALU.mult).then_inc(sem["k_ready"], 1)
                dve.wait_ge(sem["v_mm"], b + 1)
                for t in range(TPB):
                    dve.tensor_tensor(V[:, t, :, 0:HD],
                                      B[6 + t // 2][:, (t % 2) * D:(t % 2 + 1) * D].rearrange("p (h d) -> p h d", d=HD),
                                      BR[:, 0, :].rearrange("p (h d) -> p h d", d=HD), ALU.add).then_inc(sem["v_ready"], 1)
                dve.wait_ge(sem["km_mm"], b + 1)
                for g in range(DC):
                    dve.tensor_scalar(KT[:, g, :], B[0][:, g * NC:(g + 1) * NC], BC[:, 1, g:g + 1], None,
                                      ALU.add).then_inc(sem["kt_ready"], 1)
                dve.tensor_tensor(VB[:], B[1][:, 0:D], BR[:, 0, :], ALU.add).then_inc(sem["vb_ready"], 1)
                dve.wait_ge(sem["kt_ready"], DC * (b + 1))
                for g in range(DC):
                    dve.tensor_tensor(KM[:, g], KT[:, g, :].unsqueeze(1).broadcast_to([P, GH, NC]),
                                      con["own_head"].unsqueeze(2).broadcast_to([P, GH, NC]),
                                      ALU.mult).then_inc(sem["km_ready"], 1)
                dve.wait_ge(sem["vb_ready"], b + 1)
                dve.tensor_tensor(VM[:], VB[:], con["own_rows"], ALU.mult).then_inc(sem["vm_ready"], 1)

            def finish(n, j, s):
                dve.wait_ge(sem["ot_hi"], n + 1)
                dve.tensor_tensor(OT[1][:].rearrange("p c t -> p (c t)"), TO[:, 0:D],
                                  OT[0][:].rearrange("p c t -> p (c t)").bitcast(F32), ALU.subtract).then_inc(sem["ot_lo"], 1)
                dve.wait_ge(sem["y_mm"], n + 1)
                dve.tensor_tensor(Y[s][:, j, :], TO[:, D:2 * D], BR[:, 1, :], ALU.add).then_inc(sem["y_chain"], 1)
                dve.wait_ge(sem["y_chain"], n + 1)
                dve.tensor_tensor(Y[s][:, j, :], Y[s][:, j, :], X[s][:, j, :], ALU.add).then_inc(sem["y_ready"], 1)

            def chunk(n, j, s):
                dve.wait_ge(sem["s_mm"], n + 1)
                for i in range(4):
                    dve.tensor_reduce(MX[:, i, :], S[i][:].rearrange("p (q k) -> p q k", k=P), AX_X,
                                      ALU.max).then_inc(sem["max_ready"], 1)
                    dve.wait_ge(sem["max_ready"], 4 * n + i + 1)
                    at_least(dve, sem["pt_mm"], 4 * (n - 1) + i + 1)
                    dve.tensor_tensor(PB[:, i], S[i][:].rearrange("p (q k) -> p q k", k=P),
                                      MX[:, i, :].unsqueeze(2).broadcast_to([P, 4, P]),
                                      ALU.subtract).then_inc(sem["sub_ready"], 1)
                    if i == 0:
                        ic = chain("i_chain", 4 * n)
                        dve.wait_ge(sem["i_mm"], n + 1)
                        ic.step(dve.tensor_tensor(SI[:], IB[:].rearrange("p (h c) -> p h c", c=NC),
                                                  con["causal"][:, bass.ds(n, 1), :].broadcast_to([P, H, NC]), ALU.add))
                        ic.step(dve.tensor_reduce(IM[:], SI[:], AX_X, ALU.max))
                        dve.tensor_tensor(SI[:], SI[:], IM[:].unsqueeze(2).broadcast_to([P, H, NC]),
                                          ALU.subtract).then_inc(sem["isub_ready"], 1)
                dve.wait_ge(sem["iexp_ready"], n + 1)
                ic = chain("i_chain", 4 * n + 2)
                ic.step(dve.tensor_reduce(IS[:], AI[:], AX_X, ALU.add))
                ic.step(dve.reciprocal(IR[:], IS[:]))
                dve.tensor_tensor(AI[:], AI[:], IR[:].unsqueeze(2).broadcast_to([P, H, NC]),
                                  ALU.mult).then_inc(sem["anorm_ready"], 1)
                oc = chain("o_chain", 2 * n)
                heads = OB[:, 0:H * (HD + 1)].rearrange("p (h d) -> p h d", d=HD + 1)
                dve.wait_ge(sem["pv_mm"], 4 * (n + 1))
                oc.step(dve.reciprocal(RS[:].unsqueeze(2), heads[:, :, HD:HD + 1]))
                oc.step(dve.tensor_tensor(O[:], heads[:, :, 0:HD], RS[:].unsqueeze(2).broadcast_to([P, H, HD]), ALU.mult))
                dve.wait_ge(sem["oi_mm"], n + 1)
                dve.tensor_tensor(O[:].rearrange("p h d -> p (h d)"), O[:].rearrange("p h d -> p (h d)"), IB[:, 0:D],
                                  ALU.add).then_inc(sem["heads_ready"], 1)
                finish(n, j, s)

            def body(i):
                for s in range(2):
                    b = 2 * i + s
                    block_stage(i, s)
                    at_least(dve, stored[s], 16 * i)
                    for j in range(TPB):
                        chunk(b * TPB + j, j, s)

            loop(dve, half, body)

        @block.tensor
        def _(pe):
            pe.wait_ge(sem["w_lo"], 4)

            def block_stage(b):
                pe.wait_ge(nm.xn_ready, TPB * (b + 1))
                for c in range(DC):
                    for t in range(TPB):
                        ins = pe.transpose(B[c][:, t * P:(t + 1) * P], XN[:, t, c * P:(c + 1) * P], con["ident"])
                ins.then_inc(sem["xt_ready"], 1)
                pe.wait_ge(sem["x_lo"], DC * (b + 1))
                for k, done in ((0, "q_mm"), (1, "k_mm")):
                    for g in range(DC):
                        for c in range(DC):
                            ins = split3(pe, B[2 + 2 * k + g][:],
                                         [W[h][:, k, c, g * P:(g + 1) * P] for h in range(2)],
                                         [XT[h][:, c, :] for h in range(2)], c == 0, c == DC - 1)
                    ins.then_inc(sem[done], 1)
                for t in range(TPB):
                    for c in range(DC):
                        ins = split3(pe, B[6 + t // 2][:, (t % 2) * D:(t % 2 + 1) * D],
                                     [XT[h][:, c, t * P:(t + 1) * P] for h in range(2)],
                                     [W[h][:, 2, c, :] for h in range(2)], c == 0, c == DC - 1)
                ins.then_inc(sem["v_mm"], 1)
                pe.wait_ge(sem["x_means"], DC * (b + 1))
                pe.wait_ge(sem["clear"], 2)
                for g in range(DC):
                    for c in range(DC):
                        ins = pe.matmul(B[0][:, g * NC:(g + 1) * NC], WR[:, 1, c, g * P:(g + 1) * P], XA[:, c, 0, :],
                                        start=c == 0, stop=c == DC - 1)
                for c in range(DC):
                    ins = pe.matmul(B[1][:, 0:D], XA[:, c].rearrange("p a j -> p (a j)"), WR[:, 2, c, :],
                                    start=c == 0, stop=c == DC - 1)
                ins.then_inc(sem["km_mm"], 1)

            def chunk(n, j):
                rows = slice(j * P, (j + 1) * P)
                for g in range(DC):
                    for k in range(2):
                        for i in range(4):
                            strip = slice(32 * i, 32 * i + 32)
                            ins = pe.matmul(S[i][:, (2 * g + k) * P:(2 * g + k + 1) * P], Q[strip, g, rows],
                                            KE[k][strip, g, rows], start=True, stop=True)
                ins.then_inc(sem["s_mm"], 1)
                for g in range(DC):
                    ins = pe.matmul(IB[:, g * D:(g + 1) * D], Q[:, g, rows],
                                    KM[:, g].rearrange("p h j -> p (h j)"), start=True, stop=True)
                ins.then_inc(sem["i_mm"], 1)

                def turn(i):
                    pe.wait_ge(sem["exp_ready"], 4 * n + i + 1)
                    for q in range(4):
                        ins = pe.transpose(S[i][:, q * P:(q + 1) * P], PB[:, i, q, :], con["ident"])
                    ins.then_inc(sem["pt_mm"], 1)

                def values(i):
                    pe.wait_ge(sem["pt_ready"], 4 * n + i + 1)
                    for q in range(4):
                        h = (q // 2) * GH + 2 * i + q % 2
                        ins = pe.matmul(OB[:, h * (HD + 1):(h + 1) * (HD + 1)], PT[i % 2][:, q * P:(q + 1) * P],
                                        V[:, j, h, :], start=True, stop=True)
                    ins.then_inc(sem["pv_mm"], 1)

                turn(0)
                for i in range(1, 4):
                    turn(i)
                    values(i - 1)
                values(3)
                pe.wait_ge(sem["anorm_ready"], n + 1)
                for g in range(4):
                    ins = pe.transpose(IB[:, g * P:(g + 1) * P], AI[:, 4 * g:4 * g + 4, :].rearrange("p h j -> p (h j)"),
                                       con["ident"])
                ins.then_inc(sem["at_mm"], 1)
                pe.wait_ge(sem["at_ready"], n + 1)
                for g in range(4):
                    ins = pe.matmul(IB[:, g * 64:(g + 1) * 64], AT[:, g * P:(g + 1) * P], VM[:, g * 64:(g + 1) * 64],
                                    start=True, stop=True)
                ins.then_inc(sem["oi_mm"], 1)
                pe.wait_ge(sem["heads_ready"], n + 1)
                for c in range(DC):
                    ins = pe.transpose(TO[:, c * P:(c + 1) * P],
                                       O[:, c * GH:(c + 1) * GH, :].rearrange("p h d -> p (h d)"), con["ident"])
                ins.then_inc(sem["ot_mm"], 1)
                pe.wait_ge(sem["ot_lo"], n + 1)
                for c in range(DC):
                    ins = split3(pe, TO[:, D:2 * D], [OT[h][:, c, :] for h in range(2)],
                                 [W[h][:, 3, c, :] for h in range(2)], c == 0, c == DC - 1)
                ins.then_inc(sem["y_mm"], 1)

            def body(i):
                for s in range(2):
                    b = 2 * i + s
                    block_stage(b)
                    pe.wait_ge(sem["q_ready"], DC * (b + 1))
                    pe.wait_ge(sem["k_ready"], 2 * DC * (b + 1))
                    pe.wait_ge(sem["v_ready"], TPB * (b + 1))
                    pe.wait_ge(sem["km_ready"], DC * (b + 1))
                    pe.wait_ge(sem["vm_ready"], b + 1)
                    for j in range(TPB):
                        chunk(b * TPB + j, j)

            loop(pe, half, body)


CONSTANTS = [("ident", (P, P), F32), ("ones", (P, P), BF16), ("before", (P, P), BF16), ("slots", (P, P), BF16),
             ("row", (P, 1), F32), ("tile", (P, E * NT), F32), ("restart", (P, E * NT), F32), ("top_bit", (P, 1), U32),
             ("parity", (P, 2), F32), ("own_head", (P, GH), F32), ("own_rows", (P, D), F32), ("causal", (P, NC, NC), F32)]


def program(nc, out, x, gate, shared_w, expert_w, attn_w, attn_bias_col, attn_bias_row, **constants):
    table = nc.dram_tensor("table", (TOK, ROW), F32, kind="Internal").ap()
    x1 = nc.dram_tensor("x_after_ffn", (TOK, D), F32, kind="Internal").ap()
    x2 = nc.dram_tensor("x_after_attention", (TOK, D), F32, kind="Internal").ap()
    with ExitStack() as ctx:
        m = Memory(nc, ctx, "")
        con, loaded = {}, m.sem("constants_loaded")
        tiles = [(n, m.sb("const_" + n, list(shape), dt)) for n, shape, dt in CONSTANTS]
        with m.run() as block:
            @block.sync
            def _(sp):
                for n, t in tiles:
                    con[n] = t[:]
                    sp.dma_start(t[:], constants[n]).then_inc(loaded, 16)
                sp.wait_ge(loaded, 16 * len(tiles))
        ffn(nc, "f1_", con, x, x1, gate, shared_w, expert_w, table)
        attention(nc, "at_", con, x1, x2, attn_w, attn_bias_col, attn_bias_row)
        ffn(nc, "f2_", con, x2, out, gate, shared_w, expert_w, table)


def kernel(**inputs):
    import ml_dtypes
    import numpy as np
    import concourse.bacc as bacc
    from concourse.bass_utils import run_bass_kernel_spmd

    a = {k.replace("L0_", ""): np.asarray(v) for k, v in inputs.items()}
    f, p = np.float32, np.arange(P)

    def units(gate, up, down):
        rows = [w.reshape(-1, P, DC, P).transpose(0, 3, 2, 1).reshape(-1, P, D) for w in (gate, up)]
        return np.ascontiguousarray(np.concatenate(rows + [np.swapaxes(down, -1, -2).reshape(-1, P, D)], -1))

    def columns(w):
        return np.ascontiguousarray(w.reshape(-1, DC, P).transpose(2, 1, 0))

    arrays = {
        "x": a["attn_hidden_states"].reshape(TOK, D),
        "gate": columns(a["ffn_gate_w"]),
        "shared_w": units(a["ffn_Sg"], a["ffn_Su"], a["ffn_Sd"]),
        "expert_w": units(a["ffn_Wg"], a["ffn_Wu"], a["ffn_Wd"]),
        "attn_w": np.ascontiguousarray(np.stack([columns(a["attn_w" + n]) for n in "qkvo"], 1)),
        "attn_bias_col": np.ascontiguousarray(np.stack([a["attn_b" + n].reshape(DC, P).T for n in "qk"], 1)),
        "attn_bias_row": np.ascontiguousarray(np.broadcast_to(np.stack([a["attn_b" + n] for n in "vo"]), (P, 2, D))),
        "ident": np.eye(P, dtype=f),
        "ones": np.ones((P, P), ml_dtypes.bfloat16),
        "before": np.triu(np.ones((P, P)), 1).astype(ml_dtypes.bfloat16),
        "slots": np.ascontiguousarray(np.broadcast_to(p, (P, P))).astype(ml_dtypes.bfloat16),
        "row": p.astype(f)[:, None],
        "tile": np.tile(np.arange(NT, dtype=f), (P, E)),
        "restart": np.tile((np.arange(NT) > 0).astype(f), (P, E)),
        "top_bit": np.full((P, 1), 1 << (BITS - 1), np.uint32),
        "parity": np.stack([p // HD % 2 == 0, p // HD % 2 == 1], 1).astype(f),
        "own_head": (p[:, None] // HD == np.arange(GH)).astype(f),
        "own_rows": (p[:, None] // NC == np.arange(D) // HD % 4).astype(f),
        "causal": np.tile(np.where(np.arange(NC)[:, None] >= np.arange(NC), 0, NEG).astype(f), (P, 1, 1)),
    }
    nc = bacc.Bacc("TRN2", target_bir_lowering=False, num_devices=1)
    handles = {n: nc.dram_tensor("in_" + n, v.shape, mybir.dt.from_np(v.dtype), kind="ExternalInput").ap()
               for n, v in arrays.items()}
    out = nc.dram_tensor("out", (TOK, D), F32, kind="ExternalOutput").ap()
    program(nc, out, **handles)
    r = run_bass_kernel_spmd(nc, [{"in_" + n: v for n, v in arrays.items()}], core_ids=[0])
    return r.results[0]["out"].reshape(1, TOK, D)
```

```python
from contextlib import ExitStack, contextmanager

import concourse.bass as bass
from concourse import mybir

F32 = mybir.dt.float32
F32R = mybir.dt.float32r
BF16 = mybir.dt.bfloat16
U32 = mybir.dt.uint32
ALU = mybir.AluOpType
ACT = mybir.ActivationFunctionType
AX_X = mybir.AxisListType.X

P = 128
TOK = 4096
D = 256
DC = D // P
NT = TOK // P
BLK = 512
TPB = BLK // P
NB = TOK // BLK
E = 16
CAP = TOK * 2 // E
IE = 1024
UE = IE // P
US = 512 // P
UW = 3 * D
ROW = D + E
EPS = 1e-5
BITS = 30
ROUNDS = NB * US
AHEAD = 6
RAW = 4

H = 16
HD = D // H
GH = P // HD
NC = NT
SCALE = 1.0 / HD ** 0.5
NEG = -1e30


def at_least(engine, sem, value):
    if isinstance(value, int) and value <= 0:
        return
    engine.wait_ge(sem, value)


def first(i):
    return isinstance(i, int) and i == 0


def loop(engine, n, body):
    body(0)
    if n > 1:
        with engine.Fori(1, n) as i:
            body(i)


def loop_last(engine, n, body):
    body(0, False)
    with engine.Fori(1, n - 1) as i:
        body(i, False)
    body(n - 1, True)


class Chain:

    def __init__(self, engine, sem, base=0):
        self.engine, self.sem, self.base, self.n = engine, sem, base, 0

    def step(self, instruction):
        self.n += 1
        instruction.then_inc(self.sem, 1)
        self.engine.wait_ge(self.sem, self.base + self.n)


def split3(pe, out, lhs, rhs, first, last):
    pairs = [(0, 0), (0, 1), (1, 0)]
    for n, (a, b) in enumerate(pairs):
        ins = pe.matmul(out, lhs[a], rhs[b], start=first and n == 0, stop=last and n == 2,
                        skip_group_check=True)
    return ins


class Memory:

    def __init__(self, nc, ctx, prefix):
        self.nc, self.ctx, self.prefix, self.sems = nc, ctx, prefix, []

    def sb(self, name, shape, dt=F32):
        return self.ctx.enter_context(self.nc.sbuf_tensor(self.prefix + name, shape, dt))

    def ps(self, name, shape=(P, BLK), dt=F32):
        return self.ctx.enter_context(self.nc.psum_tensor(self.prefix + name, list(shape), dt))

    def sem(self, name):
        self.sems.append(self.ctx.enter_context(self.nc.semaphore(self.prefix + name)))
        return self.sems[-1]

    @contextmanager
    def run(self):
        with self.nc.Block() as block:
            yield block
        with self.nc.Block() as block:
            @block.sync
            def _(sp):
                for s in self.sems:
                    sp.sem_clear(s)


class Norm:

    STEPS = 7

    def __init__(self, m):
        self.stats = [m.sb(f"stats{s}", [P, TPB, 6]) for s in range(2)]
        self.mv = [m.sb(f"meanvar{s}", [P, TPB, 2]) for s in range(2)]
        self.ve = [m.sb(f"vareps{s}", [P, TPB]) for s in range(2)]
        self.sd = [m.sb(f"std{s}", [P, TPB]) for s in range(2)]
        self.ri = [m.sb(f"rstd{s}", [P, 3, TPB]) for s in range(2)]
        self.chain, self.note = m.sem("norm_chain"), m.sem("norm_note")
        self.var_ready, self.std_ready, self.xn_ready = m.sem("var_ready"), m.sem("std_ready"), m.sem("xn_ready")

    def statistics(self, dve, b, s, tiles):
        for t in range(TPB):
            last = dve.bn_stats(self.stats[s][:, t, :], tiles(t))
        Chain(dve, self.chain, b * self.STEPS).step(last)
        dve.sem_inc(self.note, 1)
        for t in range(TPB):
            last = dve.bn_aggr(self.mv[s][:, t, :], self.stats[s][:, t, :])
        Chain(dve, self.chain, b * self.STEPS + 1).step(last)
        dve.tensor_scalar(self.ve[s][:], self.mv[s][:, :, 1], EPS, None, ALU.add).then_inc(self.var_ready, 1)

    def root(self, act, b, s):
        act.wait_ge(self.var_ready, b + 1)
        act.activation(self.sd[s][:], self.ve[s][:], ACT.Sqrt).then_inc(self.std_ready, 1)

    def scale(self, dve, b, s):
        dve.wait_ge(self.std_ready, b + 1)
        ch = Chain(dve, self.chain, b * self.STEPS + 2)
        r0, r1, r2 = (self.ri[s][:, k, :] for k in range(3))
        ch.step(dve.reciprocal(r0, self.sd[s][:]))
        ch.step(dve.tensor_tensor(r1, r0, r0, ALU.mult))
        ch.step(dve.tensor_tensor(r2, r1, self.ve[s][:], ALU.mult))
        ch.step(dve.tensor_scalar(r1, r2, -0.5, 1.5, ALU.mult, ALU.add))
        ch.step(dve.tensor_tensor(r2, r0, r1, ALU.mult))

    def apply(self, dve, b, s, out, tiles):
        for t in range(TPB):
            dve.tensor_scalar(out[:, t, :], tiles(t), self.mv[s][:, t, 0:1], self.ri[s][:, 2, t:t + 1],
                              ALU.subtract, ALU.mult).then_inc(self.xn_ready, 1)


def ffn_prepare(nc, name, con, X, x_in, gate, table, XTH, XTL, LG):
    with ExitStack() as ctx:
        m = Memory(nc, ctx, name)
        nm = Norm(m)
        XN = [m.sb(f"xn{s}", [P, TPB, D]) for s in range(2)]
        GR = m.sb("gate_raw", [P, DC, E])
        G = [m.sb(f"gate_part{s}", [P, DC, P], F32R) for s in range(2)]
        LS = [m.sb(f"logits_t{s}", [P, BLK]) for s in range(2)]
        TP = [[m.ps(f"tp{s}{c}") for c in range(DC)] for s in range(2)]
        LP = [m.ps(f"lp{s}") for s in range(2)]
        TL = [m.ps(f"tl{s}") for s in range(2)]
        x_loaded = [m.sem(f"x_loaded{s}") for s in range(2)]
        gate_loaded, gate_split = m.sem("gate_loaded"), m.sem("gate_split")
        xn_ready = nm.xn_ready
        xn_stored = [m.sem(f"xn_stored{s}") for s in range(2)]
        xt_ready, hi_ready, lo_ready = m.sem("xt_ready"), m.sem("hi_ready"), m.sem("lo_ready")
        lt_ready, ls_ready, tl_ready, lg_ready = (m.sem("lt_ready"), m.sem("ls_ready"),
                                                  m.sem("tl_ready"), m.sem("lg_ready"))
        block = ctx.enter_context(m.run())
        tab = table.rearrange("(t p) c -> p t c", p=P)
        half = NB // 2

        @block.sync
        def _(sp):
            sp.dma_start(GR[:], gate).then_inc(gate_loaded, 16)

            def body(i):
                for s in range(2):
                    b = 2 * i + s
                    at_least(sp, x_loaded[s], 16 * i)
                    sp.dma_start(X[:, bass.ds(b * TPB, TPB), :],
                                 x_in.rearrange("(t p) c -> p t c", p=P)[:, bass.ds(b * TPB, TPB), :]
                                 ).then_inc(x_loaded[s], 16)

            def store(i):
                for s in range(2):
                    b = 2 * i + s
                    sp.wait_ge(xn_ready, TPB * (b + 1))
                    sp.dma_start(tab[:, bass.ds(b * TPB, TPB), 0:D], XN[s][:]).then_inc(xn_stored[s], 16)

            loop(sp, half, body)
            loop(sp, half, store)
            for s in range(2):
                sp.wait_ge(xn_stored[s], 16 * half)

        @block.vector
        def _(dve):
            gc = Chain(dve, gate_split)
            gc.step(dve.memset(G[0][:].bitcast(F32), 0.0))
            gc.step(dve.memset(G[1][:].bitcast(F32), 0.0))
            dve.wait_ge(gate_loaded, 16)
            gc.step(dve.tensor_copy(G[0][:, :, 0:E], GR[:]))
            gc.step(dve.tensor_tensor(G[1][:, :, 0:E], GR[:], G[0][:, :, 0:E].bitcast(F32), ALU.subtract))
            def stats(i, s):
                b = 2 * i + s
                dve.wait_ge(x_loaded[s], 16 * (i + 1))
                nm.statistics(dve, b, s, lambda t: X[:, b * TPB + t, :])

            def norm(i, s):
                b = 2 * i + s
                nm.scale(dve, b, s)
                at_least(dve, xn_stored[s], 16 * i)
                at_least(dve, xt_ready, b - 1)
                nm.apply(dve, b, s, XN[s], lambda t: X[:, b * TPB + t, :])

            def low(i, s):
                b = 2 * i + s
                dve.wait_ge(hi_ready, DC * (b + 1))
                for c in range(DC):
                    dve.tensor_tensor(XTL[:, c, bass.ds(b * BLK, BLK)], TP[s][c][:],
                                      XTH[:, c, bass.ds(b * BLK, BLK)].bitcast(F32),
                                      ALU.subtract).then_inc(lo_ready, 1)

            def logits(i, s):
                b = 2 * i + s
                dve.wait_ge(tl_ready, b + 1)
                dve.tensor_copy(LG[:, bass.ds(b * TPB, TPB), :],
                                TL[s][:].rearrange("p (t e) -> p t e", e=P)[:, :, 0:E]).then_inc(lg_ready, 1)

            def body(i, last):
                for s in range(2):
                    if not (last and s):
                        stats(*((i, 1) if s == 0 else (i + 1, 0)))
                    low(i, s)
                    if not (last and s):
                        norm(*((i, 1) if s == 0 else (i + 1, 0)))
                    logits(i, s)

            stats(0, 0)
            norm(0, 0)
            loop_last(dve, half, body)

        @block.scalar
        def _(act):
            def body(i, last):
                for s in range(2):
                    b = 2 * i + s
                    if not (last and s):
                        nm.root(act, b + 1, 1 - s)
                    act.wait_ge(xt_ready, b + 1)
                    for c in range(DC):
                        nc.scalar.activation(XTH[:, c, bass.ds(b * BLK, BLK)], TP[s][c][:],
                                             ACT.Copy).then_inc(hi_ready, 1)
                    act.wait_ge(lt_ready, b + 1)
                    at_least(act, tl_ready, b - 1)
                    nc.scalar.activation(LS[s][:], LP[s][:], ACT.Copy).then_inc(ls_ready, 1)

            nm.root(act, 0, 0)
            loop_last(act, half, body)

        @block.tensor
        def _(pe):
            pe.wait_ge(gate_split, 4)

            def body(i):
                for s in range(2):
                    b = 2 * i + s
                    pe.wait_ge(xn_ready, TPB * (b + 1))
                    at_least(pe, lo_ready, DC * (b - 1))
                    for c in range(DC):
                        for t in range(TPB):
                            last = pe.transpose(TP[s][c][:, t * P:(t + 1) * P], XN[s][:, t, c * P:(c + 1) * P],
                                                con["ident"])
                    last.then_inc(xt_ready, 1)
                    pe.wait_ge(lo_ready, DC * (b + 1))
                    at_least(pe, ls_ready, b - 1)
                    for c in range(DC):
                        last = split3(pe, LP[s][:], [G[k][:, c, :] for k in range(2)],
                                      [x[:, c, bass.ds(b * BLK, BLK)] for x in (XTH, XTL)],
                                      c == 0, c == DC - 1)
                    last.then_inc(lt_ready, 1)
                    pe.wait_ge(ls_ready, b + 1)
                    at_least(pe, lg_ready, b - 1)
                    for t in range(TPB):
                        last = pe.transpose(TL[s][:, t * P:(t + 1) * P], LS[s][:, t * P:(t + 1) * P],
                                            con["ident"])
                    last.then_inc(tl_ready, 1)

            loop(pe, half, body)


def ffn_shared_and_route(nc, name, con, X, acc, shared_w, table, XTH, XTL, LG, SLOT, CODE):
    with ExitStack() as ctx:
        m = Memory(nc, ctx, name)
        WR = m.sb("w_raw", [P, US, UW])
        W = [m.sb(f"w_part{k}", [P, US, UW], F32R) for k in range(2)]
        GEL = [m.sb(f"gelu{s}", [P, BLK]) for s in range(2)]
        HF = [m.sb(f"h{s}", [P, BLK]) for s in range(2)]
        HP = [[m.sb(f"h_part{k}{s}", [P, BLK], F32R) for k in range(2)] for s in range(2)]
        SC = m.sb("scores", [P, E, NT])
        EX = m.sb("exp", [P, NT, E])
        MX = m.sb("max", [P, NT])
        PR = m.sb("probs", [P, NT, E])
        THR, CAND, HIT, BIT, NGT = (m.sb(n, [P, E]) for n in ("thr", "cand", "hit", "bit", "need"))
        CNT = m.sb("count", [P, E])
        MASK = m.sb("mask", [P, E, NT], BF16)
        EQ = m.sb("equal", [P, E, NT], BF16)
        ABOVE = m.sb("above", [P, E, NT], BF16)
        INC, RANK, COL, FIT = (m.sb(n, [P, E, NT]) for n in ("incl", "rank", "column", "fit"))
        GP = [m.ps(f"g{s}") for s in range(2)]
        UP = [m.ps(f"u{s}") for s in range(2)]
        OP = [m.ps(f"o{s}") for s in range(2)]
        CP = m.ps("count_ps")
        WP = m.ps("within_ps")
        w_loaded, w_hi, w_lo = m.sem("w_loaded"), m.sem("w_hi"), m.sem("w_lo")
        g_ready, u_ready, gelu_done, h_chain, h_ready = (m.sem("g_ready"), m.sem("u_ready"),
                                                         m.sem("gelu_done"), m.sem("h_chain"), m.sem("h_ready"))
        h_used, x_ready, stored = m.sem("h_used"), m.sem("x_ready"), m.sem("stored")
        soft, ex_ready, mask_ready, count_ready, route = (m.sem("soft"), m.sem("ex_ready"), m.sem("mask_ready"),
                                                          m.sem("count_ready"), m.sem("route"))
        sc_stored, ranks, bis, hf_ready, pick = (m.sem("sc_stored"), m.sem("ranks"), m.sem("bis"),
                                              m.sem("hf_ready"), m.sem("pick"))
        block = ctx.enter_context(m.run())
        acc_v = acc.rearrange("(t p) c -> p t c", p=P)

        @block.sync
        def _(sp):
            sp.dma_start(WR[:], shared_w.rearrange("u p w -> p u w")).then_inc(w_loaded, 16)
            sp.wait_ge(soft, 5)
            with nc.allow_non_contiguous_dma(reason="64 bytes of scores a row"):
                sp.dma_start(table.rearrange("(t p) c -> p t c", p=P)[:, :, D:ROW], PR[:]).then_inc(sc_stored, 16)

            for b in range(NB):
                sp.wait_ge(x_ready, 2 * (b + 1))
                sp.dma_start(acc_v[:, b * TPB:(b + 1) * TPB, :], X[:, b * TPB:(b + 1) * TPB, :]).then_inc(stored, 16)
            sp.wait_ge(stored, 16 * NB)
            sp.wait_ge(sc_stored, 16)

        @block.gpsimd
        def _(pool):
            for u in range(US):
                pool.wait_ge(w_hi, u + 1)
                pool.tensor_tensor(W[1][:, u, :], WR[:, u, :], W[0][:, u, :].bitcast(F32),
                                   ALU.subtract).then_inc(w_lo, 1)

        @block.scalar
        def _(act):
            act.wait_ge(w_loaded, 16)
            for u in range(US):
                nc.scalar.activation(W[0][:, u, :], WR[:, u, :], ACT.Copy).then_inc(w_hi, 1)
            act.wait_ge(soft, 2)
            nc.scalar.activation(EX[:].rearrange("p t e -> p (t e)"), PR[:].rearrange("p t e -> p (t e)"),
                                 ACT.Exp).then_inc(ex_ready, 1)

            def body(b):
                for u in range(US):
                    n = b * US + u
                    act.wait_ge(g_ready, n + 1)
                    at_least(act, hf_ready, n - 1)
                    nc.scalar.activation(GEL[u % 2][:], GP[u % 2][:], ACT.Gelu).then_inc(gelu_done, 1)

            loop(act, NB, body)

        @block.tensor
        def _(pe):
            def down(n, u, last):
                pe.wait_ge(h_ready, n + 1)
                for t in range(TPB):
                    o = OP[t // 2][:, (t % 2) * D:(t % 2 + 1) * D]
                    ins = split3(pe, o, [HP[u % 2][k][:, t * P:(t + 1) * P] for k in range(2)],
                                 [W[k][:, u, 2 * D:UW] for k in range(2)], u == 0 and t % 2 == 0,
                                 u == US - 1 and t % 2 == 1)
                ins.then_inc(h_used, 1)

            def up(b, u, n):
                pe.wait_ge(w_lo, u + 1)
                at_least(pe, gelu_done, n - 1)
                for g, bank, ready in ((0, GP, g_ready), (1, UP, u_ready)):
                    if g:
                        at_least(pe, hf_ready, n - 1)
                    for c in range(DC):
                        ins = split3(pe, bank[u % 2][:],
                                     [W[k][:, u, g * D + c * P:g * D + (c + 1) * P] for k in range(2)],
                                     [x[:, c, bass.ds(b * BLK, BLK)] for x in (XTH, XTL)], c == 0, c == DC - 1)
                    ins.then_inc(ready, 1)

            def count(n):
                pe.wait_ge(mask_ready, n + 1)
                pe.matmul(CP[:], con["ones"], MASK[:].rearrange("p e t -> p (e t)"), start=True,
                          stop=True).then_inc(count_ready, 1)

            def body(b):
                for u in range(US):
                    n = b * US + u
                    up(b, u, n)
                    if u:
                        if u == 1:
                            at_least(pe, x_ready, 2 * b)
                        down(n - 1, u - 1, False)
                    elif not first(b):
                        down(n - 1, US - 1, False)
                    count(n)

            loop(pe, NB, body)
            down(NB * US - 1, US - 1, True)
            for r in range(3):
                pe.wait_ge(ranks, r + 1)
                flat = (MASK, EQ, MASK)[r][:].rearrange("p e t -> p (e t)")
                pe.matmul(WP[:], con["before"], flat, start=True, stop=True)
                pe.matmul(CP[:], con["ones"], flat, start=True, stop=True).then_inc(route, 1)

        @block.vector
        def _(dve):
            sc = Chain(dve, soft)
            lg = LG[:]
            sc.step(dve.tensor_reduce(MX[:], lg, AX_X, ALU.max))
            sc.step(dve.tensor_tensor(PR[:], lg, MX[:].unsqueeze(2).broadcast_to([P, NT, E]), ALU.subtract))
            dve.wait_ge(ex_ready, 1)
            sc.step(dve.tensor_reduce(MX[:], EX[:], AX_X, ALU.add))
            sc.step(dve.reciprocal(MX[:], MX[:]))
            sc.step(dve.tensor_tensor(PR[:], EX[:], MX[:].unsqueeze(2).broadcast_to([P, NT, E]), ALU.mult))
            sc.step(dve.tensor_copy(SC[:].rearrange("p e t -> p t e"), PR[:]))
            sc.step(dve.memset(THR[:], 0.0))
            sc.step(dve.tensor_copy(BIT[:].bitcast(U32), con["top_bit"].broadcast_to([P, E])))
            sc.step(dve.tensor_copy(CAND[:].bitcast(U32), con["top_bit"].broadcast_to([P, E])))

            def compare(n):
                dve.tensor_tensor(MASK[:], SC[:], CAND[:].unsqueeze(2).broadcast_to([P, E, NT]),
                                  ALU.is_ge).then_inc(mask_ready, 1)

            def update(n):
                ch = Chain(dve, bis, 5 * n)
                dve.wait_ge(count_ready, n + 1)
                ch.step(dve.tensor_reduce(CNT[:], CP[:].rearrange("p (e t) -> p e t", t=NT), AX_X, ALU.add))
                ch.step(dve.scalar_tensor_tensor(HIT[:], CNT[:], CAP - 0.5, CAND[:], ALU.is_ge, ALU.mult))
                ch.step(dve.tensor_tensor(THR[:], THR[:], HIT[:], ALU.max))
                ch.step(dve.tensor_single_scalar(BIT[:].bitcast(U32), BIT[:].bitcast(U32), 1,
                                                 ALU.logical_shift_right))
                ch.step(dve.tensor_tensor(CAND[:].bitcast(U32), THR[:].bitcast(U32), BIT[:].bitcast(U32),
                                          ALU.bitwise_or))

            def hidden(n, u):
                s = u % 2
                ch = Chain(dve, h_chain, n)
                dve.wait_ge(gelu_done, n + 1)
                dve.wait_ge(u_ready, n + 1)
                dve.tensor_tensor(HF[s][:], GEL[s][:], UP[s][:], ALU.mult).then_inc(hf_ready, 1)
                dve.wait_ge(hf_ready, n + 1)
                at_least(dve, h_used, n - 1)
                ch.step(dve.tensor_copy(HP[s][0][:], HF[s][:]))
                dve.tensor_tensor(HP[s][1][:], HF[s][:], HP[s][0][:].bitcast(F32), ALU.subtract).then_inc(h_ready, 1)

            def residual(b):
                dve.wait_ge(h_used, US * (b + 1))
                for k in range(2):
                    xs = X[:, bass.ds(b * TPB + 2 * k, 2), :].rearrange("p t c -> p (t c)")
                    dve.scalar_tensor_tensor(xs, OP[k][:], 0.5, xs, ALU.mult, ALU.add).then_inc(x_ready, 1)

            def body(b):
                for u in range(US):
                    n = b * US + u
                    if u or not first(b):
                        update(n - 1)
                    compare(n)
                    if u == 1 and not first(b):
                        residual(b - 1)
                    hidden(n, u)

            loop(dve, NB, body)
            update(ROUNDS - 1)
            residual(NB - 1)
            rc = Chain(dve, pick)
            thr = THR[:].unsqueeze(2).broadcast_to([P, E, NT])
            flat = lambda x: x[:].rearrange("p e t -> p (e t)")
            totals = CP[:].rearrange("p (e t) -> p e t", t=NT)

            def rank_of():
                rc.step(dve.tensor_tensor_scan(flat(INC), con["restart"], CP[:], 0.0, ALU.mult, ALU.add))
                rc.step(dve.tensor_tensor(RANK[:], INC[:], totals, ALU.subtract))
                rc.step(dve.tensor_tensor(flat(RANK), flat(RANK), WP[:], ALU.add))

            rc.step(dve.tensor_tensor(MASK[:], SC[:], thr, ALU.is_gt))
            dve.tensor_copy(ABOVE[:], MASK[:]).then_inc(ranks, 1)
            rc.step(dve.tensor_tensor(EQ[:], SC[:], thr, ALU.is_equal))
            dve.wait_ge(route, 1)
            rc.step(dve.tensor_reduce(CNT[:], totals, AX_X, ALU.add))
            dve.tensor_scalar(NGT[:], CNT[:], -1.0, float(CAP), ALU.mult, ALU.add).then_inc(ranks, 1)
            dve.wait_ge(ranks, 2)
            dve.wait_ge(route, 2)
            rank_of()
            rc.step(dve.tensor_tensor(FIT[:], RANK[:], NGT[:].unsqueeze(2).broadcast_to([P, E, NT]), ALU.is_lt))
            rc.step(dve.tensor_tensor(FIT[:], FIT[:], EQ[:], ALU.mult))
            dve.tensor_tensor(MASK[:], FIT[:], ABOVE[:], ALU.add).then_inc(ranks, 1)
            dve.wait_ge(ranks, 3)
            dve.wait_ge(route, 3)
            rank_of()
            rc.step(dve.tensor_scalar(COL[:], RANK[:], float(P), None, ALU.is_ge))
            for k in range(2, TPB):
                rc.step(dve.scalar_tensor_tensor(COL[:], RANK[:], float(k * P), COL[:], ALU.is_ge, ALU.add))
            rc.step(dve.scalar_tensor_tensor(RANK[:], COL[:], -float(P), RANK[:], ALU.mult, ALU.add))
            rc.step(dve.scalar_tensor_tensor(RANK[:], RANK[:], 1.0, MASK[:], ALU.add, ALU.mult))
            rc.step(dve.tensor_scalar(SLOT[:], RANK[:], 1.0, None, ALU.subtract))
            for k in range(TPB):
                dve.tensor_scalar(CODE[:, :, :, k, 0], COL[:], float(k), con["row"], ALU.is_equal, ALU.mult)
                dve.scalar_tensor_tensor(CODE[:, :, :, k, 1], COL[:], float(k),
                                         con["tile"].rearrange("p (e t) -> p e t", t=NT), ALU.is_equal, ALU.mult)


def ffn_experts(nc, name, con, acc, expert_w, table, SLOT, CODE):
    with ExitStack() as ctx:
        m = Memory(nc, ctx, name)
        WR = m.sb("w_raw", [P, RAW, UW])
        W = [m.sb(f"w_part{k}", [P, UE, UW], F32R) for k in range(2)]
        GEL = [m.sb(f"gelu{s}", [P, BLK]) for s in range(2)]
        HF = [m.sb(f"h{s}", [P, BLK]) for s in range(2)]
        HP = [[m.sb(f"h_part{k}{s}", [P, BLK], F32R) for k in range(2)] for s in range(2)]
        ONEHOT = m.sb("onehot", [P, NT, P], BF16)
        FOUND = m.sb("found", [P, TPB, 2])
        IDX = [m.sb(f"index{s}", [P, TPB], U32) for s in range(2)]
        XG = [m.sb(f"gathered{s}", [P, TPB, ROW]) for s in range(2)]
        XT = [[m.sb(f"xt_part{k}{s}", [P, DC, BLK], F32R) for k in range(2)] for s in range(2)]
        WT = [m.sb(f"weight{s}", [P, TPB]) for s in range(2)]
        EO = [m.sb(f"out{s}", [P, TPB, D]) for s in range(2)]
        GP = [m.ps(f"g{s}") for s in range(2)]
        UP = [m.ps(f"u{s}") for s in range(2)]
        OP = [m.ps(f"o{s}") for s in range(2)]
        TP = [m.ps(f"t{c}") for c in range(DC)]
        raw_loaded = [m.sem(f"raw_loaded{r}") for r in range(RAW)]
        w_hi, w_lo = m.sem("w_hi"), m.sem("w_lo")
        g_ready, u_ready, gelu_done, hf_ready, h_chain, h_ready, h_used = (
            m.sem(n) for n in ("g_ready", "u_ready", "gelu_done", "hf_ready", "h_chain", "h_ready", "h_used"))
        oh_ready, found_ready, found_read, idx_ready = (
            m.sem(n) for n in ("oh_ready", "found_ready", "found_read", "idx_ready"))
        gathered = [m.sem(f"gathered{s}") for s in range(2)]
        xt_ready, xhi_ready, xlo_ready, wt_ready = (
            m.sem(n) for n in ("xt_ready", "xhi_ready", "xlo_ready", "wt_ready"))
        eo_ready, scattered, note = m.sem("eo_ready"), m.sem("scattered"), m.sem("note")
        block = ctx.enter_context(m.run())
        half = E // 2
        PIECE = 8
        PIECES = NT // PIECE

        @block.sync
        def _(sp):
            def body(e):
                for u in range(UE):
                    n = e * UE + u
                    at_least(sp, w_lo, n - RAW + 1)
                    sp.dma_start(WR[:, u % RAW, :], expert_w[bass.ds(n, 1), :, :].rearrange("a p w -> p (a w)")
                                 ).then_inc(raw_loaded[u % RAW], 16)

            loop(sp, E, body)

        @block.gpsimd
        def _(pool):
            def low(n, u):
                pool.wait_ge(w_hi, n + 1)
                pool.tensor_tensor(W[1][:, u, :], WR[:, u % RAW, :], W[0][:, u, :].bitcast(F32),
                                   ALU.subtract).then_inc(w_lo, 1)

            def gather(x, q):
                pool.wait_ge(idx_ready, x + 1)
                at_least(pool, wt_ready, x - 1)
                at_least(pool, xt_ready, x - 1)
                pool.sem_inc(note, 1)
                for t in range(TPB):
                    pool.indirect_dma_start(XG[q][:, t, :], None, table,
                                            bass.IndirectOffsetOnAxis(IDX[q][:, t:t + 1], 0)
                                            ).then_inc(gathered[q], 16)

            def scatter(x, q):
                pool.wait_ge(eo_ready, TPB * (x + 1))
                at_least(pool, scattered, 16 * TPB * x)
                pool.sem_inc(note, 1)
                for t in range(TPB):
                    pool.indirect_dma_start(acc, bass.IndirectOffsetOnAxis(IDX[q][:, t:t + 1], 0),
                                            EO[q][:, t, :], None, compute_op=ALU.add).then_inc(scattered, 16)

            def body(i, last):
                for q in range(2):
                    e = 2 * i + q
                    final = last and q == 1
                    for u in range(UE):
                        if not (final and u + AHEAD >= UE):
                            low(e * UE + u + AHEAD, (u + AHEAD) % UE)
                        if u == 1 and (q or not first(i)):
                            scatter(e - 1, 1 - q)
                        if u == 4 and not final:
                            gather(e + 1, 1 - q)

            low(0, 0)
            gather(0, 0)
            for u in range(1, AHEAD):
                low(u, u)
            loop_last(pool, half, body)
            scatter(E - 1, 1)
            pool.wait_ge(scattered, 16 * TPB * E)

        @block.scalar
        def _(act):
            def gelu(n, u):
                act.wait_ge(g_ready, n + 1)
                at_least(act, hf_ready, n - 1)
                nc.scalar.activation(GEL[u % 2][:], GP[u % 2][:], ACT.Gelu).then_inc(gelu_done, 1)

            def high(n, e, u):
                act.wait_ge(raw_loaded[u % RAW], 16 * (e * (UE // RAW) + u // RAW + 1))
                at_least(act, h_used, n - UE + 1)
                nc.scalar.activation(W[0][:, u, :], WR[:, u % RAW, :], ACT.Copy).then_inc(w_hi, 1)

            def x_high(x, q):
                act.wait_ge(xt_ready, x + 1)
                for c in range(DC):
                    nc.scalar.activation(XT[q][0][:, c, :], TP[c][:], ACT.Copy).then_inc(xhi_ready, 1)

            def weigh(x, q):
                act.wait_ge(h_used, UE * (x + 1))
                act.wait_ge(wt_ready, x + 1)
                at_least(act, scattered, 16 * TPB * (x - 1))
                for t in range(TPB):
                    nc.scalar.activation(EO[q][:, t, :], OP[t // 2][:, (t % 2) * D:(t % 2 + 1) * D], ACT.Copy,
                                         scale=WT[q][:, t:t + 1]).then_inc(eo_ready, 1)

            def body(i, last):
                for q in range(2):
                    e = 2 * i + q
                    final = last and q == 1
                    for u in range(UE):
                        n = e * UE + u
                        if u == UE - 1 and not final:
                            x_high(e + 1, 1 - q)
                        gelu(n, u)
                        if u == 0 and (q or not first(i)):
                            weigh(e - 1, 1 - q)
                        if not (final and u + AHEAD >= UE):
                            a = u + AHEAD
                            high(n + AHEAD, e + a // UE, a % UE)

            for u in range(AHEAD):
                high(u, 0, u)
            x_high(0, 0)
            loop_last(act, half, body)
            weigh(E - 1, 1)

        @block.vector
        def _(dve):
            def onehot(x, k):
                at_least(dve, found_ready, x)
                sl = slice(k * PIECE, (k + 1) * PIECE)
                dve.tensor_tensor(ONEHOT[:, sl, :], con["slots"].unsqueeze(1).broadcast_to([P, PIECE, P]),
                                  SLOT[:, bass.ds(x, 1), sl].rearrange("p a t -> p (a t)").unsqueeze(2)
                                  .broadcast_to([P, PIECE, P]), ALU.is_equal).then_inc(oh_ready, 1)

            def index(x, q):
                dve.wait_ge(found_ready, x + 1)
                dve.tensor_copy(FOUND[:].rearrange("p t v -> p (t v)"), TP[0][:, 0:2 * TPB]).then_inc(found_read, 1)
                dve.wait_ge(found_read, x + 1)
                at_least(dve, scattered, 16 * TPB * (x - 1))
                dve.scalar_tensor_tensor(IDX[q][:], FOUND[:, :, 1], float(P), FOUND[:, :, 0], ALU.mult,
                                         ALU.add).then_inc(idx_ready, 1)

            def x_low(x, q, k):
                dve.wait_ge(gathered[q], 16 * TPB * (k + 1))
                dve.tensor_scalar(WT[q][:], XG[q][:, :, bass.ds(x + D, 1)].rearrange("p t a -> p (t a)"), 0.5, None,
                                  ALU.mult).then_inc(wt_ready, 1)
                dve.wait_ge(xhi_ready, DC * (x + 1))
                for c in range(DC):
                    dve.tensor_tensor(XT[q][1][:, c, :], TP[c][:], XT[q][0][:, c, :].bitcast(F32),
                                      ALU.subtract).then_inc(xlo_ready, 1)

            def hidden(n, u):
                s = u % 2
                dve.wait_ge(gelu_done, n + 1)
                dve.wait_ge(u_ready, n + 1)
                dve.tensor_tensor(HF[s][:], GEL[s][:], UP[s][:], ALU.mult).then_inc(hf_ready, 1)
                dve.wait_ge(hf_ready, n + 1)
                at_least(dve, h_used, n - 1)
                dve.tensor_copy(HP[s][0][:], HF[s][:]).then_inc(h_chain, 1)
                dve.wait_ge(h_chain, n + 1)
                dve.tensor_tensor(HP[s][1][:], HF[s][:], HP[s][0][:].bitcast(F32), ALU.subtract).then_inc(h_ready, 1)

            def body(i, last):
                for q in range(2):
                    e = 2 * i + q
                    final = last and q == 1
                    for u in range(UE):
                        if u == UE - 1 and not final:
                            x_low(e + 1, 1 - q, i + q)
                        if u < PIECES // 2 and not final:
                            onehot(e + 1, 2 * u)
                            onehot(e + 1, 2 * u + 1)
                        if u == 4 and not final:
                            index(e + 1, 1 - q)
                        hidden(e * UE + u, u)

            for k in range(PIECES):
                onehot(0, k)
            index(0, 0)
            x_low(0, 0, 0)
            loop_last(dve, half, body)

        @block.tensor
        def _(pe):
            def find(x):
                at_least(pe, xlo_ready, DC * x)
                pe.wait_ge(oh_ready, PIECES * (x + 1))
                for t in range(NT):
                    ins = pe.matmul(TP[0][:, 0:2 * TPB], ONEHOT[:, t, :],
                                    CODE[:, bass.ds(x, 1), t, :, :].rearrange("p a k v -> p (a k v)"),
                                    start=t == 0, stop=t == NT - 1)
                ins.then_inc(found_ready, 1)

            def transposes(x, q, k):
                pe.wait_ge(gathered[q], 16 * TPB * (k + 1))
                pe.wait_ge(found_read, x + 1)
                for c in range(DC):
                    for t in range(TPB):
                        ins = pe.transpose(TP[c][:, t * P:(t + 1) * P], XG[q][:, t, c * P:(c + 1) * P], con["ident"])
                ins.then_inc(xt_ready, 1)

            def up(n, u, q):
                pe.wait_ge(w_lo, n + 1)
                at_least(pe, gelu_done, n - 1)
                for g, bank, ready in ((0, GP, g_ready), (1, UP, u_ready)):
                    if g:
                        at_least(pe, hf_ready, n - 1)
                    for c in range(DC):
                        ins = split3(pe, bank[u % 2][:],
                                     [W[k][:, u, g * D + c * P:g * D + (c + 1) * P] for k in range(2)],
                                     [XT[q][k][:, c, :] for k in range(2)], c == 0, c == DC - 1)
                    ins.then_inc(ready, 1)

            def down(n, u):
                pe.wait_ge(h_ready, n + 1)
                for t in range(TPB):
                    ins = split3(pe, OP[t // 2][:, (t % 2) * D:(t % 2 + 1) * D],
                                 [HP[u % 2][k][:, t * P:(t + 1) * P] for k in range(2)],
                                 [W[k][:, u, 2 * D:UW] for k in range(2)], u == 0 and t % 2 == 0,
                                 u == UE - 1 and t % 2 == 1)
                ins.then_inc(h_used, 1)

            def body(i, last):
                for q in range(2):
                    e = 2 * i + q
                    final = last and q == 1
                    for u in range(UE):
                        n = e * UE + u
                        if u == 0:
                            pe.wait_ge(xlo_ready, DC * (e + 1))
                        up(n, u, q)
                        if u == 1:
                            at_least(pe, eo_ready, TPB * e)
                        if u or q or not first(i):
                            down(n - 1, (u - 1) % UE)
                        if u == 3 and not final:
                            find(e + 1)
                        if u == 6 and not final:
                            transposes(e + 1, 1 - q, i + q)

            find(0)
            transposes(0, 0, 0)
            loop_last(pe, half, body)
            down(E * UE - 1, UE - 1)


def ffn(nc, name, con, x_in, acc, gate, shared_w, expert_w, table):
    with ExitStack() as outer:
        m = Memory(nc, outer, name)
        SLOT = m.sb("slot", [P, E, NT], BF16)
        CODE = m.sb("code", [P, E, NT, TPB, 2], BF16)
        with ExitStack() as ctx:
            m = Memory(nc, ctx, name)
            X = m.sb("x", [P, NT, D])
            XTH = m.sb("xth", [P, DC, TOK], F32R)
            XTL = m.sb("xtl", [P, DC, TOK], F32R)
            LG = m.sb("logits", [P, NT, E])
            ffn_prepare(nc, name + "p_", con, X, x_in, gate, table, XTH, XTL, LG)
            ffn_shared_and_route(nc, name + "s_", con, X, acc, shared_w, table, XTH, XTL, LG, SLOT, CODE)
        ffn_experts(nc, name + "e_", con, acc, expert_w, table, SLOT, CODE)


USE_PROBS, USE_INTER, USE_HEADS, USE_OUT, PIECES = (0, 4, 5, 8), 1, 2, 7, (3, 6, 9, 10)


def turn_bank(use):
    return use % 4


def attention(nc, name, con, x_in, out, w_in, bias_in, row_bias_in):
    with ExitStack() as ctx:
        m = Memory(nc, ctx, name)
        nm = Norm(m)
        WR = m.sb("w_raw", [P, 4, DC, D])
        W = [m.sb(f"w_part{k}", [P, 4, DC, D], F32R) for k in range(2)]
        BC = m.sb("bias_col", [P, 2, DC])
        KF = m.sb("k", [P, DC, BLK])
        BR = m.sb("bias_row", [P, 2, D])
        X = [m.sb(f"x{s}", [P, TPB, D]) for s in range(2)]
        XB = [m.sb(f"x_plus_bias{s}", [P, TPB, D]) for s in range(2)]
        XN = m.sb("xn", [P, TPB, D])
        XT = [m.sb(f"xt_part{k}", [P, DC, BLK], F32R) for k in range(2)]
        XM = m.sb("x_sum", [P, DC, TPB])
        XA = m.sb("x_means", [P, DC, 4, NC])
        KT = m.sb("k_means", [P, DC, NC])
        KM = [m.sb(f"k_means_by_head{s}", [P, DC, GH, NC]) for s in range(2)]
        VB = m.sb("v_means_all", [P, D])
        VM = [m.sb(f"v_means_by_head{s}", [P, H, HD + 1]) for s in range(2)]
        Q = [m.sb(f"q{s}", [P, DC, BLK]) for s in range(2)]
        KE = [[m.sb(f"k_parity{k}{s}", [P, DC, BLK]) for k in range(2)] for s in range(2)]
        V = [m.sb(f"v{s}", [P, TPB, H, HD + 1]) for s in range(2)]
        MX = m.sb("max", [P, 4, 4])
        PB = m.sb("probs", [P, 4, 4, P])
        PT = [m.sb(f"probs_t{s}", [P, BLK]) for s in range(2)]
        SI = m.sb("inter", [P, H, NC])
        AI = m.sb("inter_probs", [P, H, NC])
        IM, IR, RS = (m.sb(n, [P, H]) for n in ("inter_max", "inter_recip", "recip"))
        AT = m.sb("inter_t", [P, BLK])
        O2 = m.sb("inter_heads", [P, H, HD])
        O = m.sb("heads", [P, H, HD])
        OT = [m.sb(f"heads_t{k}", [P, DC, P], F32R) for k in range(2)]
        Y = [m.sb(f"y{s}", [P, TPB, D]) for s in range(2)]
        S = [m.ps(f"scores{i}") for i in range(2)]
        TB = [m.ps(f"turn{i}") for i in range(4)]
        IB, OB = m.ps("inter_ps"), m.ps("heads_ps")
        names = ("w_loaded", "w_hi", "w_lo", "clear", "xt_mm", "x_hi", "x_lo", "x_sums", "x_means", "q_mm",
                 "k_mm", "v_mm", "km_mm", "vm_mm", "q_ready", "kf_ready", "ke_ready", "v_ready", "kt_ready", "km_ready",
                 "vb_ready", "vm_ready", "xb_ready", "s_mm", "max_ready", "sub_ready", "exp_ready", "pt_mm", "pt_ready",
                 "pv_mm", "i_mm", "si_ready", "im_ready", "isub_ready", "iexp_ready", "at_mm", "at_ready", "oi_mm",
                 "ir_ready", "o2_ready", "o_chain", "heads_ready", "ot_mm", "ot_hi", "ot_lo", "y_mm", "y_ready")
        sem = {n: m.sem(n) for n in names}
        x_loaded = [m.sem(f"x_loaded{s}") for s in range(2)]
        stored = [m.sem(f"stored{s}") for s in range(2)]
        block = ctx.enter_context(m.run())
        half = NB // 2
        x_v = x_in.rearrange("(t p) c -> p t c", p=P)
        out_v = out.rearrange("(t p) c -> p t c", p=P)

        @block.sync
        def _(sp):
            sp.dma_start(X[0][:], x_v[:, 0:TPB, :]).then_inc(x_loaded[0], 16)
            sp.dma_start(WR[:], w_in).then_inc(sem["w_loaded"], 16)
            sp.dma_start(BC[:], bias_in).then_inc(sem["w_loaded"], 16)
            sp.dma_start(BR[:], row_bias_in).then_inc(sem["w_loaded"], 16)
            for b in range(1, NB + 2):
                if b < NB:
                    at_least(sp, nm.xn_ready, TPB * (b - 1))
                    at_least(sp, sem["xb_ready"], b - 1)
                    sp.dma_start(X[b % 2][:], x_v[:, b * TPB:(b + 1) * TPB, :]).then_inc(x_loaded[b % 2], 16)
                if b > 1:
                    sp.wait_ge(sem["y_ready"], TPB * (b - 1))
                    sp.dma_start(out_v[:, (b - 2) * TPB:(b - 1) * TPB, :], Y[b % 2][:]).then_inc(stored[b % 2], 16)
            for s in range(2):
                sp.wait_ge(stored[s], 16 * half)

        @block.gpsimd
        def _(pool):
            pool.memset(XA[:], 0.0).then_inc(sem["clear"], 1)
            for s in range(2):
                pool.memset(V[s][:], 1.0).then_inc(sem["clear"], 1)
            pool.wait_ge(sem["w_hi"], 4)
            for k in range(4):
                pool.tensor_tensor(W[1][:, k], WR[:, k], W[0][:, k].bitcast(F32), ALU.subtract).then_inc(sem["w_lo"], 1)
            for s in range(2):
                pool.tensor_copy(VM[s][:, :, HD:HD + 1],
                                 con["own_rows"].rearrange("p (h d) -> p h d", d=HD)[:, :, 0:1]).then_inc(sem["clear"], 1)

            def residual(i, b, s):
                pool.wait_ge(x_loaded[s], 16 * (i + 1))
                at_least(pool, sem["y_ready"], TPB * (b - 1))
                pool.tensor_tensor(XB[s][:], X[s][:], BR[:, 1, :].unsqueeze(1).broadcast_to([P, TPB, D]),
                                   ALU.add).then_inc(sem["xb_ready"], 1)

            def keys(b, s):
                at_least(pool, sem["s_mm"], 4 * TPB * (b - 1))
                for g in range(DC):
                    pool.wait_ge(sem["kf_ready"], DC * b + g + 1)
                    for k in range(2):
                        pool.tensor_tensor(KE[s][k][:, g, :], KF[:, g, :], con["parity"][:, k:k + 1].broadcast_to([P, BLK]),
                                           ALU.mult).then_inc(sem["ke_ready"], 1)

            def means(b, s):
                pool.wait_ge(sem["kt_ready"], DC * (b + 1))
                at_least(pool, sem["i_mm"], TPB * (b - 1))
                for g in range(DC):
                    pool.tensor_tensor(KM[s][:, g], KT[:, g, :].unsqueeze(1).broadcast_to([P, GH, NC]),
                                       con["own_head"].unsqueeze(2).broadcast_to([P, GH, NC]),
                                       ALU.mult).then_inc(sem["km_ready"], 1)
                pool.wait_ge(sem["vb_ready"], b + 1)
                at_least(pool, sem["oi_mm"], TPB * (b - 1))
                pool.tensor_tensor(VM[s][:, :, 0:HD], VB[:].rearrange("p (h d) -> p h d", d=HD),
                                   con["own_rows"].rearrange("p (h d) -> p h d", d=HD), ALU.mult).then_inc(sem["vm_ready"], 1)

            def inter(n):
                pool.wait_ge(sem["im_ready"], n + 1)
                pool.tensor_tensor(SI[:], SI[:], IM[:].unsqueeze(2).broadcast_to([P, H, NC]),
                                   ALU.subtract).then_inc(sem["isub_ready"], 1)

            def body(i, last):
                for s in range(2):
                    b = 2 * i + s
                    final = last and s == 1
                    for j in range(TPB):
                        if not (final and j == TPB - 1):
                            inter(b * TPB + j + 1)
                        if not final:
                            if j == 0:
                                residual(i + s, b + 1, 1 - s)
                            if j == 1:
                                means(b + 1, 1 - s)
                            if j == 2:
                                keys(b + 1, 1 - s)

            pool.wait_ge(sem["w_loaded"], 48)
            residual(0, 0, 0)
            means(0, 0)
            keys(0, 0)
            inter(0)
            loop_last(pool, half, body)

        @block.scalar
        def _(act):
            act.wait_ge(sem["w_loaded"], 48)
            for k in range(4):
                nc.scalar.activation(W[0][:, k], WR[:, k], ACT.Copy).then_inc(sem["w_hi"], 1)

            def copy(out, in_, done):
                nc.scalar.activation(out, in_, ACT.Copy).then_inc(sem[done], 1)

            def x_high(b, c):
                act.wait_ge(sem["xt_mm"], DC * b + c + 1)
                copy(XT[0][:, c, :], TB[turn_bank(PIECES[2 + c])][:], "x_hi")

            def queries(b, s, g):
                act.wait_ge(sem["q_mm"], DC * b + g + 1)
                nc.scalar.activation(Q[s][:, g, :], TB[turn_bank(PIECES[g])][:], ACT.Identity,
                                     bias=BC[:, 0, g:g + 1]).then_inc(sem["q_ready"], 1)

            def keys(b, g):
                act.wait_ge(sem["k_mm"], DC * b + g + 1)
                at_least(act, sem["ke_ready"], 2 * DC * b)
                nc.scalar.activation(KF[:, g, :], TB[turn_bank(PIECES[g])][:], ACT.Identity,
                                     bias=BC[:, 1, g:g + 1]).then_inc(sem["kf_ready"], 1)

            def probs(n, i):
                act.wait_ge(sem["sub_ready"], 4 * n + i + 1)
                nc.scalar.activation(PB[:, i], PB[:, i], ACT.Exp, scale=SCALE).then_inc(sem["exp_ready"], 1)

            def inter(n):
                act.wait_ge(sem["isub_ready"], n + 1)
                at_least(act, sem["at_mm"], n)
                nc.scalar.activation(AI[:], SI[:], ACT.Exp, scale=SCALE).then_inc(sem["iexp_ready"], 1)

            def evacuate(n, i):
                act.wait_ge(sem["pt_mm"], 4 * n + i + 1)
                at_least(act, sem["pv_mm"], 4 * n + i - 1)
                copy(PT[i % 2][:], TB[turn_bank(USE_PROBS[i])][:], "pt_ready")

            def heads_high(n):
                act.wait_ge(sem["ot_mm"], n + 1)
                at_least(act, sem["y_mm"], n)
                copy(OT[0][:].rearrange("p c t -> p (c t)"), TB[turn_bank(USE_HEADS)][:, 0:D], "ot_hi")

            def chunk(n, j, s, b, final, start):
                nxt = not (final and j == TPB - 1)

                def piece(k):
                    if final:
                        return
                    if j == 0 and k >= 2:
                        x_high(b + 1, k - 2)
                    if j == 1 and k < 2:
                        queries(b + 1, 1 - s, k)
                    if j == 2 and k < 2:
                        keys(b + 1, k)

                evacuate(n, 0)
                act.wait_ge(sem["at_mm"], n + 1)
                at_least(act, sem["oi_mm"], n)
                copy(AT[:], TB[turn_bank(USE_INTER)][:], "at_ready")
                if not start:
                    heads_high(n - 1)
                piece(0)
                evacuate(n, 1)
                if j == 0 and not final:
                    nm.root(act, b + 1, 1 - s)
                evacuate(n, 2)
                if nxt:
                    probs(n + 1, 0)
                piece(1)
                evacuate(n, 3)
                if nxt:
                    probs(n + 1, 1)
                    inter(n + 1)
                    probs(n + 1, 2)
                piece(2)
                if nxt:
                    probs(n + 1, 3)
                piece(3)

            def body(i, last):
                for s in range(2):
                    b = 2 * i + s
                    for j in range(TPB):
                        chunk(b * TPB + j, j, s, b, last and s == 1, first(i) and s == 0 and j == 0)

            nm.root(act, 0, 0)
            for c in range(DC):
                x_high(0, c)
            for g in range(DC):
                queries(0, 0, g)
            for g in range(DC):
                keys(0, g)
            for i in range(4):
                probs(0, i)
            inter(0)
            loop_last(act, half, body)
            heads_high(NC - 1)

        @block.vector
        def _(dve):
            dve.wait_ge(sem["w_loaded"], 48)

            def statistics(i, b, s):
                dve.wait_ge(x_loaded[s], 16 * (i + 1))
                nm.statistics(dve, b, s, lambda t: X[s][:, t, :])

            def norm(b, s):
                nm.scale(dve, b, s)
                nm.apply(dve, b, s, XN, lambda t: X[s][:, t, :])

            def x_low(b, c):
                t = TB[turn_bank(PIECES[2 + c])]
                dve.wait_ge(sem["x_hi"], DC * b + c + 1)
                dve.tensor_reduce(XM[:, c, :], t[:].rearrange("p (t k) -> p t k", k=P), AX_X,
                                  ALU.add).then_inc(sem["x_sums"], 1)
                dve.tensor_tensor(XT[1][:, c, :], t[:], XT[0][:, c, :].bitcast(F32),
                                  ALU.subtract).then_inc(sem["x_lo"], 1)
                dve.wait_ge(sem["x_sums"], DC * b + c + 1)
                if first(b):
                    dve.wait_ge(sem["clear"], 1)
                dve.tensor_scalar(XA[:, c, :, bass.ds(b * TPB, TPB)],
                                  XM[:, c, :].unsqueeze(1).broadcast_to([P, 4, TPB]), 1.0 / P, None,
                                  ALU.mult).then_inc(sem["x_means"], 1)

            def values(b, s, v):
                if first(b):
                    dve.wait_ge(sem["clear"], 3)
                dve.wait_ge(sem["v_mm"], 2 * b + v + 1)
                for t in range(2):
                    dve.tensor_tensor(V[s][:, 2 * v + t, :, 0:HD],
                                      TB[turn_bank(PIECES[2 + v])][:, t * D:(t + 1) * D].rearrange("p (h d) -> p h d", d=HD),
                                      BR[:, 0, :].rearrange("p (h d) -> p h d", d=HD), ALU.add).then_inc(sem["v_ready"], 1)

            def key_means(b):
                dve.wait_ge(sem["km_mm"], b + 1)
                at_least(dve, sem["km_ready"], DC * b)
                for g in range(DC):
                    dve.tensor_scalar(KT[:, g, :], TB[turn_bank(PIECES[2])][:, g * NC:(g + 1) * NC],
                                      BC[:, 1, g:g + 1], None, ALU.add).then_inc(sem["kt_ready"], 1)

            def value_means(b):
                dve.wait_ge(sem["vm_mm"], b + 1)
                at_least(dve, sem["vm_ready"], b)
                dve.tensor_tensor(VB[:], TB[turn_bank(PIECES[3])][:, 0:D], BR[:, 0, :],
                                  ALU.add).then_inc(sem["vb_ready"], 1)

            def scores(n, i):
                s4 = S[i % 2][:].rearrange("p (q k) -> p q k", k=P)
                dve.wait_ge(sem["s_mm"], 4 * n + i + 1)
                dve.tensor_reduce(MX[:, i, :], s4, AX_X, ALU.max).then_inc(sem["max_ready"], 1)
                dve.wait_ge(sem["max_ready"], 4 * n + i + 1)
                at_least(dve, sem["pt_mm"], 4 * (n - 1) + i + 1)
                dve.tensor_tensor(PB[:, i], s4, MX[:, i, :].unsqueeze(2).broadcast_to([P, 4, P]),
                                  ALU.subtract).then_inc(sem["sub_ready"], 1)

            def inter(n):
                dve.wait_ge(sem["i_mm"], n + 1)
                at_least(dve, sem["iexp_ready"], n)
                dve.tensor_tensor(SI[:], IB[:].rearrange("p (h c) -> p h c", c=NC),
                                  con["causal"][:, bass.ds(n, 1), :].broadcast_to([P, H, NC]),
                                  ALU.add).then_inc(sem["si_ready"], 1)
                dve.wait_ge(sem["si_ready"], n + 1)
                dve.tensor_reduce(IM[:], SI[:], AX_X, ALU.max).then_inc(sem["im_ready"], 1)

            def heads_of(bank):
                return bank[:, 0:H * (HD + 1)].rearrange("p (h d) -> p h d", d=HD + 1)

            def inter_heads(n):
                dve.wait_ge(sem["oi_mm"], n + 1)
                dve.reciprocal(IR[:].unsqueeze(2), heads_of(IB)[:, :, HD:HD + 1]).then_inc(sem["ir_ready"], 1)
                dve.wait_ge(sem["ir_ready"], n + 1)
                dve.tensor_tensor(O2[:], heads_of(IB)[:, :, 0:HD], IR[:].unsqueeze(2).broadcast_to([P, H, HD]),
                                  ALU.mult).then_inc(sem["o2_ready"], 1)

            def heads(n):
                oc = Chain(dve, sem["o_chain"], 2 * n)
                dve.wait_ge(sem["pv_mm"], 4 * (n + 1))
                oc.step(dve.reciprocal(RS[:].unsqueeze(2), heads_of(OB)[:, :, HD:HD + 1]))
                at_least(dve, sem["ot_mm"], n)
                oc.step(dve.tensor_tensor(O[:], heads_of(OB)[:, :, 0:HD], RS[:].unsqueeze(2).broadcast_to([P, H, HD]),
                                          ALU.mult))
                dve.tensor_tensor(O[:], O[:], O2[:], ALU.add).then_inc(sem["heads_ready"], 1)

            def heads_low(n):
                dve.wait_ge(sem["ot_hi"], n + 1)
                dve.tensor_tensor(OT[1][:].rearrange("p c t -> p (c t)"), TB[turn_bank(USE_HEADS)][:, 0:D],
                                  OT[0][:].rearrange("p c t -> p (c t)").bitcast(F32), ALU.subtract).then_inc(sem["ot_lo"], 1)

            def output(n, j, s, i):
                dve.wait_ge(sem["y_mm"], n + 1)
                if j == 0:
                    dve.wait_ge(sem["xb_ready"], 2 * i + s + 1)
                    at_least(dve, stored[s], 16 * i)
                dve.tensor_tensor(Y[s][:, j, :], TB[turn_bank(USE_OUT)][:, 0:D], XB[s][:, j, :],
                                  ALU.add).then_inc(sem["y_ready"], 1)

            def chunk(i, n, j, s, b, final, start):
                nxt = not (final and j == TPB - 1)

                def piece(k):
                    if final:
                        return
                    if j == 0 and k >= 2:
                        x_low(b + 1, k - 2)
                    if j == 1 and k == 2:
                        key_means(b + 1)
                    if j == 1 and k == 3:
                        value_means(b + 1)
                    if j == 2 and k >= 2:
                        values(b + 1, 1 - s, k - 2)

                if not start:
                    heads_low(n - 1)
                if j == 0 and not final:
                    statistics(i + s, b + 1, 1 - s)
                inter_heads(n)
                if nxt:
                    scores(n + 1, 0)
                    inter(n + 1)
                if j:
                    output(n - 1, j - 1, s, i)
                elif not start:
                    output(n - 1, TPB - 1, 1 - s, i)
                if j == 0 and not final:
                    norm(b + 1, 1 - s)
                if nxt:
                    scores(n + 1, 1)
                    scores(n + 1, 2)
                piece(2)
                heads(n)
                if nxt:
                    scores(n + 1, 3)
                piece(3)

            def body(i, last):
                for s in range(2):
                    b = 2 * i + s
                    for j in range(TPB):
                        chunk(i, b * TPB + j, j, s, b, last and s == 1, first(i) and s == 0 and j == 0)

            statistics(0, 0, 0)
            norm(0, 0)
            for c in range(DC):
                x_low(0, c)
            key_means(0)
            value_means(0)
            for v in range(2):
                values(0, 0, v)
            for i in range(4):
                scores(0, i)
            inter(0)
            loop_last(dve, half, body)
            heads_low(NC - 1)
            output(NC - 1, TPB - 1, 1, half - 1)

        @block.tensor
        def _(pe):
            pe.wait_ge(sem["w_lo"], 4)
            pending = [None] * 4

            def take(use, freed, value):
                bank = turn_bank(use)
                if pending[bank]:
                    at_least(pe, *pending[bank])
                pending[bank] = (sem[freed], value)
                return TB[bank]

            def x_turn(b, c):
                pe.wait_ge(nm.xn_ready, TPB * (b + 1))
                t_ = take(PIECES[2 + c], "x_lo", DC * b + c + 1)
                for t in range(TPB):
                    ins = pe.transpose(t_[:, t * P:(t + 1) * P], XN[:, t, c * P:(c + 1) * P], con["ident"])
                ins.then_inc(sem["xt_mm"], 1)

            def project(b, k, g):
                pe.wait_ge(sem["x_lo"], DC * (b + 1))
                t_ = take(PIECES[g], ("q_ready", "kf_ready")[k], DC * b + g + 1)
                for c in range(DC):
                    ins = split3(pe, t_[:], [W[h][:, k, c, g * P:(g + 1) * P] for h in range(2)],
                                 [XT[h][:, c, :] for h in range(2)], c == 0, c == DC - 1)
                ins.then_inc(sem[("q_mm", "k_mm")[k]], 1)

            def values(b, v):
                t_ = take(PIECES[2 + v], "v_ready", TPB * b + 2 * (v + 1))
                for t in range(2 * v, 2 * v + 2):
                    for c in range(DC):
                        ins = split3(pe, t_[:, (t % 2) * D:(t % 2 + 1) * D],
                                     [XT[h][:, c, t * P:(t + 1) * P] for h in range(2)],
                                     [W[h][:, 2, c, :] for h in range(2)], c == 0, c == DC - 1)
                ins.then_inc(sem["v_mm"], 1)

            def key_means(b):
                pe.wait_ge(sem["x_means"], DC * (b + 1))
                t_ = take(PIECES[2], "kt_ready", DC * (b + 1))
                for g in range(DC):
                    for c in range(DC):
                        ins = pe.matmul(t_[:, g * NC:(g + 1) * NC], WR[:, 1, c, g * P:(g + 1) * P], XA[:, c, 0, :],
                                        start=c == 0, stop=c == DC - 1)
                ins.then_inc(sem["km_mm"], 1)

            def value_means(b):
                t_ = take(PIECES[3], "vb_ready", b + 1)
                for c in range(DC):
                    ins = pe.matmul(t_[:, 0:D], XA[:, c].rearrange("p a j -> p (a j)"), WR[:, 2, c, :],
                                    start=c == 0, stop=c == DC - 1)
                ins.then_inc(sem["vm_mm"], 1)

            def scores(n, j, s, i):
                at_least(pe, sem["sub_ready"], 4 * n + i - 1)
                rows, strip = slice(j * P, (j + 1) * P), slice(32 * i, 32 * i + 32)
                for g in range(DC):
                    for k in range(2):
                        ins = pe.matmul(S[i % 2][:, (2 * g + k) * P:(2 * g + k + 1) * P], Q[s][strip, g, rows],
                                        KE[s][k][strip, g, rows], start=True, stop=True)
                ins.then_inc(sem["s_mm"], 1)

            def inter_scores(n, j, s):
                at_least(pe, sem["o2_ready"], n)
                for g in range(DC):
                    ins = pe.matmul(IB[:, g * D:(g + 1) * D], Q[s][:, g, j * P:(j + 1) * P],
                                    KM[s][:, g].rearrange("p h j -> p (h j)"), start=True, stop=True)
                ins.then_inc(sem["i_mm"], 1)

            def turn(n, i):
                pe.wait_ge(sem["exp_ready"], 4 * n + i + 1)
                t_ = take(USE_PROBS[i], "pt_ready", 4 * n + i + 1)
                for q in range(4):
                    ins = pe.transpose(t_[:, q * P:(q + 1) * P], PB[:, i, q, :], con["ident"])
                ins.then_inc(sem["pt_mm"], 1)

            def inter_turn(n):
                pe.wait_ge(sem["iexp_ready"], n + 1)
                t_ = take(USE_INTER, "at_ready", n + 1)
                for g in range(4):
                    ins = pe.transpose(t_[:, g * P:(g + 1) * P],
                                       AI[:, 4 * g:4 * g + 4, :].rearrange("p h j -> p (h j)"), con["ident"])
                ins.then_inc(sem["at_mm"], 1)

            def inter_products(n, s):
                pe.wait_ge(sem["at_ready"], n + 1)
                w = 4 * (HD + 1)
                for g in range(4):
                    ins = pe.matmul(IB[:, g * w:(g + 1) * w], AT[:, g * P:(g + 1) * P],
                                    VM[s][:, 4 * g:4 * g + 4, :].rearrange("p h d -> p (h d)"), start=True, stop=True)
                ins.then_inc(sem["oi_mm"], 1)

            def products(n, j, s, i):
                pe.wait_ge(sem["pt_ready"], 4 * n + i + 1)
                for q in range(4):
                    h = (q // 2) * GH + 2 * i + q % 2
                    ins = pe.matmul(OB[:, h * (HD + 1):(h + 1) * (HD + 1)], PT[i % 2][:, q * P:(q + 1) * P],
                                    V[s][:, j, h, :], start=True, stop=True)
                ins.then_inc(sem["pv_mm"], 1)

            def heads_turn(n):
                pe.wait_ge(sem["heads_ready"], n + 1)
                t_ = take(USE_HEADS, "ot_lo", n + 1)
                for c in range(DC):
                    ins = pe.transpose(t_[:, c * P:(c + 1) * P],
                                       O[:, c * GH:(c + 1) * GH, :].rearrange("p h d -> p (h d)"), con["ident"])
                ins.then_inc(sem["ot_mm"], 1)

            def output(n):
                pe.wait_ge(sem["ot_lo"], n + 1)
                t_ = take(USE_OUT, "y_ready", n + 1)
                for c in range(DC):
                    ins = split3(pe, t_[:, 0:D], [OT[h][:, c, :] for h in range(2)],
                                 [W[h][:, 3, c, :] for h in range(2)], c == 0, c == DC - 1)
                ins.then_inc(sem["y_mm"], 1)

            def chunk(n, j, s, b, final, start):
                nxt = not (final and j == TPB - 1)
                nj, ns = (j + 1) % TPB, (1 - s if j == TPB - 1 else s)

                def piece(k):
                    if final:
                        return
                    if j == 0 and k >= 2:
                        x_turn(b + 1, k - 2)
                    if j == 1:
                        if k < 2:
                            project(b + 1, 0, k)
                        else:
                            (key_means, value_means)[k - 2](b + 1)
                    if j == 2:
                        if k < 2:
                            project(b + 1, 1, k)
                        else:
                            values(b + 1, k - 2)

                turn(n, 0)
                inter_turn(n)
                if not start:
                    heads_turn(n - 1)
                piece(0)
                turn(n, 1)
                if j == 0:
                    pe.wait_ge(sem["vm_ready"], b + 1)
                    pe.wait_ge(sem["v_ready"], TPB * (b + 1))
                inter_products(n, s)
                at_least(pe, sem["heads_ready"], n)
                products(n, j, s, 0)
                if nxt:
                    if j == TPB - 1:
                        pe.wait_ge(sem["ke_ready"], 2 * DC * (b + 2))
                    scores(n + 1, nj, ns, 0)
                turn(n, 2)
                products(n, j, s, 1)
                if nxt:
                    if j == TPB - 1:
                        pe.wait_ge(sem["km_ready"], DC * (b + 2))
                    inter_scores(n + 1, nj, ns)
                piece(1)
                if not start:
                    output(n - 1)
                if nxt:
                    scores(n + 1, nj, ns, 1)
                turn(n, 3)
                products(n, j, s, 2)
                if nxt:
                    scores(n + 1, nj, ns, 2)
                piece(2)
                products(n, j, s, 3)
                if nxt:
                    scores(n + 1, nj, ns, 3)
                piece(3)

            def body(i, last):
                if not first(i):
                    n0 = 2 * i * TPB
                    pending[turn_bank(USE_PROBS[3])] = (sem["pt_ready"], 4 * n0)
                    pending[turn_bank(USE_PROBS[2])] = (sem["pt_ready"], 4 * n0 - 1)
                    pending[turn_bank(USE_HEADS)] = (sem["ot_lo"], n0 - 1)
                    pending[turn_bank(USE_OUT)] = (sem["y_ready"], n0 - 1)
                for s in range(2):
                    b = 2 * i + s
                    for j in range(TPB):
                        chunk(b * TPB + j, j, s, b, last and s == 1, first(i) and s == 0 and j == 0)

            for c in range(DC):
                x_turn(0, c)
            for g in range(DC):
                project(0, 0, g)
            pe.wait_ge(sem["clear"], 5)
            key_means(0)
            value_means(0)
            for g in range(DC):
                project(0, 1, g)
            for v in range(2):
                values(0, v)
            pe.wait_ge(sem["ke_ready"], 2 * DC)
            for i in range(4):
                scores(0, 0, 0, i)
            pe.wait_ge(sem["km_ready"], DC)
            inter_scores(0, 0, 0)
            loop_last(pe, half, body)
            heads_turn(NC - 1)
            output(NC - 1)


CONSTANTS = [("ident", (P, P), F32), ("ones", (P, P), BF16), ("before", (P, P), BF16), ("slots", (P, P), BF16),
             ("row", (P, 1), F32), ("tile", (P, E * NT), F32), ("restart", (P, E * NT), F32), ("top_bit", (P, 1), U32),
             ("parity", (P, 2), F32), ("own_head", (P, GH), F32), ("own_rows", (P, D), F32), ("causal", (P, NC, NC), F32)]


def program(nc, out, x, gate, shared_w, expert_w, attn_w, attn_bias_col, attn_bias_row, **constants):
    table = nc.dram_tensor("table", (TOK, ROW), F32, kind="Internal").ap()
    x1 = nc.dram_tensor("x_after_ffn", (TOK, D), F32, kind="Internal").ap()
    x2 = nc.dram_tensor("x_after_attention", (TOK, D), F32, kind="Internal").ap()
    with ExitStack() as ctx:
        m = Memory(nc, ctx, "")
        con, loaded = {}, m.sem("constants_loaded")
        tiles = [(n, m.sb("const_" + n, list(shape), dt)) for n, shape, dt in CONSTANTS]
        with m.run() as block:
            @block.sync
            def _(sp):
                for n, t in tiles:
                    con[n] = t[:]
                    sp.dma_start(t[:], constants[n]).then_inc(loaded, 16)
                sp.wait_ge(loaded, 16 * len(tiles))
        ffn(nc, "f1_", con, x, x1, gate, shared_w, expert_w, table)
        attention(nc, "at_", con, x1, x2, attn_w, attn_bias_col, attn_bias_row)
        ffn(nc, "f2_", con, x2, out, gate, shared_w, expert_w, table)


def kernel(**inputs):
    import ml_dtypes
    import numpy as np
    import concourse.bacc as bacc
    from concourse.bass_utils import run_bass_kernel_spmd

    a = {k.replace("L0_", ""): np.asarray(v) for k, v in inputs.items()}
    f, p = np.float32, np.arange(P)

    def units(gate, up, down):
        rows = [w.reshape(-1, P, DC, P).transpose(0, 3, 2, 1).reshape(-1, P, D) for w in (gate, up)]
        return np.ascontiguousarray(np.concatenate(rows + [np.swapaxes(down, -1, -2).reshape(-1, P, D)], -1))

    def columns(w):
        return np.ascontiguousarray(w.reshape(-1, DC, P).transpose(2, 1, 0))

    arrays = {
        "x": a["attn_hidden_states"].reshape(TOK, D),
        "gate": columns(a["ffn_gate_w"]),
        "shared_w": units(a["ffn_Sg"], a["ffn_Su"], a["ffn_Sd"]),
        "expert_w": units(a["ffn_Wg"], a["ffn_Wu"], a["ffn_Wd"]),
        "attn_w": np.ascontiguousarray(np.stack([columns(a["attn_w" + n]) for n in "qkvo"], 1)),
        "attn_bias_col": np.ascontiguousarray(np.stack([a["attn_b" + n].reshape(DC, P).T for n in "qk"], 1)),
        "attn_bias_row": np.ascontiguousarray(np.broadcast_to(np.stack([a["attn_b" + n] for n in "vo"]), (P, 2, D))),
        "ident": np.eye(P, dtype=f),
        "ones": np.ones((P, P), ml_dtypes.bfloat16),
        "before": np.triu(np.ones((P, P)), 1).astype(ml_dtypes.bfloat16),
        "slots": np.ascontiguousarray(np.broadcast_to(p, (P, P))).astype(ml_dtypes.bfloat16),
        "row": p.astype(f)[:, None],
        "tile": np.tile(np.arange(NT, dtype=f), (P, E)),
        "restart": np.tile((np.arange(NT) > 0).astype(f), (P, E)),
        "top_bit": np.full((P, 1), 1 << (BITS - 1), np.uint32),
        "parity": np.stack([p // HD % 2 == 0, p // HD % 2 == 1], 1).astype(f),
        "own_head": (p[:, None] // HD == np.arange(GH)).astype(f),
        "own_rows": (p[:, None] // NC == np.arange(D) // HD % 4).astype(f),
        "causal": np.tile(np.where(np.arange(NC)[:, None] >= np.arange(NC), 0, NEG).astype(f), (P, 1, 1)),
    }
    nc = bacc.Bacc("TRN2", target_bir_lowering=False, num_devices=1)
    handles = {n: nc.dram_tensor("in_" + n, v.shape, mybir.dt.from_np(v.dtype), kind="ExternalInput").ap()
               for n, v in arrays.items()}
    out = nc.dram_tensor("out", (TOK, D), F32, kind="ExternalOutput").ap()
    program(nc, out, **handles)
    r = run_bass_kernel_spmd(nc, [{"in_" + n: v for n, v in arrays.items()}], core_ids=[0])
    return r.results[0]["out"].reshape(1, TOK, D)
```

```python
from contextlib import ExitStack, contextmanager

import concourse.bass as bass
from concourse import mybir

F32 = mybir.dt.float32
F32R = mybir.dt.float32r
BF16 = mybir.dt.bfloat16
U32 = mybir.dt.uint32
ALU = mybir.AluOpType
ACT = mybir.ActivationFunctionType
AX_X = mybir.AxisListType.X

P = 128
TOK = 4096
D = 256
DC = D // P
NT = TOK // P
BLK = 512
TPB = BLK // P
NB = TOK // BLK
E = 16
CAP = TOK * 2 // E
IE = 1024
UE = IE // P
US = 512 // P
UW = 3 * D
ROW = D + E
EPS = 1e-5
BITS = 30
SEARCH = NB // 2
ROUNDS = 2 * (US * SEARCH - 1)
assert ROUNDS >= BITS
AHEAD = 6
RAW = 4

H = 16
HD = D // H
GH = P // HD
NC = NT
SCALE = 1.0 / HD ** 0.5
NEG = -1e30


class Constants(dict):

    def __init__(self, nc, ctx, sources):
        self.sources, self.tiles = sources, {}
        self.loaded = ctx.enter_context(nc.semaphore("constants_loaded"))
        self.ident_loaded = ctx.enter_context(nc.semaphore("ident_loaded"))
        for n, shape, dt in CONSTANTS:
            self.tiles[n] = ctx.enter_context(nc.sbuf_tensor("const_" + n, list(shape), dt))
            self[n] = self.tiles[n][:]
        self.asked = False

    def load_ident(self, sp):
        if not self.asked:
            sp.dma_start(self.tiles["ident"][:], self.sources["ident"]).then_inc(self.ident_loaded, 16)

    def load_rest(self, sp):
        if not self.asked:
            for n, tile in self.tiles.items():
                if n != "ident":
                    sp.dma_start(tile[:], self.sources[n]).then_inc(self.loaded, 16)
        self.asked = True

    def wait_rest(self, engine):
        engine.wait_ge(self.loaded, 16 * (len(self.tiles) - 1))


def at_least(engine, sem, value):
    if isinstance(value, int) and value <= 0:
        return
    engine.wait_ge(sem, value)


def first(i):
    return isinstance(i, int) and i == 0


def loop(engine, n, body):
    body(0)
    if n > 1:
        with engine.Fori(1, n) as i:
            body(i)


def loop_last(engine, n, body):
    body(0, False)
    with engine.Fori(1, n - 1) as i:
        body(i, False)
    body(n - 1, True)


class Chain:

    def __init__(self, engine, sem, base=0):
        self.engine, self.sem, self.base, self.n = engine, sem, base, 0

    def step(self, instruction):
        self.n += 1
        instruction.then_inc(self.sem, 1)
        self.engine.wait_ge(self.sem, self.base + self.n)


def split3(pe, out, lhs, rhs, first, last):
    pairs = [(0, 0), (0, 1), (1, 0)]
    for n, (a, b) in enumerate(pairs):
        ins = pe.matmul(out, lhs[a], rhs[b], start=first and n == 0, stop=last and n == 2,
                        skip_group_check=True)
    return ins


class Memory:

    def __init__(self, nc, ctx, prefix):
        self.nc, self.ctx, self.prefix, self.sems = nc, ctx, prefix, []

    def sb(self, name, shape, dt=F32):
        return self.ctx.enter_context(self.nc.sbuf_tensor(self.prefix + name, shape, dt))

    def ps(self, name, shape=(P, BLK), dt=F32):
        return self.ctx.enter_context(self.nc.psum_tensor(self.prefix + name, list(shape), dt))

    def sem(self, name):
        self.sems.append(self.ctx.enter_context(self.nc.semaphore(self.prefix + name)))
        return self.sems[-1]

    @contextmanager
    def run(self):
        with self.nc.Block() as block:
            yield block
        with self.nc.Block() as block:
            @block.sync
            def _(sp):
                for s in self.sems:
                    sp.sem_clear(s)


HALF = P // 2
COLS = CAP // HALF
AT_FIND = 9
AT_TURN = 12
AT_SPLIT = (2, 4, 6, 8)


class Norm:

    STEPS = 2
    SCALE_STEPS = 5

    def __init__(self, m):
        self.stats = [m.sb(f"stats{s}", [P, TPB, 6]) for s in range(2)]
        self.mv = [m.sb(f"meanvar{s}", [P, TPB, 2]) for s in range(2)]
        self.ve = [m.sb(f"vareps{s}", [P, TPB]) for s in range(2)]
        self.sd = [m.sb(f"std{s}", [P, TPB]) for s in range(2)]
        self.ri = [m.sb(f"rstd{s}", [P, 3, TPB]) for s in range(2)]
        self.chain, self.note = m.sem("norm_chain"), m.sem("norm_note")
        self.scale_chain = m.sem("norm_scale_chain")
        self.var_ready, self.std_ready, self.xn_ready = m.sem("var_ready"), m.sem("std_ready"), m.sem("xn_ready")

    def statistics(self, dve, b, s, tiles):
        for t in range(TPB):
            last = dve.bn_stats(self.stats[s][:, t, :], tiles(t))
        Chain(dve, self.chain, b * self.STEPS).step(last)
        dve.sem_inc(self.note, 1)
        for t in range(TPB):
            last = dve.bn_aggr(self.mv[s][:, t, :], self.stats[s][:, t, :])
        Chain(dve, self.chain, b * self.STEPS + 1).step(last)
        dve.tensor_scalar(self.ve[s][:], self.mv[s][:, :, 1], EPS, None, ALU.add).then_inc(self.var_ready, 1)

    def root(self, act, b, s):
        act.wait_ge(self.var_ready, b + 1)
        act.activation(self.sd[s][:], self.ve[s][:], ACT.Sqrt).then_inc(self.std_ready, 1)

    def scale(self, dve, b, s):
        dve.wait_ge(self.std_ready, b + 1)
        ch = Chain(dve, self.scale_chain, b * self.SCALE_STEPS)
        r0, r1, r2 = (self.ri[s][:, k, :] for k in range(3))
        ch.step(dve.reciprocal(r0, self.sd[s][:]))
        ch.step(dve.tensor_tensor(r1, r0, r0, ALU.mult))
        ch.step(dve.tensor_tensor(r2, r1, self.ve[s][:], ALU.mult))
        ch.step(dve.tensor_scalar(r1, r2, -0.5, 1.5, ALU.mult, ALU.add))
        ch.step(dve.tensor_tensor(r2, r0, r1, ALU.mult))

    def apply(self, dve, b, s, out, tiles, which=range(TPB)):
        for t in which:
            dve.tensor_scalar(out[:, t, :], tiles(t), self.mv[s][:, t, 0:1], self.ri[s][:, 2, t:t + 1],
                              ALU.subtract, ALU.mult).then_inc(self.xn_ready, 1)


class PrepareNorm:

    def __init__(self, m, X, XN):
        self.X, self.XN = X, XN
        self.stats = [m.sb(f"stats{s}", [P, TPB, 6]) for s in range(2)]
        self.mv = [m.sb(f"meanvar{s}", [P, TPB, 2]) for s in range(2)]
        self.ve = [m.sb(f"vareps{s}", [P, TPB]) for s in range(2)]
        self.sd = [m.sb(f"std{s}", [P, TPB]) for s in range(2)]
        self.ri = [m.sb(f"rstd{s}", [P, 3, TPB]) for s in range(2)]
        self.shift = [m.sb(f"shift{s}", [P, TPB]) for s in range(2)]
        self.stats_done, self.mv_done, self.var_ready, self.std_ready, self.steps, self.shift_ready, self.xn_ready = (
            m.sem(n) for n in ("stats_done", "mv_done", "var_ready", "std_ready", "scale_steps", "shift_ready",
                               "xn_ready"))

    def tile_statistics(self, dve, b, t):
        ins = dve.bn_stats(self.stats[b % 2][:, t, :], self.X[b % len(self.X)][:, t, :])
        if t == TPB - 1:
            ins.then_inc(self.stats_done, 1)

    def variance(self, dve, b):
        s = b % 2
        dve.wait_ge(self.stats_done, b + 1)
        at_least(dve, self.shift_ready, b - 1)
        for t in range(TPB):
            ins = dve.bn_aggr(self.mv[s][:, t, :], self.stats[s][:, t, :])
        ins.then_inc(self.mv_done, 1)
        dve.wait_ge(self.mv_done, b + 1)
        dve.tensor_scalar(self.ve[s][:], self.mv[s][:, :, 1], EPS, None, ALU.add).then_inc(self.var_ready, 1)

    def root(self, act, b):
        act.wait_ge(self.var_ready, b + 1)
        act.activation(self.sd[b % 2][:], self.ve[b % 2][:], ACT.Sqrt).then_inc(self.std_ready, 1)

    def scale(self, dve, b, between):
        s = b % 2
        dve.wait_ge(self.std_ready, b + 1)
        at_least(dve, self.xn_ready, TPB * (b - 1))
        r0, r1, r2 = (self.ri[s][:, k, :] for k in range(3))
        steps = [lambda: dve.reciprocal(r0, self.sd[s][:]),
                 lambda: dve.tensor_tensor(r1, r0, r0, ALU.mult),
                 lambda: dve.tensor_tensor(r2, r1, self.ve[s][:], ALU.mult),
                 lambda: dve.tensor_scalar(r1, r2, -0.5, 1.5, ALU.mult, ALU.add),
                 lambda: dve.tensor_tensor(r2, r0, r1, ALU.mult)]
        for k, step in enumerate(steps):
            step().then_inc(self.steps, 1)
            between(k)
            dve.wait_ge(self.steps, b * len(steps) + k + 1)
        dve.scalar_tensor_tensor(self.shift[s][:], self.mv[s][:, :, 0], -1.0, r2, ALU.mult,
                                 ALU.mult).then_inc(self.shift_ready, 1)

    def apply(self, act, b):
        s = b % 2
        act.wait_ge(self.shift_ready, b + 1)
        for t in range(TPB):
            act.activation(self.XN[s][:, t, :], self.X[b % len(self.X)][:, t, :], ACT.Identity,
                           bias=self.shift[s][:, t:t + 1],
                           scale=self.ri[s][:, 2, t:t + 1]).then_inc(self.xn_ready, 1)


class Finder:

    PIECE = 8
    PIECES = NT // PIECE

    def __init__(self, m, con, r):
        self.con, self.r = con, r
        self.made, self.hit, self.found, self.copied, self.placed, self.read, self.idx_ready = (
            m.sem(n) for n in ("onehot_made", "code_hit", "found", "found_copied", "placed", "placed_read", "idx_ready"))

    def code(self, dve, x, n):
        at_least(dve, self.found, n)
        wide = [P, NT, COLS]
        col = self.r.COL[:, bass.ds(x, 1), :].rearrange("p a t -> p (a t)").unsqueeze(2).broadcast_to(wide)
        dve.tensor_tensor(self.r.HIT[:], col, self.con["cols"].unsqueeze(1).broadcast_to(wide),
                          ALU.is_equal).then_inc(self.hit, 1)
        dve.wait_ge(self.hit, n + 1)
        dve.tensor_tensor(self.r.CODE[:, :, :, 0], self.r.HIT[:], self.con["row"].unsqueeze(2).broadcast_to(wide),
                          ALU.mult).then_inc(self.made, 1)
        dve.tensor_tensor(self.r.CODE[:, :, :, 1], self.r.HIT[:], self.con["tile"].unsqueeze(2).broadcast_to(wide),
                          ALU.mult).then_inc(self.made, 1)

    def onehot(self, dve, x, n, k):
        at_least(dve, self.found, n)
        sl = slice(k * self.PIECE, (k + 1) * self.PIECE)
        wide = [P, self.PIECE, HALF]
        dve.tensor_tensor(self.r.ONEHOT[:, sl, :], self.con["slots"].unsqueeze(1).broadcast_to(wide),
                          self.r.SLOT[:, bass.ds(x, 1), sl].rearrange("p a t -> p (a t)").unsqueeze(2)
                          .broadcast_to(wide), ALU.is_equal).then_inc(self.made, 1)

    def find(self, pe, n, bank):
        pe.wait_ge(self.made, (self.PIECES + 2) * (n + 1))
        for t in range(NT):
            ins = pe.matmul(bank[0:HALF, 0:2 * COLS], self.r.ONEHOT[:, t, :],
                            self.r.CODE[:, t, :, :].rearrange("p k v -> p (k v)"), start=t == 0, stop=t == NT - 1)
        ins.then_inc(self.found, 1)

    def copy(self, dve, n, bank):
        dve.wait_ge(self.found, n + 1)
        at_least(dve, self.placed, n)
        dve.tensor_copy(self.r.FOUND[:].rearrange("p h c v -> p c h v"),
                        bank[0:HALF, 0:2 * COLS].rearrange("p (c h v) -> p c h v", h=2, v=2)).then_inc(self.copied, 1)

    def place(self, pe, n, bank):
        pe.wait_ge(self.copied, n + 1)
        half = [self.r.FOUND[:, h].rearrange("p c v -> p (c v)") for h in range(2)]
        pe.matmul(bank[:, HALF:HALF + COLS], self.con["ident"][0:HALF, :], half[0], start=True, stop=False)
        pe.matmul(bank[:, HALF:HALF + COLS], self.con["upper"], half[1], start=False, stop=True).then_inc(self.placed, 1)

    def index(self, dve, n, bank, q):
        dve.wait_ge(self.placed, n + 1)
        dve.tensor_copy(self.r.PLACED[:].rearrange("p c v -> p (c v)"), bank[:, HALF:HALF + COLS]).then_inc(self.read, 1)
        dve.wait_ge(self.read, n + 1)
        dve.scalar_tensor_tensor(self.r.IDX[q][:], self.r.PLACED[:, :, 1], float(P), self.r.PLACED[:, :, 0], ALU.mult,
                                 ALU.add).then_inc(self.idx_ready, 1)


class Hidden:

    def __init__(self, nc, m):
        self.nc = nc
        self.GEL = [m.sb(f"gelu{s}", [P, BLK]) for s in range(2)]
        self.HF = [m.sb(f"h{s}", [P, BLK]) for s in range(2)]
        self.HP = [[m.sb(f"h_part{k}{s}", [P, BLK], F32R) for k in range(2)] for s in range(2)]
        self.GP = [m.ps(f"g{s}") for s in range(2)]
        self.UP = [m.ps(f"u{s}") for s in range(2)]
        self.OP = [m.ps(f"o{s}") for s in range(2)]
        self.g_ready, self.u_ready, self.gelu_done, self.hf_ready, self.hi_ready, self.ready, self.used = (
            m.sem(n) for n in ("g_ready", "u_ready", "gelu_done", "hf_ready", "hhi_ready", "h_ready", "h_used"))

    def up(self, pe, n, u, w, x, between=None):
        at_least(pe, self.gelu_done, n - 1)
        for g, bank, ready in ((0, self.GP, self.g_ready), (1, self.UP, self.u_ready)):
            if g:
                at_least(pe, self.hf_ready, n - 1)
            for c in range(DC):
                ins = split3(pe, bank[u % 2][:], [wk[:, g * D + c * P:g * D + (c + 1) * P] for wk in w],
                             [xk[:, c, :] for xk in x], c == 0, c == DC - 1)
                if g and c == 0 and between:
                    between()
            ins.then_inc(ready, 1)

    def gelu(self, act, n, u):
        act.wait_ge(self.g_ready, n + 1)
        at_least(act, self.hf_ready, n - 1)
        self.nc.scalar.activation(self.GEL[u % 2][:], self.GP[u % 2][:], ACT.Gelu).then_inc(self.gelu_done, 1)

    def product(self, dve, n, u):
        dve.wait_ge(self.gelu_done, n + 1)
        dve.wait_ge(self.u_ready, n + 1)
        at_least(dve, self.ready, n - 1)
        dve.tensor_tensor(self.HF[u % 2][:], self.GEL[u % 2][:], self.UP[u % 2][:], ALU.mult).then_inc(self.hf_ready, 1)

    def high(self, engine, n, u):
        engine.wait_ge(self.hf_ready, n + 1)
        at_least(engine, self.used, n - 1)
        if engine is self.nc.vector:
            ins = engine.tensor_copy(self.HP[u % 2][0][:], self.HF[u % 2][:])
        else:
            ins = self.nc.scalar.activation(self.HP[u % 2][0][:], self.HF[u % 2][:], ACT.Copy)
        ins.then_inc(self.hi_ready, 1)

    def low(self, engine, n, u):
        engine.wait_ge(self.hi_ready, n + 1)
        at_least(engine, self.used, n - 1)
        engine.tensor_tensor(self.HP[u % 2][1][:], self.HF[u % 2][:], self.HP[u % 2][0][:].bitcast(F32),
                             ALU.subtract).then_inc(self.ready, 1)

    def down(self, pe, n, u, units, w):
        pe.wait_ge(self.ready, n + 1)
        for t in range(TPB):
            ins = split3(pe, self.OP[t // 2][:, (t % 2) * D:(t % 2 + 1) * D],
                         [self.HP[u % 2][k][:, t * P:(t + 1) * P] for k in range(2)], w,
                         u == 0 and t % 2 == 0, u == units - 1 and t % 2 == 1)
        ins.then_inc(self.used, 1)


def ffn_prepare(nc, name, con, r, x_in, gate, shared_w, table):
    with ExitStack() as ctx:
        m = Memory(nc, ctx, name)
        X = [m.sb(f"x{s}", [P, TPB, D]) for s in range(4)]
        XN = [m.sb(f"xn{s}", [P, TPB, D]) for s in range(2)]
        nm = PrepareNorm(m, X, XN)
        GR = m.sb("gate_raw", [P, DC, E])
        G = [m.sb(f"gate_part{s}", [P, DC, P], F32R) for s in range(2)]
        LS = [m.sb(f"logits_t{s}", [P, BLK]) for s in range(2)]
        TP = [[m.ps(f"tp{s}{c}") for c in range(DC)] for s in range(2)]
        LP = [m.ps(f"lp{s}") for s in range(2)]
        TL = [m.ps(f"tl{s}") for s in range(2)]
        x_loaded = [m.sem(f"x_loaded{s}") for s in range(4)]
        gate_loaded, gate_split = m.sem("gate_loaded"), m.sem("gate_split")
        w_loaded, w_hi, w_lo = m.sem("w_loaded"), m.sem("w_hi"), m.sem("w_lo")
        xn_ready = nm.xn_ready
        xn_stored = [m.sem(f"xn_stored{s}") for s in range(2)]
        xt_ready, hi_ready, lo_ready = m.sem("xt_ready"), m.sem("hi_ready"), m.sem("lo_ready")
        lt_ready, ls_ready, tl_ready, lg_ready = (m.sem("lt_ready"), m.sem("ls_ready"),
                                                  m.sem("tl_ready"), m.sem("lg_ready"))
        block = ctx.enter_context(m.run())
        tab = table.rearrange("(t p) c -> p t c", p=P)
        x_v = x_in.rearrange("(t p) c -> p t c", p=P)

        def rows(b):
            return slice(b * TPB, (b + 1) * TPB)

        def block_of(x, c, b):
            return x[:, c, b * BLK:(b + 1) * BLK]

        @block.sync
        def _(sp):
            sp.dma_start(X[0][:], x_v[:, rows(0), :]).then_inc(x_loaded[0], 16)
            con.load_ident(sp)
            for b in range(1, 4):
                sp.dma_start(X[b][:], x_v[:, rows(b), :]).then_inc(x_loaded[b], 16)
            sp.dma_start(GR[:], gate).then_inc(gate_loaded, 16)
            con.load_rest(sp)
            sp.dma_start(r.WR[:], shared_w.rearrange("u p w -> p u w")).then_inc(w_loaded, 16)
            for b in range(NB):
                sp.wait_ge(xn_ready, TPB * (b + 1))
                if b + 4 < NB:
                    sp.dma_start(X[b % 4][:], x_v[:, rows(b + 4), :]).then_inc(x_loaded[b % 4], 16)
                sp.dma_start(tab[:, rows(b), 0:D], XN[b % 2][:]).then_inc(xn_stored[b % 2], 16)
            for s in range(2):
                sp.wait_ge(xn_stored[s], 16 * NB // 2)

        @block.gpsimd
        def _(pool):
            for u in range(US):
                pool.wait_ge(w_hi, u + 1)
                pool.tensor_tensor(r.W[1][:, u, :], r.WR[:, u, :], r.W[0][:, u, :].bitcast(F32),
                                   ALU.subtract).then_inc(w_lo, 1)
            pool.wait_ge(w_lo, US)

        @block.vector
        def _(dve):
            def statistics(b, t):
                if t == 0:
                    dve.wait_ge(x_loaded[b % 4], 16 * (b // 4 + 1))
                nm.tile_statistics(dve, b, t)

            def low(b):
                for c in range(DC):
                    dve.wait_ge(hi_ready, DC * b + c + 1)
                    dve.tensor_tensor(block_of(r.XTL, c, b), TP[b % 2][c][:], block_of(r.XTH, c, b).bitcast(F32),
                                      ALU.subtract).then_inc(lo_ready, 1)

            def logits(b):
                dve.wait_ge(tl_ready, b + 1)
                dve.tensor_copy(r.LG[:, rows(b), :],
                                TL[b % 2][:].rearrange("p (t e) -> p t e", e=P)[:, :, 0:E]).then_inc(lg_ready, 1)

            for t in range(TPB):
                statistics(0, t)
            nm.variance(dve, 0)
            gc = Chain(dve, gate_split)
            gc.step(dve.memset(G[0][:].bitcast(F32), 0.0))
            gc.step(dve.memset(G[1][:].bitcast(F32), 0.0))
            for b in range(-2, NB):
                if b + 2 < NB:
                    nm.scale(dve, b + 2, lambda k: statistics(b + 3, k) if b + 3 < NB and k < TPB else None)
                if b + 3 < NB:
                    nm.variance(dve, b + 3)
                if b == -1:
                    dve.wait_ge(gate_loaded, 16)
                    gc.step(dve.tensor_copy(G[0][:, :, 0:E], GR[:]))
                    gc.step(dve.tensor_tensor(G[1][:, :, 0:E], GR[:], G[0][:, :, 0:E].bitcast(F32), ALU.subtract))
                if b >= 0:
                    low(b)
                if b > 1:
                    logits(b - 2)
            logits(NB - 2)
            logits(NB - 1)

        @block.scalar
        def _(act):
            def high(b):
                act.wait_ge(xt_ready, b + 1)
                for c in range(DC):
                    nc.scalar.activation(block_of(r.XTH, c, b), TP[b % 2][c][:], ACT.Copy).then_inc(hi_ready, 1)

            def logits(b):
                act.wait_ge(lt_ready, b + 1)
                at_least(act, tl_ready, b - 1)
                nc.scalar.activation(LS[b % 2][:], LP[b % 2][:], ACT.Copy).then_inc(ls_ready, 1)

            nm.root(act, 0)
            for b in range(-2, NB):
                if b + 2 < NB:
                    at_least(act, xn_stored[b % 2], 16 * ((b + 2) // 2))
                    at_least(act, xt_ready, b + 1)
                    nm.apply(act, b + 2)
                if b + 3 < NB:
                    nm.root(act, b + 3)
                if 0 <= b + 1 < NB:
                    high(b + 1)
                if b > 0:
                    logits(b - 1)
                if 0 <= b < US:
                    act.wait_ge(w_loaded, 16)
                    nc.scalar.activation(r.W[0][:, b, :], r.WR[:, b, :], ACT.Copy).then_inc(w_hi, 1)
            logits(NB - 1)

        @block.tensor
        def _(pe):
            def turn(b):
                pe.wait_ge(xn_ready, TPB * (b + 1))
                at_least(pe, lo_ready, DC * (b - 1))
                for c in range(DC):
                    for t in range(TPB):
                        last = pe.transpose(TP[b % 2][c][:, t * P:(t + 1) * P], XN[b % 2][:, t, c * P:(c + 1) * P],
                                            con["ident"])
                last.then_inc(xt_ready, 1)

            def logits(b):
                pe.wait_ge(lo_ready, DC * (b + 1))
                at_least(pe, ls_ready, b - 1)
                for c in range(DC):
                    last = split3(pe, LP[b % 2][:], [G[k][:, c, :] for k in range(2)],
                                  [block_of(x, c, b) for x in (r.XTH, r.XTL)], c == 0, c == DC - 1)
                last.then_inc(lt_ready, 1)

            def logits_turn(b):
                pe.wait_ge(ls_ready, b + 1)
                at_least(pe, lg_ready, b - 1)
                for t in range(TPB):
                    last = pe.transpose(TL[b % 2][:, t * P:(t + 1) * P], LS[b % 2][:, t * P:(t + 1) * P],
                                        con["ident"])
                last.then_inc(tl_ready, 1)

            pe.wait_ge(con.ident_loaded, 16)
            turn(0)
            turn(1)
            pe.wait_ge(gate_split, 4)
            for b in range(NB):
                logits(b)
                if b + 2 < NB:
                    turn(b + 2)
                if b > 0:
                    logits_turn(b - 1)
            logits_turn(NB - 1)
            con.wait_rest(pe)


def ffn_shared_and_route(nc, name, con, r, x_in, acc, expert_w, table):
    with ExitStack() as ctx:
        m = Memory(nc, ctx, name)
        X, stored = r.X, r.stored
        Y = m.sb("y", [P, TPB * D])
        hid = Hidden(nc, m)
        PR, EX, SCT, ABOVE = (m.sb(n, [P, BLK])[:] for n in ("probs", "exp", "scores", "above"))
        MX = m.sb("max", [P, NT])
        EQ = m.sb("equal", [P, BLK])
        MARK = m.sb("mark", [P, BLK], BF16)
        THR, CAND, HIT, CNT = (m.sb(n, [P, 1]) for n in ("thr", "cand", "hit", "count"))
        MANY = m.sb("many", [P, 3])
        LIM, PRE = m.sb("limit", [P, 1]), m.sb("before", [P, 1])
        RP = [m.ps(f"route{k}") for k in range(2)]
        raw_loaded, w_hi, w_lo = m.sem("raw_loaded"), m.sem("w_hi"), m.sem("w_lo")
        x_loaded, y_ready, x_ready, last_ready = (m.sem(n) for n in ("x_loaded", "y_ready", "x_ready", "last_ready"))
        soft, ex_ready, sct_mm, mark_ready, count_ready = (
            m.sem(n) for n in ("soft", "ex_ready", "sct_mm", "mark_ready", "count_ready"))
        sc_stored, bis, pick, ranks, route = (m.sem(n) for n in ("sc_stored", "bis", "pick", "ranks", "route"))
        fd = Finder(m, con, r)
        xt_ready, xhi_ready = m.sem("xt_ready"), m.sem("xhi_ready")
        block = ctx.enter_context(m.run())
        acc_v = acc.rearrange("(t p) c -> p t c", p=P)
        x_v = x_in.rearrange("(t p) c -> p t c", p=P)
        x3 = X[:].rearrange("p (t c) -> p t c", c=D)

        @block.sync
        def _(sp):
            sp.dma_start(x3, x_v[:, 0:TPB, :]).then_inc(x_loaded, 16)
            sp.dma_start(r.WR[:], expert_w[0:RAW].rearrange("u p w -> p u w")).then_inc(raw_loaded, 16)
            sp.wait_ge(soft, 5)
            with nc.allow_non_contiguous_dma(reason="64 bytes of scores a row"):
                sp.dma_start(table.rearrange("(t p) c -> p t c", p=P)[:, :, D:ROW],
                             PR.rearrange("p (t e) -> p t e", e=E)).then_inc(sc_stored, 16)
            for b in range(NB):
                if b + 1 < NB:
                    sp.wait_ge(x_ready, b + 1)
                else:
                    sp.wait_ge(last_ready, 2)
                sp.dma_start(acc_v[:, b * TPB:(b + 1) * TPB, :], x3).then_inc(stored, 16)
                if b + 1 < NB:
                    sp.wait_ge(stored, 16 * (b + 1))
                    sp.dma_start(x3, x_v[:, (b + 1) * TPB:(b + 2) * TPB, :]).then_inc(x_loaded, 16)
            sp.wait_ge(sc_stored, 16)

        @block.gpsimd
        def _(pool):
            def residual(b):
                pool.wait_ge(x_loaded, 16 * (b + 1))
                pool.wait_ge(y_ready, 2 * (b + 1))
                pool.tensor_tensor(X[:], X[:], Y[:], ALU.add).then_inc(x_ready, 1)

            def body(b):
                for u in range(US):
                    hid.low(pool, b * US + u, u)
                    if u == 1 and not first(b):
                        residual(b - 1)

            loop(pool, SEARCH, body)
            for b in range(SEARCH, NB):
                for u in range(US):
                    k = (b - SEARCH) * US + u
                    hid.low(pool, b * US + u, u)
                    if u == 1:
                        residual(b - 1)
                    if k in AT_SPLIT:
                        w = AT_SPLIT.index(k)
                        pool.wait_ge(w_hi, w + 1)
                        pool.tensor_tensor(r.W[1][:, US + w, :], r.WR[:, w, :], r.W[0][:, US + w, :].bitcast(F32),
                                           ALU.subtract).then_inc(w_lo, 1)
                    if k == AT_FIND + 1:
                        pool.wait_ge(sc_stored, 16)
                        pool.wait_ge(fd.idx_ready, 1)
                        for t in range(TPB):
                            pool.indirect_dma_start(r.XG[0][:, t, :], None, table,
                                                    bass.IndirectOffsetOnAxis(r.IDX[0][:, t:t + 1], 0)
                                                    ).then_inc(r.gathered[0], 16)
            pool.wait_ge(w_lo, RAW)

        @block.scalar
        def _(act):
            act.wait_ge(soft, 2)
            nc.scalar.activation(EX, PR, ACT.Exp).then_inc(ex_ready, 1)

            def result(b):
                act.wait_ge(hid.used, US * (b + 1))
                at_least(act, x_ready, b)
                for k in range(2):
                    nc.scalar.activation(Y[:, k * BLK:(k + 1) * BLK], hid.OP[k][:], ACT.Copy, scale=0.5
                                         ).then_inc(y_ready, 1)

            def unit(b, u):
                n = b * US + u
                hid.gelu(act, n, u)
                if u == 1 and not first(b):
                    result(b - 1)
                hid.high(act, n, u)

            def body(b):
                for u in range(US):
                    unit(b, u)

            loop(act, SEARCH, body)
            for b in range(SEARCH, NB):
                for u in range(US):
                    k = (b - SEARCH) * US + u
                    unit(b, u)
                    if k in AT_SPLIT:
                        w = AT_SPLIT.index(k)
                        act.wait_ge(raw_loaded, 16)
                        nc.scalar.activation(r.W[0][:, US + w, :], r.WR[:, w, :], ACT.Copy).then_inc(w_hi, 1)
                    if k == AT_TURN:
                        act.wait_ge(xt_ready, 1)
                        for c in range(DC):
                            nc.scalar.activation(r.XT[0][0][:, c, :], RP[c][:], ACT.Copy).then_inc(xhi_ready, 1)

        @block.tensor
        def _(pe):
            down = lambda n, u: hid.down(pe, n, u, US, [r.W[k][:, u, 2 * D:UW] for k in range(2)])

            def up(b, u, n, between):
                hid.up(pe, n, u, [r.W[k][:, u, :] for k in range(2)],
                       [x[:, :, bass.ds(b * BLK, BLK)] for x in (r.XTH, r.XTL)], between)

            def count(r_):
                pe.wait_ge(mark_ready, r_ + 1)
                pe.matmul(RP[1][:, 0:1], con["same"], CNT[:], start=True, stop=True).then_inc(count_ready, 1)

            def unit(b, u, between):
                n = b * US + u
                up(b, u, n, between)
                if u == 1:
                    at_least(pe, y_ready, 2 * b)
                if u or not first(b):
                    down(n - 1, (u - 1) % US)
                return n

            def scores_turn():
                pe.wait_ge(soft, 6)
                for t in range(TPB):
                    ins = pe.transpose(RP[0][:, t * P:(t + 1) * P], EX[:, t * P:(t + 1) * P], con["ident"])
                ins.then_inc(sct_mm, 1)

            def body(b):
                for u in range(US):
                    n = b * US + u
                    if not first(b) or u > 1:
                        unit(b, u, lambda: count(2 * n - 3))
                    else:
                        unit(b, u, scores_turn if u == 1 else None)
                    if not first(b) or u:
                        count(2 * n - 2)

            def step(k):
                if k == 0:
                    count(ROUNDS - 1)
                if k == 1:
                    pe.wait_ge(ranks, 1)
                    pe.matmul(RP[1][:, 1:2], con["same"], MANY[:, 0:1], start=True, stop=False)
                    pe.matmul(RP[1][:, 1:2], con["prior"], MANY[:, 1:2], start=False, stop=True).then_inc(route, 1)
                if k == 2:
                    pe.wait_ge(ranks, 2)
                    pe.matmul(RP[1][:, 2:3], con["prior"], MANY[:, 2:3], start=True, stop=True).then_inc(route, 1)
                if k == 3:
                    pe.wait_ge(ranks, 3)
                    for t in range(TPB):
                        ins = pe.transpose(RP[0][:, t * P:(t + 1) * P], SCT[:, t * P:(t + 1) * P], con["ident"])
                    ins.then_inc(route, 1)

            loop(pe, SEARCH, body)
            for b in range(SEARCH, NB):
                for u in range(US):
                    k = (b - SEARCH) * US + u
                    unit(b, u, lambda: step(k))
                    if k == AT_FIND:
                        fd.find(pe, 0, RP[0])
                    if k == AT_FIND + 1:
                        fd.place(pe, 0, RP[0])
                    if k == AT_TURN:
                        r.wait_gathered(pe, 0, 1)
                        pe.wait_ge(fd.read, 1)
                        for c in range(DC):
                            for t in range(TPB):
                                ins = pe.transpose(RP[c][:, t * P:(t + 1) * P], r.XG[0][:, t, c * P:(c + 1) * P],
                                                   con["ident"])
                        ins.then_inc(xt_ready, 1)
            down(NB * US - 1, US - 1)

        @block.vector
        def _(dve):
            sc = Chain(dve, soft)
            wide = MX[:].unsqueeze(2).broadcast_to([P, NT, E])
            pr3, ex3 = (x.rearrange("p (t e) -> p t e", e=E) for x in (PR, EX))
            sc.step(dve.tensor_reduce(MX[:], r.LG[:], AX_X, ALU.max))
            sc.step(dve.tensor_tensor(pr3, r.LG[:], wide, ALU.subtract))
            dve.wait_ge(ex_ready, 1)
            sc.step(dve.tensor_reduce(MX[:], ex3, AX_X, ALU.add))
            sc.step(dve.reciprocal(MX[:], MX[:]))
            sc.step(dve.tensor_tensor(pr3, ex3, wide, ALU.mult))
            sc.step(dve.tensor_copy(EX.rearrange("p (t b e) -> p b t e", b=NB, t=TPB),
                                    PR.rearrange("p (b t e) -> p b t e", b=NB, t=TPB)))
            sc.step(dve.memset(THR[:], 0.0))
            sc.step(dve.tensor_copy(CAND[:].bitcast(U32), con["bits"][:, 0:1]))

            def compare():
                dve.tensor_scalar(MARK[:], SCT, CAND[:], None, ALU.is_ge, ALU.add, accum_out=CNT[:]).then_inc(mark_ready, 1)

            def update(n):
                ch = Chain(dve, bis, 3 * n)
                dve.wait_ge(count_ready, n + 1)
                ch.step(dve.scalar_tensor_tensor(HIT[:], RP[1][:, 0:1], CAP - 0.5, CAND[:], ALU.is_ge, ALU.mult))
                ch.step(dve.tensor_tensor(THR[:], THR[:], HIT[:], ALU.max))
                ch.step(dve.tensor_tensor(CAND[:].bitcast(U32), THR[:].bitcast(U32), con["bits"][:, bass.ds(n + 1, 1)],
                                          ALU.bitwise_or))

            def body(b):
                for u in range(US):
                    n = b * US + u
                    hid.product(dve, n, u)
                    if first(b) and u == 0:
                        dve.wait_ge(sct_mm, 1)
                        sc.step(dve.tensor_copy(SCT, RP[0][:]))
                        compare()
                    else:
                        update(2 * n - 2)
                        compare()
                        update(2 * n - 1)
                        compare()

            rc = Chain(dve, pick)
            RANK, COL = PR, EQ
            INC = EX
            unit_col = con["unit"].broadcast_to([P, BLK])

            def step(k):
                if k == 0:
                    dve.tensor_scalar(ABOVE, SCT, THR[:], None, ALU.is_gt, ALU.add, accum_out=MANY[:, 0:1]).then_inc(pick, 1)
                    rc.n += 1
                    rc.step(dve.tensor_scalar(EQ[:], SCT, THR[:], None, ALU.is_equal, ALU.add, accum_out=MANY[:, 1:2]))
                    dve.sem_inc(ranks, 1)
                if k == 1:
                    rc.step(dve.tensor_tensor_scan(INC, unit_col, EQ[:], 0.0, ALU.mult, ALU.add))
                    dve.wait_ge(route, 1)
                    rc.step(dve.tensor_scalar(LIM[:], RP[1][:, 1:2], -1.0, float(CAP), ALU.mult, ALU.add))
                    rc.step(dve.scalar_tensor_tensor(EQ[:], INC, LIM[:], EQ[:], ALU.is_le, ALU.mult))
                    rc.step(dve.scalar_tensor_tensor(ABOVE, EQ[:], 1.0, ABOVE, ALU.mult, ALU.add,
                                                     accum_out=MANY[:, 2:3]))
                    dve.sem_inc(ranks, 1)
                if k == 2:
                    rc.step(dve.tensor_tensor_scan(INC, unit_col, ABOVE, 0.0, ALU.mult, ALU.add))
                    dve.wait_ge(route, 2)
                    rc.step(dve.tensor_copy(PRE[:], RP[1][:, 2:3]))
                    rc.step(dve.scalar_tensor_tensor(SCT, INC, PRE[:], ABOVE, ALU.add, ALU.mult))
                    dve.sem_inc(ranks, 1)
                if k == 3:
                    dve.wait_ge(route, 3)
                    dve.wait_ge(sc_stored, 16)
                    rc.step(dve.tensor_copy(RANK.rearrange("p (e b t) -> p e b t", b=NB, t=TPB),
                                            RP[0][:].rearrange("p (t b e) -> p e b t", b=NB, e=E)))
                    rc.step(dve.tensor_scalar(COL[:], RANK, float(HALF + 1), None, ALU.is_ge))
                if k in (4, 5):
                    for c in range(2, 5) if k == 4 else range(5, COLS):
                        rc.step(dve.scalar_tensor_tensor(COL[:], RANK, float(c * HALF + 1), COL[:], ALU.is_ge, ALU.add))
                if k == 5:
                    rc.step(dve.tensor_copy(r.COL[:].rearrange("p e t -> p (e t)"), COL[:]))
                    rc.step(dve.scalar_tensor_tensor(RANK, COL[:], -float(HALF), RANK, ALU.mult, ALU.add))
                    rc.step(dve.tensor_scalar(r.SLOT[:].rearrange("p e t -> p (e t)"), RANK, 1.0, None, ALU.subtract))
                if k == 6:
                    fd.code(dve, 0, 0)
                if 6 <= k < 8:
                    for p_ in range(2):
                        fd.onehot(dve, 0, 0, 2 * (k - 6) + p_)
                if k == AT_FIND:
                    fd.copy(dve, 0, RP[0])
                if k == AT_FIND + 1:
                    fd.index(dve, 0, RP[0], 0)
                if k == AT_TURN:
                    r.wait_gathered(dve, 0, 1)
                    dve.tensor_scalar(r.WT[0][:], r.XG[0][:, :, D], 0.5, None, ALU.mult)
                    dve.wait_ge(xhi_ready, DC)
                    for c in range(DC):
                        dve.tensor_tensor(r.XT[0][1][:, c, :], RP[c][:], r.XT[0][0][:, c, :].bitcast(F32), ALU.subtract)

            loop(dve, SEARCH, body)
            for b in range(SEARCH, NB):
                for u in range(US):
                    hid.product(dve, b * US + u, u)
                    step((b - SEARCH) * US + u)
            dve.wait_ge(x_loaded, 16 * NB)
            dve.wait_ge(hid.used, US * NB)
            for k in range(2):
                xs = X[:, k * BLK:(k + 1) * BLK]
                dve.scalar_tensor_tensor(xs, hid.OP[k][:], 0.5, xs, ALU.mult, ALU.add).then_inc(last_ready, 1)


def ffn_experts(nc, name, con, r, acc, expert_w, table):
    with ExitStack() as ctx:
        m = Memory(nc, ctx, name)
        hid = Hidden(nc, m)
        EO = [m.sb(f"out{s}", [P, TPB, D]) for s in range(2)]
        TP = [m.ps(f"t{c}") for c in range(DC)]
        raw_loaded = [m.sem(f"raw_loaded{r}") for r in range(RAW)]
        w_hi, w_lo = m.sem("w_hi"), m.sem("w_lo")
        fd = Finder(m, con, r)
        gathered, scattered = r.gathered, r.scattered
        xt_ready, xhi_ready, xlo_ready, wt_ready = (
            m.sem(n) for n in ("xt_ready", "xhi_ready", "xlo_ready", "wt_ready"))
        eo_ready, note = m.sem("eo_ready"), m.sem("note")
        m.sems.append(r.stored)
        block = ctx.enter_context(m.run())
        half = E // 2
        WR, W, XG, XT, WT, IDX = r.WR, r.W, r.XG, r.XT, r.WT, r.IDX

        def place(u):
            return (u + US) % UE

        @block.sync
        def _(sp):
            def body(e):
                for u in range(UE):
                    n = e * UE + u
                    if first(e) and u < RAW:
                        continue
                    at_least(sp, w_lo, n - 2 * RAW + 1)
                    sp.dma_start(WR[:, u % RAW, :], expert_w[bass.ds(n, 1), :, :].rearrange("a p w -> p (a w)")
                                 ).then_inc(raw_loaded[u % RAW], 16)

            loop(sp, E, body)

        @block.gpsimd
        def _(pool):
            def low(n, u):
                pool.wait_ge(w_hi, n - RAW + 1)
                pool.tensor_tensor(W[1][:, place(u), :], WR[:, u % RAW, :], W[0][:, place(u), :].bitcast(F32),
                                   ALU.subtract).then_inc(w_lo, 1)

            def gather(x, q):
                pool.wait_ge(fd.idx_ready, x)
                at_least(pool, wt_ready, x - 2)
                at_least(pool, xt_ready, x - 2)
                pool.sem_inc(note, 1)
                for t in range(TPB):
                    pool.indirect_dma_start(XG[q][:, t, :], None, table,
                                            bass.IndirectOffsetOnAxis(IDX[q][:, t:t + 1], 0)
                                            ).then_inc(gathered[q], 16)

            def scatter(x, q):
                pool.wait_ge(eo_ready, TPB * (x + 1))
                r.wait_scattered(pool, x)
                pool.sem_inc(note, 1)
                for t in range(TPB):
                    pool.indirect_dma_start(acc, bass.IndirectOffsetOnAxis(IDX[q][:, t:t + 1], 0),
                                            EO[q][:, t, :], None, compute_op=ALU.add).then_inc(scattered, 16)

            def body(i, last):
                for q in range(2):
                    e = 2 * i + q
                    final = last and q == 1
                    for u in range(UE):
                        if not (final and u + AHEAD >= UE):
                            low(e * UE + u + AHEAD, (u + AHEAD) % UE)
                        if u == 1 and (q or not first(i)):
                            scatter(e - 1, 1 - q)
                        if u == 4 and not final:
                            gather(e + 1, 1 - q)

            for u in range(RAW, AHEAD):
                low(u, u)
            pool.wait_ge(r.stored, 16 * NB)
            loop_last(pool, half, body)
            r.wait_scattered(pool, E - 1)
            for t in range(TPB):
                pool.wait_ge(eo_ready, TPB * (E - 1) + t + 1)
                pool.indirect_dma_start(acc, bass.IndirectOffsetOnAxis(IDX[1][:, t:t + 1], 0), EO[1][:, t, :], None,
                                        compute_op=ALU.add).then_inc(r.scattered, 16)
            r.wait_scattered(pool, E)

        @block.scalar
        def _(act):
            def high(n, e, u):
                act.wait_ge(raw_loaded[u % RAW], 16 * (e * (UE // RAW) + u // RAW))
                at_least(act, hid.used, n - UE + 1)
                nc.scalar.activation(W[0][:, place(u), :], WR[:, u % RAW, :], ACT.Copy).then_inc(w_hi, 1)

            def x_high(x, q):
                act.wait_ge(xt_ready, x)
                for c in range(DC):
                    nc.scalar.activation(XT[q][0][:, c, :], TP[c][:], ACT.Copy).then_inc(xhi_ready, 1)

            def weigh(x, q):
                act.wait_ge(hid.used, UE * (x + 1))
                at_least(act, wt_ready, x)
                r.wait_scattered(act, x - 1)
                for t in range(TPB):
                    nc.scalar.activation(EO[q][:, t, :], hid.OP[t // 2][:, (t % 2) * D:(t % 2 + 1) * D], ACT.Copy,
                                         scale=WT[q][:, t:t + 1]).then_inc(eo_ready, 1)

            def body(i, last):
                for q in range(2):
                    e = 2 * i + q
                    final = last and q == 1
                    for u in range(UE):
                        n = e * UE + u
                        if u == UE - 1 and not final:
                            x_high(e + 1, 1 - q)
                        hid.gelu(act, n, u)
                        if u == 0 and (q or not first(i)):
                            weigh(e - 1, 1 - q)
                        if not (final and u + AHEAD >= UE):
                            a = u + AHEAD
                            high(n + AHEAD, e + a // UE, a % UE)

            for u in range(RAW, AHEAD):
                high(u, 0, u)
            loop_last(act, half, body)
            weigh(E - 1, 1)

        @block.vector
        def _(dve):
            def index(x, q):
                r.wait_scattered(dve, x - 1)
                fd.index(dve, x - 1, TP[0], q)

            def x_low(x, q, k):
                r.wait_gathered(dve, q, k)
                dve.tensor_scalar(WT[q][:], XG[q][:, :, bass.ds(x + D, 1)].rearrange("p t a -> p (t a)"), 0.5, None,
                                  ALU.mult).then_inc(wt_ready, 1)
                dve.wait_ge(xhi_ready, DC * x)
                for c in range(DC):
                    dve.tensor_tensor(XT[q][1][:, c, :], TP[c][:], XT[q][0][:, c, :].bitcast(F32),
                                      ALU.subtract).then_inc(xlo_ready, 1)

            def body(i, last):
                for q in range(2):
                    e = 2 * i + q
                    final = last and q == 1
                    for u in range(UE):
                        if u == UE - 1 and not final:
                            x_low(e + 1, 1 - q, i + 1 + q)
                        if u == 0 and not final:
                            fd.code(dve, e + 1, e)
                        if u < 2 and not final:
                            fd.onehot(dve, e + 1, e, 2 * u)
                            fd.onehot(dve, e + 1, e, 2 * u + 1)
                        if u == 3 and not final:
                            fd.copy(dve, e, TP[0])
                        if u == 4 and not final:
                            index(e + 1, 1 - q)
                        n = e * UE + u
                        hid.product(dve, n, u)
                        hid.high(dve, n, u)
                        hid.low(dve, n, u)

            loop_last(dve, half, body)

        @block.tensor
        def _(pe):
            def transposes(x, q, k):
                r.wait_gathered(pe, q, k)
                pe.wait_ge(fd.read, x)
                for c in range(DC):
                    for t in range(TPB):
                        ins = pe.transpose(TP[c][:, t * P:(t + 1) * P], XG[q][:, t, c * P:(c + 1) * P], con["ident"])
                ins.then_inc(xt_ready, 1)

            def up(n, u, q):
                at_least(pe, w_lo, n - RAW + 1)
                hid.up(pe, n, u, [W[k][:, place(u), :] for k in range(2)], XT[q])

            def down(n, u):
                hid.down(pe, n, u, UE, [W[k][:, place(u), 2 * D:UW] for k in range(2)])

            def body(i, last):
                for q in range(2):
                    e = 2 * i + q
                    final = last and q == 1
                    for u in range(UE):
                        n = e * UE + u
                        if u == 0:
                            at_least(pe, xlo_ready, DC * e)
                        up(n, u, q)
                        if u == 1:
                            at_least(pe, eo_ready, TPB * e)
                        if u or q or not first(i):
                            down(n - 1, (u - 1) % UE)
                        if u == 2 and not final:
                            at_least(pe, xlo_ready, DC * e)
                            fd.find(pe, e, TP[0])
                        if u == 3 and not final:
                            fd.place(pe, e, TP[0])
                        if u == 6 and not final:
                            transposes(e + 1, 1 - q, i + 1 + q)

            loop_last(pe, half, body)
            down(E * UE - 1, UE - 1)


class Resident:

    def __init__(self, m, dma_sems, layer):
        self.gathered, self.scattered, self.layer = dma_sems[0:2], dma_sems[2], layer
        self.SLOT = m.sb("slot", [P, E, NT], BF16)
        self.X, self.stored = m.sb("x", [P, TPB * D]), m.sem("stored")
        self.COL = m.sb("column", [P, E, NT], BF16)
        self.HIT = m.sb("code_hit", [P, NT, COLS], BF16)
        self.CODE = m.sb("code", [P, NT, COLS, 2], BF16)
        self.ONEHOT = m.sb("onehot", [P, NT, HALF], BF16)
        self.FOUND = m.sb("found", [HALF, 2, COLS // 2, 2])
        self.PLACED = m.sb("placed", [P, COLS // 2, 2])
        self.LG = m.sb("logits", [P, NT, E])
        self.WR = m.sb("w_raw", [P, RAW, UW])
        self.W = [m.sb(f"w_part{k}", [P, UE, UW], F32R) for k in range(2)]
        self.XTH = m.sb("xth", [P, DC, TOK], F32R)
        self.XTL = m.sb("xtl", [P, DC, TOK], F32R)
        self.XT = [[x[:, :, q * BLK:(q + 1) * BLK] for x in (self.XTH, self.XTL)] for q in range(2)]
        self.XG = [m.sb(f"gathered{s}", [P, TPB, ROW]) for s in range(2)]
        self.IDX = [m.sb(f"index{s}", [P, TPB], U32) for s in range(2)]
        self.WT = [m.sb(f"weight{s}", [P, TPB]) for s in range(2)]

    def wait_gathered(self, engine, q, count):
        engine.wait_ge(self.gathered[q], 16 * TPB * (count + self.layer * E // 2))

    def wait_scattered(self, engine, experts):
        if not (isinstance(experts, int) and experts <= 0):
            engine.wait_ge(self.scattered, 16 * TPB * (experts + self.layer * E))


def ffn(nc, name, con, dma_sems, layer, x_in, acc, gate, shared_w, expert_w, table):
    with ExitStack() as ctx:
        r = Resident(Memory(nc, ctx, name), dma_sems, layer)
        ffn_prepare(nc, name + "p_", con, r, x_in, gate, shared_w, table)
        ffn_shared_and_route(nc, name + "s_", con, r, x_in, acc, expert_w, table)
        ffn_experts(nc, name + "e_", con, r, acc, expert_w, table)


X_PIECES = (1, 2)
USE_PROBS, USE_INTER, USE_HEADS, USE_OUT, PIECES = (0, 4, 5, 8), 1, 2, 7, (3, 6, 11, 10)


def turn_bank(use):
    return use % 4


def attention(nc, name, con, x_in, out, w_in, bias_in, row_bias_in):
    with ExitStack() as ctx:
        m = Memory(nc, ctx, name)
        nm = Norm(m)
        WR = m.sb("w_raw", [P, 4, DC, D])
        W = [m.sb(f"w_part{k}", [P, 4, DC, D], F32R) for k in range(2)]
        BC = m.sb("bias_col", [P, 2, DC])
        KF = m.sb("k", [P, DC, BLK])
        BR = m.sb("bias_row", [P, 2, D])
        X = [m.sb(f"x{s}", [P, TPB, D]) for s in range(2)]
        XB = [m.sb(f"x_plus_bias{s}", [P, TPB, D]) for s in range(2)]
        XN = m.sb("xn", [P, TPB, D])
        XT = [m.sb(f"xt_part{k}", [P, DC, BLK], F32R) for k in range(2)]
        XM = m.sb("x_sum", [P, DC, TPB, P])
        XA = m.sb("x_means", [P, DC, 4, NC])
        KT = m.sb("k_means", [P, DC, NC])
        KM = [m.sb(f"k_means_by_head{s}", [P, DC, GH, NC]) for s in range(2)]
        VB = m.sb("v_means_all", [P, D])
        VM = [m.sb(f"v_means_by_head{s}", [P, H, HD + 1]) for s in range(2)]
        Q = [m.sb(f"q{s}", [P, DC, BLK]) for s in range(2)]
        KE = m.sb("k_by_head", [P, DC, TPB, GH, P])
        V = [m.sb(f"v{s}", [P, TPB, H, HD + 1]) for s in range(2)]
        MX = m.sb("max", [P, 4, 4])
        PB = m.sb("probs", [P, 4, 4, P])
        PT = [m.sb(f"probs_t{s}", [P, BLK]) for s in range(2)]
        SI = m.sb("inter", [P, H, NC])
        AI = m.sb("inter_probs", [P, H, NC])
        IM, IR, RS = (m.sb(n, [P, H]) for n in ("inter_max", "inter_recip", "recip"))
        AT = m.sb("inter_t", [P, BLK])
        O2 = m.sb("inter_heads", [P, H, HD])
        O = m.sb("heads", [P, H, HD])
        OT = [m.sb(f"heads_t{k}", [P, DC, P], F32R) for k in range(2)]
        Y = [m.sb(f"y{s}", [P, TPB, D]) for s in range(2)]
        S = [m.ps(f"scores{i}") for i in range(2)]
        TB = [m.ps(f"turn{i}") for i in range(4)]
        IB, OB = m.ps("inter_ps"), m.ps("heads_ps")
        names = ("w_loaded", "w_hi", "w_lo", "clear", "xt_mm", "x_hi", "x_lo", "x_part_sums", "x_sums", "x_means", "q_mm",
                 "k_mm", "v_mm", "km_mm", "vm_mm", "q_ready", "kf_ready", "ke_ready", "v_ready", "kt_ready", "km_ready",
                 "vb_ready", "vm_ready", "xb_ready", "s_mm", "max_ready", "sub_ready", "exp_ready", "pt_mm", "pt_ready",
                 "pv_mm", "i_mm", "si_ready", "im_ready", "isub_ready", "iexp_ready", "at_mm", "at_ready", "oi_mm",
                 "ir_ready", "o2_ready", "o_chain", "heads_ready", "ot_mm", "ot_hi", "ot_lo", "y_mm", "y_ready")
        sem = {n: m.sem(n) for n in names}
        x_loaded = [m.sem(f"x_loaded{s}") for s in range(2)]
        stored = [m.sem(f"stored{s}") for s in range(2)]
        block = ctx.enter_context(m.run())
        half = NB // 2
        x_v = x_in.rearrange("(t p) c -> p t c", p=P)
        out_v = out.rearrange("(t p) c -> p t c", p=P)

        @block.sync
        def _(sp):
            sp.dma_start(X[0][:], x_v[:, 0:TPB, :]).then_inc(x_loaded[0], 16)
            sp.dma_start(WR[:], w_in).then_inc(sem["w_loaded"], 16)
            sp.dma_start(BC[:], bias_in).then_inc(sem["w_loaded"], 16)
            sp.dma_start(BR[:], row_bias_in).then_inc(sem["w_loaded"], 16)
            for b in range(1, NB + 2):
                if b < NB:
                    at_least(sp, nm.xn_ready, TPB * (b - 1))
                    at_least(sp, sem["xb_ready"], b - 1)
                    sp.dma_start(X[b % 2][:], x_v[:, b * TPB:(b + 1) * TPB, :]).then_inc(x_loaded[b % 2], 16)
                if b > 1:
                    sp.wait_ge(sem["y_ready"], TPB * (b - 1))
                    sp.dma_start(out_v[:, (b - 2) * TPB:(b - 1) * TPB, :], Y[b % 2][:]).then_inc(stored[b % 2], 16)
            for s in range(2):
                sp.wait_ge(stored[s], 16 * half)

        @block.gpsimd
        def _(pool):
            pool.memset(XA[:], 0.0).then_inc(sem["clear"], 1)
            for s in range(2):
                pool.memset(V[s][:], 1.0).then_inc(sem["clear"], 1)
            pool.wait_ge(sem["w_hi"], 4)
            for k in range(4):
                pool.tensor_tensor(W[1][:, k], WR[:, k], W[0][:, k].bitcast(F32), ALU.subtract).then_inc(sem["w_lo"], 1)
            for s in range(2):
                pool.tensor_copy(VM[s][:, :, HD:HD + 1],
                                 con["own_rows"].rearrange("p (h d) -> p h d", d=HD)[:, :, 0:1]).then_inc(sem["clear"], 1)

            def residual(i, b, s):
                pool.wait_ge(x_loaded[s], 16 * (i + 1))
                at_least(pool, sem["y_ready"], TPB * (b - 1))
                pool.tensor_tensor(XB[s][:], X[s][:], BR[:, 1, :].unsqueeze(1).broadcast_to([P, TPB, D]),
                                   ALU.add).then_inc(sem["xb_ready"], 1)

            def keys(b, j):
                n = b * TPB + j
                at_least(pool, sem["s_mm"], 4 * (n - TPB + 1))
                for g in range(DC):
                    pool.wait_ge(sem["kf_ready"], DC * b + g + 1)
                    pool.tensor_tensor(KE[:, g, j], KF[:, g, j * P:(j + 1) * P].unsqueeze(1).broadcast_to([P, GH, P]),
                                       con["own_head"].unsqueeze(2).broadcast_to([P, GH, P]),
                                       ALU.mult).then_inc(sem["ke_ready"], 1)

            def means(b, s):
                pool.wait_ge(sem["kt_ready"], DC * (b + 1))
                at_least(pool, sem["i_mm"], TPB * (b - 1))
                for g in range(DC):
                    pool.tensor_tensor(KM[s][:, g], KT[:, g, :].unsqueeze(1).broadcast_to([P, GH, NC]),
                                       con["own_head"].unsqueeze(2).broadcast_to([P, GH, NC]),
                                       ALU.mult).then_inc(sem["km_ready"], 1)
                pool.wait_ge(sem["vb_ready"], b + 1)
                at_least(pool, sem["oi_mm"], TPB * (b - 1))
                pool.tensor_tensor(VM[s][:, :, 0:HD], VB[:].rearrange("p (h d) -> p h d", d=HD),
                                   con["own_rows"].rearrange("p (h d) -> p h d", d=HD), ALU.mult).then_inc(sem["vm_ready"], 1)

            def x_sums(b):
                pool.wait_ge(sem["x_lo"], DC * (b + 1))
                at_least(pool, sem["x_means"], DC * b)
                halvings = P.bit_length() - 1
                ch = Chain(pool, sem["x_part_sums"], b * halvings)
                hi, lo = (x[:].bitcast(F32).rearrange("p c (t k) -> p c t k", k=P) for x in XT)
                ch.step(pool.tensor_tensor(XM[:], hi, lo, ALU.add))
                for w in (P >> k for k in range(1, halvings)):
                    ch.step(pool.tensor_tensor(XM[:, :, :, 0:w], XM[:, :, :, 0:w], XM[:, :, :, w:2 * w], ALU.add))
                pool.tensor_tensor(XM[:, :, :, 0], XM[:, :, :, 0], XM[:, :, :, 1], ALU.add).then_inc(sem["x_sums"], 1)

            def inter(n):
                pool.wait_ge(sem["im_ready"], n + 1)
                pool.tensor_tensor(SI[:], SI[:], IM[:].unsqueeze(2).broadcast_to([P, H, NC]),
                                   ALU.subtract).then_inc(sem["isub_ready"], 1)

            def body(i, last):
                for s in range(2):
                    b = 2 * i + s
                    final = last and s == 1
                    for j in range(TPB):
                        if not (final and j == TPB - 1):
                            inter(b * TPB + j + 1)
                        if not final:
                            if j == 0:
                                residual(i + s, b + 1, 1 - s)
                                x_sums(b + 1)
                            if j == 1:
                                means(b + 1, 1 - s)
                            if j >= 2:
                                keys(b + 1, 2 * (j - 2))
                                keys(b + 1, 2 * (j - 2) + 1)

            pool.wait_ge(sem["w_loaded"], 48)
            x_sums(0)
            keys(0, 0)
            means(0, 0)
            inter(0)
            residual(0, 0, 0)
            for j in range(1, TPB):
                keys(0, j)
            loop_last(pool, half, body)

        @block.scalar
        def _(act):
            nm.root(act, 0, 0)
            act.wait_ge(sem["w_loaded"], 48)
            for k in range(4):
                nc.scalar.activation(W[0][:, k], WR[:, k], ACT.Copy).then_inc(sem["w_hi"], 1)

            def copy(out, in_, done):
                nc.scalar.activation(out, in_, ACT.Copy).then_inc(sem[done], 1)

            def x_high(b, c):
                act.wait_ge(sem["xt_mm"], DC * b + c + 1)
                at_least(act, sem["x_sums"], b)
                copy(XT[0][:, c, :], TB[turn_bank(PIECES[X_PIECES[c]])][:], "x_hi")

            def queries(b, s, g):
                act.wait_ge(sem["q_mm"], DC * b + g + 1)
                nc.scalar.activation(Q[s][:, g, :], TB[turn_bank(PIECES[g])][:], ACT.Identity,
                                     bias=BC[:, 0, g:g + 1]).then_inc(sem["q_ready"], 1)

            def keys(b, g):
                act.wait_ge(sem["k_mm"], DC * b + g + 1)
                at_least(act, sem["ke_ready"], DC * TPB * b)
                nc.scalar.activation(KF[:, g, :], TB[turn_bank(PIECES[g])][:], ACT.Identity,
                                     bias=BC[:, 1, g:g + 1]).then_inc(sem["kf_ready"], 1)

            def probs(n, i):
                act.wait_ge(sem["sub_ready"], 4 * n + i + 1)
                nc.scalar.activation(PB[:, i], PB[:, i], ACT.Exp, scale=SCALE).then_inc(sem["exp_ready"], 1)

            def inter(n):
                act.wait_ge(sem["isub_ready"], n + 1)
                at_least(act, sem["at_mm"], n)
                nc.scalar.activation(AI[:], SI[:], ACT.Exp, scale=SCALE).then_inc(sem["iexp_ready"], 1)

            def evacuate(n, i):
                act.wait_ge(sem["pt_mm"], 4 * n + i + 1)
                at_least(act, sem["pv_mm"], 4 * n + i - 1)
                copy(PT[i % 2][:], TB[turn_bank(USE_PROBS[i])][:], "pt_ready")

            def heads_high(n):
                act.wait_ge(sem["ot_mm"], n + 1)
                at_least(act, sem["y_mm"], n)
                copy(OT[0][:].rearrange("p c t -> p (c t)"), TB[turn_bank(USE_HEADS)][:, 0:D], "ot_hi")

            def chunk(n, j, s, b, final, start, last):
                nxt = not (final and j == TPB - 1)

                def piece(k):
                    if final:
                        return
                    if j == 0 and k in X_PIECES:
                        x_high(b + 1, X_PIECES.index(k))
                    if j == 1 and k < 2:
                        queries(b + 1, 1 - s, k)
                    if j == 2 and k < 2:
                        keys(b + 1, k)

                evacuate(n, 0)
                act.wait_ge(sem["at_mm"], n + 1)
                at_least(act, sem["oi_mm"], n)
                copy(AT[:], TB[turn_bank(USE_INTER)][:], "at_ready")
                if not start:
                    heads_high(n - 1)
                probs(n, 3)
                piece(0)
                evacuate(n, 1)
                if j == 3 and not last:
                    nm.root(act, b + 2, s)
                evacuate(n, 2)
                if nxt:
                    probs(n + 1, 0)
                piece(1)
                evacuate(n, 3)
                if nxt:
                    probs(n + 1, 1)
                    inter(n + 1)
                piece(2)
                if nxt:
                    probs(n + 1, 2)
                piece(3)

            def body(i, last):
                for s in range(2):
                    b = 2 * i + s
                    for j in range(TPB):
                        chunk(b * TPB + j, j, s, b, last and s == 1, first(i) and s == 0 and j == 0, last)

            for c in range(DC):
                x_high(0, c)
            nm.root(act, 1, 1)
            for g in range(DC):
                queries(0, 0, g)
            for g in range(DC):
                keys(0, g)
            for i in range(3):
                probs(0, i)
            inter(0)
            loop_last(act, half, body)
            heads_high(NC - 1)

        @block.vector
        def _(dve):
            def statistics(i, b, s):
                dve.wait_ge(x_loaded[s], 16 * (i + 1))
                nm.statistics(dve, b, s, lambda t: X[s][:, t, :])

            def norm(b, s, t):
                nm.apply(dve, b, s, XN, lambda t: X[s][:, t, :], [t])

            def x_low(b, c):
                t = TB[turn_bank(PIECES[X_PIECES[c]])]
                dve.wait_ge(sem["x_hi"], DC * b + c + 1)
                dve.tensor_tensor(XT[1][:, c, :], t[:], XT[0][:, c, :].bitcast(F32),
                                  ALU.subtract).then_inc(sem["x_lo"], 1)

            def x_means(b):
                dve.wait_ge(sem["x_sums"], b + 1)
                if first(b):
                    dve.wait_ge(sem["clear"], 1)
                for c in range(DC):
                    dve.tensor_scalar(XA[:, c, :, bass.ds(b * TPB, TPB)],
                                      XM[:, c, :, 0].unsqueeze(1).broadcast_to([P, 4, TPB]), 1.0 / P, None,
                                      ALU.mult).then_inc(sem["x_means"], 1)

            def values(b, s, v):
                if first(b):
                    dve.wait_ge(sem["clear"], 3)
                dve.wait_ge(sem["v_mm"], 2 * b + v + 1)
                for t in range(2):
                    dve.tensor_tensor(V[s][:, 2 * v + t, :, 0:HD],
                                      TB[turn_bank(PIECES[2 + v])][:, t * D:(t + 1) * D].rearrange("p (h d) -> p h d", d=HD),
                                      BR[:, 0, :].rearrange("p (h d) -> p h d", d=HD), ALU.add).then_inc(sem["v_ready"], 1)

            def key_means(b):
                dve.wait_ge(sem["km_mm"], b + 1)
                at_least(dve, sem["km_ready"], DC * b)
                for g in range(DC):
                    dve.tensor_scalar(KT[:, g, :], TB[turn_bank(PIECES[2])][:, g * NC:(g + 1) * NC],
                                      BC[:, 1, g:g + 1], None, ALU.add).then_inc(sem["kt_ready"], 1)

            def value_means(b):
                dve.wait_ge(sem["vm_mm"], b + 1)
                at_least(dve, sem["vm_ready"], b)
                dve.tensor_tensor(VB[:], TB[turn_bank(PIECES[3])][:, 0:D], BR[:, 0, :],
                                  ALU.add).then_inc(sem["vb_ready"], 1)

            def scores(n, i):
                s4 = S[i % 2][:].rearrange("p (q k) -> p q k", k=P)
                dve.wait_ge(sem["s_mm"], 4 * n + i + 1)
                dve.tensor_reduce(MX[:, i, :], s4, AX_X, ALU.max).then_inc(sem["max_ready"], 1)
                dve.wait_ge(sem["max_ready"], 4 * n + i + 1)
                at_least(dve, sem["pt_mm"], 4 * (n - 1) + i + 1)
                dve.tensor_tensor(PB[:, i], s4, MX[:, i, :].unsqueeze(2).broadcast_to([P, 4, P]),
                                  ALU.subtract).then_inc(sem["sub_ready"], 1)

            def inter(n):
                dve.wait_ge(sem["i_mm"], n + 1)
                at_least(dve, sem["iexp_ready"], n)
                dve.tensor_tensor(SI[:], IB[:].rearrange("p (h c) -> p h c", c=NC),
                                  con["causal"][:, bass.ds(n, 1), :].broadcast_to([P, H, NC]),
                                  ALU.add).then_inc(sem["si_ready"], 1)
                dve.wait_ge(sem["si_ready"], n + 1)
                dve.tensor_reduce(IM[:], SI[:], AX_X, ALU.max).then_inc(sem["im_ready"], 1)

            def heads_of(bank):
                return bank[:, 0:H * (HD + 1)].rearrange("p (h d) -> p h d", d=HD + 1)

            def inter_heads(n):
                dve.wait_ge(sem["oi_mm"], n + 1)
                dve.reciprocal(IR[:].unsqueeze(2), heads_of(IB)[:, :, HD:HD + 1]).then_inc(sem["ir_ready"], 1)
                dve.wait_ge(sem["ir_ready"], n + 1)
                dve.tensor_tensor(O2[:], heads_of(IB)[:, :, 0:HD], IR[:].unsqueeze(2).broadcast_to([P, H, HD]),
                                  ALU.mult).then_inc(sem["o2_ready"], 1)

            def heads(n):
                oc = Chain(dve, sem["o_chain"], 2 * n)
                dve.wait_ge(sem["pv_mm"], 4 * (n + 1))
                oc.step(dve.reciprocal(RS[:].unsqueeze(2), heads_of(OB)[:, :, HD:HD + 1]))
                at_least(dve, sem["ot_mm"], n)
                oc.step(dve.tensor_tensor(O[:], heads_of(OB)[:, :, 0:HD], RS[:].unsqueeze(2).broadcast_to([P, H, HD]),
                                          ALU.mult))
                dve.tensor_tensor(O[:], O[:], O2[:], ALU.add).then_inc(sem["heads_ready"], 1)

            def heads_low(n):
                dve.wait_ge(sem["ot_hi"], n + 1)
                dve.tensor_tensor(OT[1][:].rearrange("p c t -> p (c t)"), TB[turn_bank(USE_HEADS)][:, 0:D],
                                  OT[0][:].rearrange("p c t -> p (c t)").bitcast(F32), ALU.subtract).then_inc(sem["ot_lo"], 1)

            def output(n, j, s, i):
                dve.wait_ge(sem["y_mm"], n + 1)
                if j == 0:
                    dve.wait_ge(sem["xb_ready"], 2 * i + s + 1)
                    at_least(dve, stored[s], 16 * i)
                dve.tensor_tensor(Y[s][:, j, :], TB[turn_bank(USE_OUT)][:, 0:D], XB[s][:, j, :],
                                  ALU.add).then_inc(sem["y_ready"], 1)

            def chunk(i, n, j, s, b, final, start, last):
                nxt = not (final and j == TPB - 1)

                def piece(k):
                    if final:
                        return
                    if j == 0 and k in X_PIECES:
                        x_low(b + 1, X_PIECES.index(k))
                    if j == 1 and k == 1:
                        x_means(b + 1)
                    if j == 1 and k == 2:
                        key_means(b + 1)
                    if j == 1 and k == 3:
                        value_means(b + 1)
                    if j == 2 and k >= 2:
                        values(b + 1, 1 - s, k - 2)

                if not start:
                    heads_low(n - 1)
                inter_heads(n)
                if nxt:
                    scores(n + 1, 0)
                    inter(n + 1)
                if j:
                    output(n - 1, j - 1, s, i)
                elif not start:
                    output(n - 1, TPB - 1, 1 - s, i)
                if nxt:
                    scores(n + 1, 1)
                piece(1)
                if nxt:
                    scores(n + 1, 2)
                heads(n)
                piece(2)
                piece(3)
                if nxt:
                    scores(n + 1, 3)
                if j == 2 and not last:
                    statistics(i + 1, b + 2, s)
                if j == 3 and not last:
                    nm.scale(dve, b + 2, s)
                if j == 3 and not last:
                    for t in range(TPB):
                        norm(b + 2, s, t)

            def body(i, last):
                for s in range(2):
                    b = 2 * i + s
                    for j in range(TPB):
                        chunk(i, b * TPB + j, j, s, b, last and s == 1, first(i) and s == 0 and j == 0, last)

            statistics(0, 0, 0)
            nm.scale(dve, 0, 0)
            for t in range(TPB):
                norm(0, 0, t)
            for c in range(DC):
                x_low(0, c)
            statistics(0, 1, 1)
            nm.scale(dve, 1, 1)
            for t in range(TPB):
                norm(1, 1, t)
            dve.wait_ge(sem["w_loaded"], 48)
            for v in range(2):
                values(0, 0, v)
            x_means(0)
            key_means(0)
            value_means(0)
            for i in range(4):
                scores(0, i)
            inter(0)
            loop_last(dve, half, body)
            heads_low(NC - 1)
            output(NC - 1, TPB - 1, 1, half - 1)

        @block.tensor
        def _(pe):
            pending = [None] * 4

            def take(use, freed, value):
                bank = turn_bank(use)
                if pending[bank]:
                    at_least(pe, *pending[bank])
                pending[bank] = (sem[freed], value)
                return TB[bank]

            def x_turn(b, c):
                pe.wait_ge(nm.xn_ready, TPB * (b + 1))
                t_ = take(PIECES[X_PIECES[c]], "x_lo", DC * b + c + 1)
                for t in range(TPB):
                    ins = pe.transpose(t_[:, t * P:(t + 1) * P], XN[:, t, c * P:(c + 1) * P], con["ident"])
                ins.then_inc(sem["xt_mm"], 1)

            def project(b, k, g):
                pe.wait_ge(sem["x_lo"], DC * (b + 1))
                t_ = take(PIECES[g], ("q_ready", "kf_ready")[k], DC * b + g + 1)
                for c in range(DC):
                    ins = split3(pe, t_[:], [W[h][:, k, c, g * P:(g + 1) * P] for h in range(2)],
                                 [XT[h][:, c, :] for h in range(2)], c == 0, c == DC - 1)
                ins.then_inc(sem[("q_mm", "k_mm")[k]], 1)

            def values(b, v):
                t_ = take(PIECES[2 + v], "v_ready", TPB * b + 2 * (v + 1))
                for t in range(2 * v, 2 * v + 2):
                    for c in range(DC):
                        ins = split3(pe, t_[:, (t % 2) * D:(t % 2 + 1) * D],
                                     [XT[h][:, c, t * P:(t + 1) * P] for h in range(2)],
                                     [W[h][:, 2, c, :] for h in range(2)], c == 0, c == DC - 1)
                ins.then_inc(sem["v_mm"], 1)

            def key_means(b):
                pe.wait_ge(sem["x_means"], DC * (b + 1))
                t_ = take(PIECES[2], "kt_ready", DC * (b + 1))
                for g in range(DC):
                    for c in range(DC):
                        ins = pe.matmul(t_[:, g * NC:(g + 1) * NC], WR[:, 1, c, g * P:(g + 1) * P], XA[:, c, 0, :],
                                        start=c == 0, stop=c == DC - 1)
                ins.then_inc(sem["km_mm"], 1)

            def value_means(b):
                t_ = take(PIECES[3], "vb_ready", b + 1)
                for c in range(DC):
                    ins = pe.matmul(t_[:, 0:D], XA[:, c].rearrange("p a j -> p (a j)"), WR[:, 2, c, :],
                                    start=c == 0, stop=c == DC - 1)
                ins.then_inc(sem["vm_mm"], 1)

            def scores(n, j, s, i):
                at_least(pe, sem["sub_ready"], 4 * n + i - 1)
                g, h = i // 2, 4 * (i % 2)
                pe.wait_ge(sem["ke_ready"], DC * n + g + 1)
                pe.matmul(S[i % 2][:], Q[s][:, g, j * P:(j + 1) * P],
                          KE[:, g, j, h:h + 4, :].rearrange("p h k -> p (h k)"), start=True, stop=True
                          ).then_inc(sem["s_mm"], 1)

            def inter_scores(n, j, s):
                at_least(pe, sem["o2_ready"], n)
                for g in range(DC):
                    ins = pe.matmul(IB[:, g * D:(g + 1) * D], Q[s][:, g, j * P:(j + 1) * P],
                                    KM[s][:, g].rearrange("p h j -> p (h j)"), start=True, stop=True)
                ins.then_inc(sem["i_mm"], 1)

            def turn(n, i):
                pe.wait_ge(sem["exp_ready"], 4 * n + i + 1)
                t_ = take(USE_PROBS[i], "pt_ready", 4 * n + i + 1)
                for q in range(4):
                    ins = pe.transpose(t_[:, q * P:(q + 1) * P], PB[:, i, q, :], con["ident"])
                ins.then_inc(sem["pt_mm"], 1)

            def inter_turn(n):
                pe.wait_ge(sem["iexp_ready"], n + 1)
                t_ = take(USE_INTER, "at_ready", n + 1)
                for g in range(4):
                    ins = pe.transpose(t_[:, g * P:(g + 1) * P],
                                       AI[:, 4 * g:4 * g + 4, :].rearrange("p h j -> p (h j)"), con["ident"])
                ins.then_inc(sem["at_mm"], 1)

            def inter_products(n, s):
                pe.wait_ge(sem["at_ready"], n + 1)
                w = 4 * (HD + 1)
                for g in range(4):
                    ins = pe.matmul(IB[:, g * w:(g + 1) * w], AT[:, g * P:(g + 1) * P],
                                    VM[s][:, 4 * g:4 * g + 4, :].rearrange("p h d -> p (h d)"), start=True, stop=True)
                ins.then_inc(sem["oi_mm"], 1)

            def products(n, j, s, i):
                pe.wait_ge(sem["pt_ready"], 4 * n + i + 1)
                for q in range(4):
                    h = 4 * i + q
                    ins = pe.matmul(OB[:, h * (HD + 1):(h + 1) * (HD + 1)], PT[i % 2][:, q * P:(q + 1) * P],
                                    V[s][:, j, h, :], start=True, stop=True)
                ins.then_inc(sem["pv_mm"], 1)

            def heads_turn(n):
                pe.wait_ge(sem["heads_ready"], n + 1)
                t_ = take(USE_HEADS, "ot_lo", n + 1)
                for c in range(DC):
                    ins = pe.transpose(t_[:, c * P:(c + 1) * P],
                                       O[:, c * GH:(c + 1) * GH, :].rearrange("p h d -> p (h d)"), con["ident"])
                ins.then_inc(sem["ot_mm"], 1)

            def output(n):
                pe.wait_ge(sem["ot_lo"], n + 1)
                t_ = take(USE_OUT, "y_ready", n + 1)
                for c in range(DC):
                    ins = split3(pe, t_[:, 0:D], [OT[h][:, c, :] for h in range(2)],
                                 [W[h][:, 3, c, :] for h in range(2)], c == 0, c == DC - 1)
                ins.then_inc(sem["y_mm"], 1)

            def chunk(n, j, s, b, final, start):
                nxt = not (final and j == TPB - 1)
                nj, ns = (j + 1) % TPB, (1 - s if j == TPB - 1 else s)

                def piece(k):
                    if final:
                        return
                    if j == 0 and k in X_PIECES:
                        x_turn(b + 1, X_PIECES.index(k))
                    if j == 1:
                        if k < 2:
                            project(b + 1, 0, k)
                        else:
                            (key_means, value_means)[k - 2](b + 1)
                    if j == 2:
                        if k < 2:
                            project(b + 1, 1, k)
                        else:
                            values(b + 1, k - 2)

                turn(n, 0)
                inter_turn(n)
                if not start:
                    heads_turn(n - 1)
                piece(0)
                turn(n, 1)
                if j == 0:
                    pe.wait_ge(sem["vm_ready"], b + 1)
                    pe.wait_ge(sem["v_ready"], TPB * (b + 1))
                inter_products(n, s)
                at_least(pe, sem["heads_ready"], n)
                products(n, j, s, 0)
                if nxt:
                    scores(n + 1, nj, ns, 0)
                turn(n, 2)
                products(n, j, s, 1)
                if nxt:
                    if j == TPB - 1:
                        pe.wait_ge(sem["km_ready"], DC * (b + 2))
                    inter_scores(n + 1, nj, ns)
                piece(1)
                if not start:
                    output(n - 1)
                if nxt:
                    scores(n + 1, nj, ns, 1)
                turn(n, 3)
                products(n, j, s, 2)
                if nxt:
                    scores(n + 1, nj, ns, 2)
                piece(2)
                products(n, j, s, 3)
                piece(3)
                if nxt:
                    scores(n + 1, nj, ns, 3)

            def body(i, last):
                if not first(i):
                    n0 = 2 * i * TPB
                    pending[turn_bank(USE_PROBS[3])] = (sem["pt_ready"], 4 * n0)
                    pending[turn_bank(USE_PROBS[2])] = (sem["pt_ready"], 4 * n0 - 1)
                    pending[turn_bank(USE_HEADS)] = (sem["ot_lo"], n0 - 1)
                    pending[turn_bank(USE_OUT)] = (sem["y_ready"], n0 - 1)
                for s in range(2):
                    b = 2 * i + s
                    for j in range(TPB):
                        chunk(b * TPB + j, j, s, b, last and s == 1, first(i) and s == 0 and j == 0)

            for c in range(DC):
                x_turn(0, c)
            pe.wait_ge(sem["w_lo"], 4)
            for k in range(2):
                for g in range(DC):
                    project(0, k, g)
            for v in range(2):
                values(0, v)
            pe.wait_ge(sem["clear"], 5)
            key_means(0)
            value_means(0)
            for i in range(4):
                scores(0, 0, 0, i)
            pe.wait_ge(sem["km_ready"], DC)
            inter_scores(0, 0, 0)
            loop_last(pe, half, body)
            heads_turn(NC - 1)
            output(NC - 1)


CONSTANTS = [("ident", (P, P), F32), ("same", (P, P), F32), ("prior", (P, P), F32), ("slots", (P, HALF), BF16),
             ("cols", (P, COLS), BF16), ("upper", (HALF, P), F32), ("row", (P, 1), F32), ("tile", (P, NT), F32),
             ("unit", (P, 1), F32), ("bits", (P, ROUNDS + 1), U32),
             ("own_head", (P, GH), F32), ("own_rows", (P, D), F32), ("causal", (P, NC, NC), F32)]


def program(nc, out, x, gate, shared_w, expert_w, attn_w, attn_bias_col, attn_bias_row, **constants):
    table = nc.dram_tensor("table", (TOK, ROW), F32, kind="Internal").ap()
    x1 = nc.dram_tensor("x_after_ffn", (TOK, D), F32, kind="Internal").ap()
    x2 = nc.dram_tensor("x_after_attention", (TOK, D), F32, kind="Internal").ap()
    with ExitStack() as ctx:
        con = Constants(nc, ctx, constants)
        dma_sems = [ctx.enter_context(nc.semaphore(n)) for n in ("gathered0", "gathered1", "scattered")]
        ffn(nc, "f1_", con, dma_sems, 0, x, x1, gate, shared_w, expert_w, table)
        attention(nc, "at_", con, x1, x2, attn_w, attn_bias_col, attn_bias_row)
        ffn(nc, "f2_", con, dma_sems, 1, x2, out, gate, shared_w, expert_w, table)


def kernel(**inputs):
    import ml_dtypes
    import numpy as np
    import concourse.bacc as bacc
    from concourse.bass_utils import run_bass_kernel_spmd

    a = {k.replace("L0_", ""): np.asarray(v) for k, v in inputs.items()}
    f, p = np.float32, np.arange(P)

    def units(gate, up, down):
        rows = [w.reshape(-1, P, DC, P).transpose(0, 3, 2, 1).reshape(-1, P, D) for w in (gate, up)]
        return np.ascontiguousarray(np.concatenate(rows + [np.swapaxes(down, -1, -2).reshape(-1, P, D)], -1))

    def columns(w):
        return np.ascontiguousarray(w.reshape(-1, DC, P).transpose(2, 1, 0))

    arrays = {
        "x": a["attn_hidden_states"].reshape(TOK, D),
        "gate": columns(a["ffn_gate_w"]),
        "shared_w": units(a["ffn_Sg"], a["ffn_Su"], a["ffn_Sd"]),
        "expert_w": units(a["ffn_Wg"], a["ffn_Wu"], a["ffn_Wd"]),
        "attn_w": np.ascontiguousarray(np.stack([columns(a["attn_w" + n]) for n in "qkvo"], 1)),
        "attn_bias_col": np.ascontiguousarray(np.stack([a["attn_b" + n].reshape(DC, P).T for n in "qk"], 1)),
        "attn_bias_row": np.ascontiguousarray(np.broadcast_to(np.stack([a["attn_b" + n] for n in "vo"]), (P, 2, D))),
        "ident": np.eye(P, dtype=f),
        "same": (p[:, None] % E == p % E).astype(f),
        "prior": ((p[:, None] % E == p % E) & (p[:, None] < p)).astype(f),
        "slots": np.tile(np.arange(HALF), (P, 1)).astype(ml_dtypes.bfloat16),
        "cols": np.tile(np.arange(COLS), (P, 1)).astype(ml_dtypes.bfloat16),
        "upper": np.eye(HALF, P, HALF, dtype=f),
        "row": p.astype(f)[:, None],
        "tile": np.tile(np.arange(NT, dtype=f), (P, 1)),
        "unit": np.ones((P, 1), f),
        "bits": np.tile(np.array([1 << (BITS - 1 - n) if n < BITS else 0 for n in range(ROUNDS + 1)], np.uint32), (P, 1)),
        "own_head": (p[:, None] // HD == np.arange(GH)).astype(f),
        "own_rows": (p[:, None] // NC == np.arange(D) // HD % 4).astype(f),
        "causal": np.tile(np.where(np.arange(NC)[:, None] >= np.arange(NC), 0, NEG).astype(f), (P, 1, 1)),
    }
    nc = bacc.Bacc("TRN2", target_bir_lowering=False, num_devices=1)
    handles = {n: nc.dram_tensor("in_" + n, v.shape, mybir.dt.from_np(v.dtype), kind="ExternalInput").ap()
               for n, v in arrays.items()}
    out = nc.dram_tensor("out", (TOK, D), F32, kind="ExternalOutput").ap()
    program(nc, out, **handles)
    r = run_bass_kernel_spmd(nc, [{"in_" + n: v for n, v in arrays.items()}], core_ids=[0])
    return r.results[0]["out"].reshape(1, TOK, D)
```
